# Optimizing a Trainium2 kernel written in Bass

```python
import numpy as np
import jax
import jax.numpy as jnp

def _softmax(x, axis=-1):
    return jax.nn.softmax(x, axis=axis)

def _gelu(x):
    return jax.nn.gelu(x, approximate=True)

def _silu(x):
    return jax.nn.silu(x)

def _sigmoid(x):
    return jax.nn.sigmoid(x)

def _layernorm(x, axis=-1, eps=1e-05):
    m = jnp.mean(x, axis=axis, keepdims=True)
    v = jnp.var(x, axis=axis, keepdims=True)
    return (x - m) / jnp.sqrt(v + eps)

def _scatter_add(tgt, idx, src, axis=0):
    return tgt.at[idx].add(src)

def _segment_sum(src, seg, n):
    return jax.ops.segment_sum(src, seg, n)
kernel_name = 'mk_audio_tower_d2_tok_aud1d256_r4_6436a9'

def setup_inputs(seed: int=0):
    np.random.seed(seed)
    _w = jnp.asarray

    def _rec_inputs():
        import jax
        import jax.numpy as jnp
        _rk = jax.random.key(seed)
        x = -0.000292821 + 1.00034 * jax.random.normal(jax.random.fold_in(_rk, 1), (128, 8192), jnp.float32)
        return x
    x = _rec_inputs()

    def _L0_tok_setup():
        import jax, jax.numpy as jnp
        import numpy as np
        EPS = 1e-05

        def _conv1d(x, W, b, stride, pad):
            y = jax.lax.conv_general_dilated(x, W, (stride,), [(pad, pad)], dimension_numbers=('NCH', 'OIH', 'NCH'))
            return y + b[None, :, None]

        def _bn(x, g, b, m, v):
            return (x - m[None, :, None]) * (g * jax.lax.rsqrt(v + EPS))[None, :, None] + b[None, :, None]

        def _maxpool(x, k):
            B, C, L = x.shape
            return x.reshape(B, C, L // k, k).max(axis=-1)

        def _self_attn(x, Wq, bq, Wk, bk, Wv, bv, gamma):
            q = jnp.einsum('oc,bcl->bol', Wq, x) + bq[None, :, None]
            k = jnp.einsum('oc,bcl->bol', Wk, x) + bk[None, :, None]
            v = jnp.einsum('oc,bcl->bol', Wv, x) + bv[None, :, None]
            energy = jnp.einsum('bci,bcj->bij', q, k)
            attn = jax.nn.softmax(energy, axis=-1)
            out = jnp.einsum('bcj,bij->bci', v, attn)
            return gamma * out + x
        key = jax.random.key(seed)
        ks = jax.random.split(key, 32)
        B, D = (128, 8192)
        r = lambda i, shape, s=0.1: jax.random.normal(ks[i], shape, jnp.float32) * s
        return {'x': jax.random.normal(ks[0], (B, D), jnp.float32), 'w1': r(1, (16, 2, 3)), 'b1': r(2, (16,)), 'g1': 1.0 + r(3, (16,)), 'be1': r(4, (16,)), 'm1': r(5, (16,)), 'v1': 0.5 + jax.random.uniform(ks[6], (16,), jnp.float32), 'w2': r(7, (64, 16, 3)), 'b2': r(8, (64,)), 'g2': 1.0 + r(9, (64,)), 'be2': r(10, (64,)), 'm2': r(11, (64,)), 'v2': 0.5 + jax.random.uniform(ks[12], (64,), jnp.float32), 'wq': r(13, (8, 64)), 'bq': r(14, (8,)), 'wk': r(15, (8, 64)), 'bk': r(16, (8,)), 'wv': r(17, (64, 64)), 'bv': r(18, (64,)), 'gamma': jnp.float32(0.7), 'w3': r(19, (128, 64, 4)), 'b3': r(20, (128,)), 'g3': 1.0 + r(21, (128,)), 'be3': r(22, (128,)), 'm3': r(23, (128,)), 'v3': 0.5 + jax.random.uniform(ks[24], (128,), jnp.float32)}
    _L0_tok_all = _L0_tok_setup()
    _L0_tok_in = {k: v for k, v in _L0_tok_all.items() if k in ('w1', 'b1', 'g1', 'be1', 'm1', 'v1', 'w2', 'b2', 'g2', 'be2', 'm2', 'v2', 'wq', 'bq', 'wk', 'bk', 'wv', 'bv', 'gamma', 'w3', 'b3', 'g3', 'be3', 'm3', 'v3')}
    del _L0_tok_all

    def _L0_attn_setup():
        import jax, jax.numpy as jnp
        import numpy as np
        key = jax.random.key(seed)
        k1, k2, k3 = jax.random.split(key, 3)
        b, n_t, n, n_h = (8, 256, 64, 8)
        s = jax.random.normal(k1, (b, n_t, n), dtype=jnp.float32)
        Q = jax.random.normal(k2, (n_h, n, n), dtype=jnp.float32) * 0.02
        E = jax.random.normal(k3, (n_h, n, n), dtype=jnp.float32) * 0.02
        return {'s': s, 'Q': Q, 'E': E}
    _L0_attn_all = _L0_attn_setup()
    _L0_attn_in = {k: v for k, v in _L0_attn_all.items() if k in ('Q', 'E')}
    del _L0_attn_all

    def _L0_ffn_setup():
        import jax, jax.numpy as jnp
        import numpy as np
        B, S, H, F, E, K = (8, 1024, 64, 128, 16, 2)
        EPS = 1e-05
        key = jax.random.key(seed)
        ks = jax.random.split(key, 9)
        sc = 0.02
        return {'x': jax.random.normal(ks[0], (B, S, H), dtype=jnp.float32), 'gate_w': jax.random.normal(ks[1], (H, E), dtype=jnp.float32) * sc, 'gate_b': jnp.zeros((E,), dtype=jnp.float32), 'w1': jax.random.normal(ks[2], (E, H, F), dtype=jnp.float32) * sc, 'b1': jnp.zeros((E, F), dtype=jnp.float32), 'w2': jax.random.normal(ks[3], (E, F, H), dtype=jnp.float32) * sc, 'b2': jnp.zeros((E, H), dtype=jnp.float32), 'gamma': jnp.ones((H,), dtype=jnp.float32), 'beta': jnp.zeros((H,), dtype=jnp.float32)}
    _L0_ffn_all = _L0_ffn_setup()
    _L0_ffn_in = {k: v for k, v in _L0_ffn_all.items() if k in ('gate_w', 'gate_b', 'w1', 'b1', 'w2', 'b2', 'gamma', 'beta')}
    del _L0_ffn_all

    def _L1_attn_setup():
        import jax, jax.numpy as jnp
        import numpy as np
        import math
        B, T, D_MODEL = (1, 512, 64)
        N_Q, N_KV = (16, 1)
        D_HEAD = D_MODEL // N_KV
        QPG = N_Q // N_KV
        ROPE_BASE = 10000.0
        WINDOW = 128
        EPS = 1.1920929e-07
        NEG = -1e+30

        def _rope(x, base=ROPE_BASE):
            t, d = (x.shape[-2], x.shape[-1])
            freqs = base ** (-2.0 * jnp.arange(d // 2, dtype=jnp.float32) / d)
            theta = jnp.arange(t, dtype=jnp.float32)[:, None] * freqs[None, :]
            cos, sin = (jnp.cos(theta), jnp.sin(theta))
            x1, x2 = (x[..., 0::2], x[..., 1::2])
            r1 = x1 * cos - x2 * sin
            r2 = x1 * sin + x2 * cos
            return jnp.stack([r1, r2], axis=-1).reshape(x.shape)

        def _rmsnorm(x, w):
            return x * jax.lax.rsqrt(jnp.mean(x * x, axis=-1, keepdims=True) + EPS) * w
        key = jax.random.key(seed)
        k0, k1, k2, k3 = jax.random.split(key, 4)
        x = jax.random.normal(k0, (B, T, D_MODEL), dtype=jnp.float32)
        wq = jax.random.normal(k1, (QPG * N_KV * D_HEAD, D_MODEL), dtype=jnp.float32) * 0.02
        wkv = jax.random.normal(k2, (2 * D_HEAD * N_KV, D_MODEL), dtype=jnp.float32) * 0.02
        wo = jax.random.normal(k3, (D_MODEL, D_HEAD * N_Q * N_KV), dtype=jnp.float32) * 0.02
        q_norm_w = jnp.ones((D_HEAD,), dtype=jnp.float32)
        k_norm_w = jnp.ones((D_HEAD,), dtype=jnp.float32)
        return {'x': x, 'wq': wq, 'wkv': wkv, 'wo': wo, 'q_norm_w': q_norm_w, 'k_norm_w': k_norm_w}
    _L1_attn_all = _L1_attn_setup()
    _L1_attn_in = {k: v for k, v in _L1_attn_all.items() if k in ('wq', 'wkv', 'wo', 'q_norm_w', 'k_norm_w')}
    del _L1_attn_all

    def _L1_ffn_setup():
        import jax, jax.numpy as jnp
        import numpy as np
        B, N, D = (16, 1024, 64)
        NUM_EXPERTS, TOP_K, HEADS = (4, 2, 4)
        N_EDGES = 262144
        LN_EPS = 1e-05

        def _layernorm(x, g, b):
            mu = x.mean(-1, keepdims=True)
            var = ((x - mu) ** 2).mean(-1, keepdims=True)
            return (x - mu) * jax.lax.rsqrt(var + LN_EPS) * g + b

        def _forward(x, edge_index, W_gat, att_src, att_dst, b_gat, ln_gamma, ln_beta, W1, b1, W2, b2):
            Bc, Nc, Dc = x.shape
            M = Bc * Nc
            x_flat = x.reshape(M, Dc)
            h = (x_flat @ W_gat).reshape(M, HEADS, NUM_EXPERTS)
            loops = jnp.arange(M, dtype=edge_index.dtype)
            src = jnp.concatenate([edge_index[0], loops])
            dst = jnp.concatenate([edge_index[1], loops])
            a_src = (h * att_src).sum(-1)
            a_dst = (h * att_dst).sum(-1)
            e = jax.nn.leaky_relu(a_src[src] + a_dst[dst], negative_slope=0.2)
            e_max = jax.ops.segment_max(e, dst, num_segments=M)
            ee = jnp.exp(e - e_max[dst])
            denom = jax.ops.segment_sum(ee, dst, num_segments=M)
            alpha = ee / (denom[dst] + 1e-16)
            msg = h[src] * alpha[:, :, None]
            agg = jax.ops.segment_sum(msg, dst, num_segments=M).reshape(M, HEADS * NUM_EXPERTS) + b_gat
            scores = _layernorm(agg, ln_gamma, ln_beta).reshape(M, HEADS, NUM_EXPERTS).mean(1)
            scores = scores.reshape(Bc, Nc, NUM_EXPERTS)
            topk_s, topk_i = jax.lax.top_k(scores, TOP_K)
            w = jax.nn.softmax(topk_s, axis=-1)
            out = jnp.zeros_like(x)
            for ei in range(NUM_EXPERTS):
                g = jnp.where(topk_i == ei, w, 0.0).sum(-1)
                hh = jax.nn.gelu(x @ W1[ei] + b1[ei], approximate=False)
                out = out + g[..., None] * (hh @ W2[ei] + b2[ei])
            return out
        key = jax.random.key(seed)
        ks = jax.random.split(key, 8)
        s = 0.05
        return {'x': jax.random.normal(ks[0], (B, N, D), jnp.float32), 'W_gat': jax.random.normal(ks[1], (D, HEADS * NUM_EXPERTS), jnp.float32) * s, 'att_src': jax.random.normal(ks[2], (HEADS, NUM_EXPERTS), jnp.float32) * s, 'att_dst': jax.random.normal(ks[3], (HEADS, NUM_EXPERTS), jnp.float32) * s, 'b_gat': jnp.zeros((HEADS * NUM_EXPERTS,), jnp.float32), 'ln_gamma': jnp.ones((HEADS * NUM_EXPERTS,), jnp.float32), 'ln_beta': jnp.zeros((HEADS * NUM_EXPERTS,), jnp.float32), 'W1': jax.random.normal(ks[4], (NUM_EXPERTS, D, 2 * D), jnp.float32) * s, 'b1': jnp.zeros((NUM_EXPERTS, 2 * D), jnp.float32), 'W2': jax.random.normal(ks[5], (NUM_EXPERTS, 2 * D, D), jnp.float32) * s, 'b2': jnp.zeros((NUM_EXPERTS, D), jnp.float32), 'edge_index': jax.random.randint(ks[6], (2, N_EDGES), 0, B * N, jnp.int32)}
    _L1_ffn_all = _L1_ffn_setup()
    _L1_ffn_in = {k: v for k, v in _L1_ffn_all.items() if k in ('W_gat', 'att_src', 'att_dst', 'b_gat', 'ln_gamma', 'ln_beta', 'W1', 'b1', 'W2', 'b2', 'edge_index')}
    del _L1_ffn_all
    return {'x': x, 'L0_tok_w1': _L0_tok_in['w1'], 'L0_tok_b1': _L0_tok_in['b1'], 'L0_tok_g1': _L0_tok_in['g1'], 'L0_tok_be1': _L0_tok_in['be1'], 'L0_tok_m1': _L0_tok_in['m1'], 'L0_tok_v1': _L0_tok_in['v1'], 'L0_tok_w2': _L0_tok_in['w2'], 'L0_tok_b2': _L0_tok_in['b2'], 'L0_tok_g2': _L0_tok_in['g2'], 'L0_tok_be2': _L0_tok_in['be2'], 'L0_tok_m2': _L0_tok_in['m2'], 'L0_tok_v2': _L0_tok_in['v2'], 'L0_tok_wq': _L0_tok_in['wq'], 'L0_tok_bq': _L0_tok_in['bq'], 'L0_tok_wk': _L0_tok_in['wk'], 'L0_tok_bk': _L0_tok_in['bk'], 'L0_tok_wv': _L0_tok_in['wv'], 'L0_tok_bv': _L0_tok_in['bv'], 'L0_tok_gamma': _L0_tok_in['gamma'], 'L0_tok_w3': _L0_tok_in['w3'], 'L0_tok_b3': _L0_tok_in['b3'], 'L0_tok_g3': _L0_tok_in['g3'], 'L0_tok_be3': _L0_tok_in['be3'], 'L0_tok_m3': _L0_tok_in['m3'], 'L0_tok_v3': _L0_tok_in['v3'], 'L0_attn_Q': _L0_attn_in['Q'], 'L0_attn_E': _L0_attn_in['E'], 'L0_ffn_gate_w': _L0_ffn_in['gate_w'], 'L0_ffn_gate_b': _L0_ffn_in['gate_b'], 'L0_ffn_w1': _L0_ffn_in['w1'], 'L0_ffn_b1': _L0_ffn_in['b1'], 'L0_ffn_w2': _L0_ffn_in['w2'], 'L0_ffn_b2': _L0_ffn_in['b2'], 'L0_ffn_gamma': _L0_ffn_in['gamma'], 'L0_ffn_beta': _L0_ffn_in['beta'], 'L1_attn_wq': _L1_attn_in['wq'], 'L1_attn_wkv': _L1_attn_in['wkv'], 'L1_attn_wo': _L1_attn_in['wo'], 'L1_attn_q_norm_w': _L1_attn_in['q_norm_w'], 'L1_attn_k_norm_w': _L1_attn_in['k_norm_w'], 'L1_ffn_W_gat': _L1_ffn_in['W_gat'], 'L1_ffn_att_src': _L1_ffn_in['att_src'], 'L1_ffn_att_dst': _L1_ffn_in['att_dst'], 'L1_ffn_b_gat': _L1_ffn_in['b_gat'], 'L1_ffn_ln_gamma': _L1_ffn_in['ln_gamma'], 'L1_ffn_ln_beta': _L1_ffn_in['ln_beta'], 'L1_ffn_W1': _L1_ffn_in['W1'], 'L1_ffn_b1': _L1_ffn_in['b1'], 'L1_ffn_W2': _L1_ffn_in['W2'], 'L1_ffn_b2': _L1_ffn_in['b2'], 'L1_ffn_edge_index': _L1_ffn_in['edge_index']}

def reference(x, L0_tok_w1, L0_tok_b1, L0_tok_g1, L0_tok_be1, L0_tok_m1, L0_tok_v1, L0_tok_w2, L0_tok_b2, L0_tok_g2, L0_tok_be2, L0_tok_m2, L0_tok_v2, L0_tok_wq, L0_tok_bq, L0_tok_wk, L0_tok_bk, L0_tok_wv, L0_tok_bv, L0_tok_gamma, L0_tok_w3, L0_tok_b3, L0_tok_g3, L0_tok_be3, L0_tok_m3, L0_tok_v3, L0_attn_Q, L0_attn_E, L0_ffn_gate_w, L0_ffn_gate_b, L0_ffn_w1, L0_ffn_b1, L0_ffn_w2, L0_ffn_b2, L0_ffn_gamma, L0_ffn_beta, L1_attn_wq, L1_attn_wkv, L1_attn_wo, L1_attn_q_norm_w, L1_attn_k_norm_w, L1_ffn_W_gat, L1_ffn_att_src, L1_ffn_att_dst, L1_ffn_b_gat, L1_ffn_ln_gamma, L1_ffn_ln_beta, L1_ffn_W1, L1_ffn_b1, L1_ffn_W2, L1_ffn_b2, L1_ffn_edge_index):
    import jax
    import jax.numpy as jnp

    def _L0_tok_ref(x, w1, b1, g1, be1, m1, v1, w2, b2, g2, be2, m2, v2, wq, bq, wk, bk, wv, bv, gamma, w3, b3, g3, be3, m3, v3):
        import jax, jax.numpy as jnp
        import numpy as np
        EPS = 1e-05

        def _conv1d(x, W, b, stride, pad):
            y = jax.lax.conv_general_dilated(x, W, (stride,), [(pad, pad)], dimension_numbers=('NCH', 'OIH', 'NCH'))
            return y + b[None, :, None]

        def _bn(x, g, b, m, v):
            return (x - m[None, :, None]) * (g * jax.lax.rsqrt(v + EPS))[None, :, None] + b[None, :, None]

        def _maxpool(x, k):
            B, C, L = x.shape
            return x.reshape(B, C, L // k, k).max(axis=-1)

        def _self_attn(x, Wq, bq, Wk, bk, Wv, bv, gamma):
            q = jnp.einsum('oc,bcl->bol', Wq, x) + bq[None, :, None]
            k = jnp.einsum('oc,bcl->bol', Wk, x) + bk[None, :, None]
            v = jnp.einsum('oc,bcl->bol', Wv, x) + bv[None, :, None]
            energy = jnp.einsum('bci,bcj->bij', q, k)
            attn = jax.nn.softmax(energy, axis=-1)
            out = jnp.einsum('bcj,bij->bci', v, attn)
            return gamma * out + x
        B, D = x.shape
        emb_sample, emb_task = (x[:, :D // 2], x[:, D // 2:])
        h = jnp.stack([emb_sample, emb_task], axis=1)
        h = _maxpool(jax.nn.relu(_bn(_conv1d(h, w1, b1, 1, 1), g1, be1, m1, v1)), 8)
        h = _maxpool(jax.nn.relu(_bn(_conv1d(h, w2, b2, 1, 1), g2, be2, m2, v2)), 4)
        h = _self_attn(h, wq, bq, wk, bk, wv, bv, gamma)
        h = _bn(_conv1d(h, w3, b3, 2, 1), g3, be3, m3, v3)
        return h

    def _L0_attn_ref(s, Q, E):
        import jax, jax.numpy as jnp
        import numpy as np
        n_t = s.shape[1]
        qs = jnp.einsum('bti,hij->bhtj', s, Q)
        Omega = jnp.einsum('bhtj,buj->bhtu', qs, s)
        mask = jnp.tril(jnp.ones((n_t, n_t), dtype=s.dtype))
        Omega = Omega * mask
        es = jnp.einsum('hij,buj->bhui', E, s)
        r = jnp.einsum('bhtu,bhui->bti', Omega, es)
        return r

    def _L0_ffn_ref(x, gate_w, gate_b, w1, b1, w2, b2, gamma, beta):
        import jax, jax.numpy as jnp
        import numpy as np
        B, S, H, F, E, K = (8, 1024, 64, 128, 16, 2)
        EPS = 1e-05
        gate_logits = x @ gate_w + gate_b
        topk_vals, topk_idx = jax.lax.top_k(gate_logits, K)
        topk_w = jax.nn.softmax(topk_vals, axis=-1)
        h = jax.nn.relu(jnp.einsum('bsh,ehf->bsef', x, w1) + b1)
        expert_out = jnp.einsum('bsef,efh->bseh', h, w2) + b2
        sel = jnp.take_along_axis(expert_out, topk_idx[:, :, :, None], axis=2)
        moe = jnp.sum(topk_w[..., None] * sel, axis=2)
        y = x + moe
        mu = jnp.mean(y, axis=-1, keepdims=True)
        var = jnp.var(y, axis=-1, keepdims=True)
        return (y - mu) / jnp.sqrt(var + EPS) * gamma + beta

    def _L1_attn_ref(x, wq, wkv, wo, q_norm_w, k_norm_w):
        import jax, jax.numpy as jnp
        import numpy as np
        import math
        B, T, D_MODEL = (1, 512, 64)
        N_Q, N_KV = (16, 1)
        D_HEAD = D_MODEL // N_KV
        QPG = N_Q // N_KV
        ROPE_BASE = 10000.0
        WINDOW = 128
        EPS = 1.1920929e-07
        NEG = -1e+30

        def _rope(x, base=ROPE_BASE):
            t, d = (x.shape[-2], x.shape[-1])
            freqs = base ** (-2.0 * jnp.arange(d // 2, dtype=jnp.float32) / d)
            theta = jnp.arange(t, dtype=jnp.float32)[:, None] * freqs[None, :]
            cos, sin = (jnp.cos(theta), jnp.sin(theta))
            x1, x2 = (x[..., 0::2], x[..., 1::2])
            r1 = x1 * cos - x2 * sin
            r2 = x1 * sin + x2 * cos
            return jnp.stack([r1, r2], axis=-1).reshape(x.shape)

        def _rmsnorm(x, w):
            return x * jax.lax.rsqrt(jnp.mean(x * x, axis=-1, keepdims=True) + EPS) * w
        Bx, Tx, C = x.shape
        q = x @ wq.T
        kv = x @ wkv.T
        k, v = (kv[..., :N_KV * D_HEAD], kv[..., N_KV * D_HEAD:])
        q = q.reshape(Bx, Tx, QPG, N_KV, D_HEAD).transpose(0, 2, 3, 1, 4)
        k = k.reshape(Bx, Tx, 1, N_KV, D_HEAD).transpose(0, 2, 3, 1, 4)
        v = v.reshape(Bx, Tx, 1, N_KV, D_HEAD).transpose(0, 2, 3, 1, 4)
        q = _rmsnorm(_rope(q), q_norm_w)
        k = _rmsnorm(_rope(k), k_norm_w)
        rows = jnp.arange(Tx)[:, None]
        cols = jnp.arange(Tx)[None, :]
        mask = (cols <= rows) & (rows - cols <= WINDOW)
        scale = 1.0 / math.sqrt(D_HEAD)
        scores = jnp.einsum('bqgtd,bqgsd->bqgts', q, k) * scale
        scores = jnp.where(mask[None, None, None], scores, NEG)
        attn = jax.nn.softmax(scores, axis=-1)
        out = jnp.einsum('bqgts,bqgsd->bqgtd', attn, v)
        out = out.transpose(0, 3, 1, 2, 4).reshape(Bx, Tx, QPG * N_KV * D_HEAD)
        return out @ wo.T

    def _L1_ffn_ref(x, W_gat, att_src, att_dst, b_gat, ln_gamma, ln_beta, W1, b1, W2, b2, edge_index):
        import jax, jax.numpy as jnp
        import numpy as np
        B, N, D = (16, 1024, 64)
        NUM_EXPERTS, TOP_K, HEADS = (4, 2, 4)
        N_EDGES = 262144
        LN_EPS = 1e-05

        def _layernorm(x, g, b):
            mu = x.mean(-1, keepdims=True)
            var = ((x - mu) ** 2).mean(-1, keepdims=True)
            return (x - mu) * jax.lax.rsqrt(var + LN_EPS) * g + b

        def _forward(x, edge_index, W_gat, att_src, att_dst, b_gat, ln_gamma, ln_beta, W1, b1, W2, b2):
            Bc, Nc, Dc = x.shape
            M = Bc * Nc
            x_flat = x.reshape(M, Dc)
            h = (x_flat @ W_gat).reshape(M, HEADS, NUM_EXPERTS)
            loops = jnp.arange(M, dtype=edge_index.dtype)
            src = jnp.concatenate([edge_index[0], loops])
            dst = jnp.concatenate([edge_index[1], loops])
            a_src = (h * att_src).sum(-1)
            a_dst = (h * att_dst).sum(-1)
            e = jax.nn.leaky_relu(a_src[src] + a_dst[dst], negative_slope=0.2)
            e_max = jax.ops.segment_max(e, dst, num_segments=M)
            ee = jnp.exp(e - e_max[dst])
            denom = jax.ops.segment_sum(ee, dst, num_segments=M)
            alpha = ee / (denom[dst] + 1e-16)
            msg = h[src] * alpha[:, :, None]
            agg = jax.ops.segment_sum(msg, dst, num_segments=M).reshape(M, HEADS * NUM_EXPERTS) + b_gat
            scores = _layernorm(agg, ln_gamma, ln_beta).reshape(M, HEADS, NUM_EXPERTS).mean(1)
            scores = scores.reshape(Bc, Nc, NUM_EXPERTS)
            topk_s, topk_i = jax.lax.top_k(scores, TOP_K)
            w = jax.nn.softmax(topk_s, axis=-1)
            out = jnp.zeros_like(x)
            for ei in range(NUM_EXPERTS):
                g = jnp.where(topk_i == ei, w, 0.0).sum(-1)
                hh = jax.nn.gelu(x @ W1[ei] + b1[ei], approximate=False)
                out = out + g[..., None] * (hh @ W2[ei] + b2[ei])
            return out
        return _forward(x, edge_index, W_gat, att_src, att_dst, b_gat, ln_gamma, ln_beta, W1, b1, W2, b2)
    h = _L0_tok_ref(x, L0_tok_w1, L0_tok_b1, L0_tok_g1, L0_tok_be1, L0_tok_m1, L0_tok_v1, L0_tok_w2, L0_tok_b2, L0_tok_g2, L0_tok_be2, L0_tok_m2, L0_tok_v2, L0_tok_wq, L0_tok_bq, L0_tok_wk, L0_tok_bk, L0_tok_wv, L0_tok_bv, L0_tok_gamma, L0_tok_w3, L0_tok_b3, L0_tok_g3, L0_tok_be3, L0_tok_m3, L0_tok_v3)
    h = h + _L0_attn_ref(_layernorm(h, axis=-1), L0_attn_Q, L0_attn_E)
    h = h + _L0_ffn_ref(_layernorm(h, axis=-1), L0_ffn_gate_w, L0_ffn_gate_b, L0_ffn_w1, L0_ffn_b1, L0_ffn_w2, L0_ffn_b2, L0_ffn_gamma, L0_ffn_beta)
    h = h + _L1_attn_ref(_layernorm(h, axis=-1), L1_attn_wq, L1_attn_wkv, L1_attn_wo, L1_attn_q_norm_w, L1_attn_k_norm_w)
    h = h + _L1_ffn_ref(_layernorm(h, axis=-1), L1_ffn_W_gat, L1_ffn_att_src, L1_ffn_att_dst, L1_ffn_b_gat, L1_ffn_ln_gamma, L1_ffn_ln_beta, L1_ffn_W1, L1_ffn_b1, L1_ffn_W2, L1_ffn_b2, L1_ffn_edge_index)
    return h

_drawn_inputs = setup_inputs


def setup_inputs(seed=0):
    import zlib

    import numpy as np

    out = dict(_drawn_inputs(seed))
    spreads = {'L0_ffn_gate_b': (0.0, 0.8),
     'L0_ffn_b1': (0.0, 0.8),
     'L0_ffn_b2': (0.0, 0.8),
     'L0_ffn_gamma': (1.0, 0.6),
     'L0_ffn_beta': (0.0, 0.8),
     'L1_attn_q_norm_w': (1.0, 0.6),
     'L1_attn_k_norm_w': (1.0, 0.6),
     'L1_ffn_b_gat': (0.0, 0.8),
     'L1_ffn_ln_gamma': (1.0, 0.6),
     'L1_ffn_ln_beta': (0.0, 0.8),
     'L1_ffn_b1': (0.0, 0.8),
     'L1_ffn_b2': (0.0, 0.8)}
    factors = {'L0_tok_wq': 8.0,
     'L0_tok_bq': 8.0,
     'L0_tok_wk': 8.0,
     'L0_tok_bk': 8.0,
     'L0_tok_b3': 7.223,
     'L0_tok_g3': 8.0,
     'L0_tok_be3': 8.0,
     'L0_tok_m3': 6.282,
     'L0_tok_v3': 8.0,
     'L0_ffn_gate_w': 8.0,
     'L0_ffn_w1': 8.0,
     'L0_ffn_w2': 8.0,
     'L1_attn_wq': 8.0,
     'L1_attn_wkv': 8.0,
     'L1_attn_wo': 8.0,
     'L1_ffn_W_gat': 8.0,
     'L1_ffn_att_src': 8.0,
     'L1_ffn_att_dst': 8.0,
     'L1_ffn_W1': 7.908,
     'L1_ffn_W2': 7.541}
    for name, (base, spread) in spreads.items():
        noise = np.random.default_rng([zlib.crc32(name.encode()), seed]).standard_normal(out[name].shape)
        drawn = base * np.exp(spread * noise) if base else spread * noise
        out[name] = jnp.asarray(drawn.astype(out[name].dtype))
    for name, factor in factors.items():
        out[name] = (out[name] * factor).astype(out[name].dtype)
    return out
```

```python
import numpy as np
import concourse.bass as bass
from concourse import mybir
from contextlib import ExitStack, contextmanager

F32 = mybir.dt.float32
BF16 = mybir.dt.bfloat16
I32 = mybir.dt.int32
U32 = mybir.dt.uint32
ALU = mybir.AluOpType
ACT = mybir.ActivationFunctionType
AX = mybir.AxisListType.X
BN_EPS = 1e-5


@contextmanager
def semaphores(nc, prefix):
    mine = []

    def one(name):
        mine.append(nc.alloc_semaphore(name=prefix + name))
        return mine[-1]
    yield one
    nc.clear_and_free_semaphores(mine)
    nc.all_engine_barrier()


class Steps:

    def __init__(self, sem, per, turn):
        self.sem, self.per, self.turn, self.n = sem, per, turn, 0

    def did(self, ins):
        ins.then_inc(self.sem, 1)
        self.n += 1
        return self.n

    def wait(self, eng, n=None):
        n = self.n if n is None else n
        eng.wait_ge(self.sem, n if self.turn is None else self.turn * self.per + n)

    def chain(self, eng, ins):
        self.did(ins)
        self.wait(eng)

    def close(self):
        assert self.n == self.per, (self.n, self.per)


def tokenizer(nc, x, wc1, p1row, p1col, wc2, p2row, p2col, wq, wk, bqk, wv, pv, wc3, p3col, h_out):
    B = x.shape[0]
    L = x.shape[1] // 2
    TURNS = B // 8
    L1, L2 = L // 8, L // 32
    with ExitStack() as ctx:
        sb = lambda n, s, d=F32: ctx.enter_context(nc.sbuf_tensor("tks_" + n, s, d))
        pb = lambda n, s, d=F32: ctx.enter_context(nc.psum_tensor("tkp_" + n, s, d))
        sem = ctx.enter_context(semaphores(nc, "tkm_"))
        xin = sb("xin", [96, L])
        w1 = sb("w1", [96, 128]); r1 = sb("r1", [96, 2, 128]); sc1 = sb("sc1", [96, 128])
        c1 = sb("c1", [128, 5]); bias1 = sb("bias1", [128, 2])
        w2 = sb("w2", [128, 12, 128]); r2 = sb("r2", [128, 2, 128]); sc2 = sb("sc2", [128, 128])
        c2 = sb("c2", [128, 5]); bias2 = sb("bias2", [128, 2])
        c3 = sb("c3", [128, 5]); bias3 = sb("bias3", [128, 2])
        half = sb("half", [128, 128])
        wq_s = sb("wq", [128, 64]); wk_s = sb("wk", [128, 64]); bqk_s = sb("bqk", [64, 2])
        wv_s = sb("wv", [128, 128]); pv_s = sb("pv", [128, 2]); gbv = sb("gbv", [128, 1])
        w3 = sb("w3", [128, 2, 4, 128])
        ident = sb("ident", [128, 128])
        a1 = sb("a1", [128, L1]); a1r = sb("a1r", [128, L1 + 2])
        a2 = sb("a2", [128, 4, L2]); h2 = sb("h2", [128, 4, L2])
        q = sb("q", [64, 4 * L2]); k = sb("k", [64, 4 * L2])
        mx = sb("mx", [128, 8]); sums = sb("sums", [128, 8]); rs = sb("rs", [128, 8])
        p = sb("p", [128, 8, 128]); pn = sb("pn", [128, 8, 128]); pT = sb("pT", [128, 8, 128])
        vT = sb("vT", [128, 4, 128])
        og = sb("og", [128, 4, L2]); h3 = sb("h3", [128, 4, L2 + 2])
        h0 = sb("h0", [128, 4, 2, 64])
        conv_ps = pb("conv_ps", [128, 2, 512])
        qk_ps = pb("qk_ps", [64, 2, 512])
        e_ps = pb("e_ps", [128, 2, 512])
        v_ps = pb("v_ps", [128, 512])
        o_ps = pb("o_ps", [128, 512])
        pT_ps = e_ps

        w_in = sem("w_in"); x_in = sem("x_in"); stored = sem("stored")
        pre = sem("pre"); pw = sem("pw"); rec = sem("rec"); ident_ok = sem("ident_ok"); clean = sem("clean")
        c1_mm = sem("c1_mm"); c1_max = sem("c1_max"); a1_ok = sem("a1_ok")
        c2_mm = sem("c2_mm"); c2_max = sem("c2_max"); h2_ok = sem("h2_ok")
        qk_mm = sem("qk_mm"); qk_ok = sem("qk_ok"); v_mm = sem("v_mm"); v_ok = sem("v_ok")
        e_mm = sem("e_mm"); mx_ok = sem("mx_ok"); exp_ok = sem("exp_ok"); soft = sem("soft")
        pT_mm = sem("pT_mm"); pT_ok = sem("pT_ok")
        o_mm = sem("o_mm"); og_ok = sem("og_ok"); h3_ok = sem("h3_ok"); c3_mm = sem("c3_mm"); h0_ok = sem("h0_ok")
        xr = x.rearrange("b (c l) -> (b c) l", c=2)
        ho = h_out.rearrange("(g p u) t n -> t g p u n", p=4, u=2)
        loads = [(w1, wc1), (r1, p1row), (c1, p1col), (w2, wc2), (r2, p2row), (c2, p2col), (c3, p3col),
                 (wq_s, wq), (wk_s, wk), (bqk_s, bqk), (wv_s, wv), (pv_s, pv), (w3, wc3)]
        block = ctx.enter_context(nc.Block())

        @block.sync
        def _(sp):
            for dst, src in loads:
                sp.dma_start(dst[:], src).then_inc(w_in, 16)
            sp.wait_ge(clean, 1)
            with sp.Fori(0, TURNS) as i:
                sp.wait_ge(c1_mm, i * 8 + 8)
                rows = xr[bass.ds(i * 16, 16), :]
                sp.dma_start(xin[0:16, 1:L], rows[:, 0:L - 1]).then_inc(x_in, 16)
                sp.dma_start(xin[32:48, :], rows).then_inc(x_in, 16)
                sp.dma_start(xin[64:80, 0:L - 1], rows[:, 1:L]).then_inc(x_in, 16)

        @block.gpsimd
        def _(pool):
            nc.gpsimd.memset(ident[:], 0.0).then_inc(ident_ok, 1)
            nc.gpsimd.memset(half[:], -0.5).then_inc(ident_ok, 1)
            pool.wait_ge(ident_ok, 2)
            nc.gpsimd.affine_select(out=ident[:], in_=ident[:], compare_op=ALU.not_equal, fill=1.0, base=0,
                                    pattern=[[-1, 128]], channel_multiplier=1).then_inc(ident_ok, 1)
            pool.wait_ge(pre, 5)
            nc.gpsimd.tensor_tensor(bias1[:, 0:1], c1[:, 4:5], half[:, 0:1], ALU.pow).then_inc(pw, 1)
            nc.gpsimd.tensor_tensor(bias2[:, 0:1], c2[:, 4:5], half[:, 0:1], ALU.pow).then_inc(pw, 1)
            nc.gpsimd.tensor_tensor(bias3[:, 0:1], c3[:, 4:5], half[:, 0:1], ALU.pow).then_inc(pw, 1)

        @block.vector
        def _(dve):
            V = nc.vector
            V.memset(xin[:], 0.0).then_inc(clean, 1)
            V.memset(a1r[:], 0.0).then_inc(clean, 1)
            V.memset(h3[:], 0.0).then_inc(clean, 1)
            dve.wait_ge(clean, 3)
            dve.wait_ge(w_in, 16 * len(loads))
            V.tensor_scalar_add(r1[:, 1, :], r1[:, 1, :], BN_EPS).then_inc(pre, 1)
            V.tensor_scalar_add(r2[:, 1, :], r2[:, 1, :], BN_EPS).then_inc(pre, 1)
            dve.wait_ge(pre, 2)
            V.reciprocal(sc1[:], r1[:, 1, :]).then_inc(rec, 1)
            V.reciprocal(sc2[:], r2[:, 1, :]).then_inc(rec, 1)
            for t in (c1, c2, c3):
                V.tensor_scalar_add(t[:, 4:5], t[:, 4:5], BN_EPS).then_inc(pre, 1)
            dve.wait_ge(pw, 5)
            done = Steps(pre, 5, None); done.n = 5
            done.did(V.tensor_tensor(sc1[:], sc1[:], r1[:, 0, :], ALU.mult))
            done.chain(dve, V.tensor_tensor(sc2[:], sc2[:], r2[:, 0, :], ALU.mult))
            done.did(V.tensor_tensor(w1[:], w1[:], sc1[:], ALU.mult))
            done.did(V.tensor_tensor(w2[:], w2[:], sc2[:].rearrange("p (a n) -> p a n", a=1).to_broadcast([128, 12, 128]), ALU.mult))
            for c, bi in ((c1, bias1), (c2, bias2), (c3, bias3)):
                done.chain(dve, V.tensor_tensor(bi[:, 0:1], bi[:, 0:1], c[:, 2:3], ALU.mult))
                done.chain(dve, V.tensor_tensor(bi[:, 1:2], c[:, 0:1], c[:, 1:2], ALU.subtract))
                done.chain(dve, V.tensor_tensor(bi[:, 1:2], bi[:, 1:2], bi[:, 0:1], ALU.mult))
                done.did(V.tensor_tensor(bi[:, 1:2], bi[:, 1:2], c[:, 3:4], ALU.add))
            done.did(V.tensor_tensor(gbv[:], pv_s[:, 0:1], pv_s[:, 1:2], ALU.mult))
            done.wait(dve)
            dve.sem_inc(pre, 100)
            with dve.Fori(0, TURNS) as i:
                soft_n = Steps(soft, 2, i)
                for c in range(8):
                    dve.wait_ge(c1_mm, i * 8 + (8 + c + 1))
                    if c == 0:
                        dve.wait_ge(a1_ok, i + 1)
                    V.tensor_reduce(a1[:, c * 64:(c + 1) * 64],
                                    conv_ps[:, c % 2, :].rearrange("p (a k) -> p a k", k=8), AX, ALU.max).then_inc(c1_max, 1)
                for pr in range(4):
                    dve.wait_ge(c2_mm, i * 4 + (pr + 1))
                    if pr == 0:
                        dve.wait_ge(h2_ok, i + 1)
                    V.tensor_reduce(a2[:, pr, :], conv_ps[:, pr % 2, :].rearrange("p (a k) -> p a k", k=4), AX, ALU.max).then_inc(c2_max, 1)
                dve.wait_ge(e_mm, i + 1)
                V.tensor_reduce(mx[:], e_ps[:].rearrange("p u (r j) -> p (u r) j", j=128), AX, ALU.max, negate=True).then_inc(mx_ok, 1)
                dve.wait_ge(exp_ok, i * 8 + 8)
                soft_n.chain(dve, V.reciprocal(rs[:], sums[:]))
                soft_n.did(V.tensor_tensor(pn[:], p[:], rs[:].rearrange("p (a o) -> p a o", o=1).to_broadcast([128, 8, 128]), ALU.mult))
                dve.wait_ge(pT_mm, i + 1)
                V.tensor_copy(pT[:, 0:4, :], pT_ps[:, 0, :].rearrange("p (a k) -> p a k", k=128)).then_inc(pT_ok, 1)
                dve.wait_ge(og_ok, i + 1)
                V.tensor_tensor(h3[:, :, 1:L2 + 1], og[:], h2[:], ALU.add).then_inc(h3_ok, 1)
                soft_n.close()

        @block.scalar
        def _(act):
            A = nc.scalar
            act.wait_ge(rec, 2)
            A.activation(sc1[:], sc1[:], ACT.Sqrt).then_inc(pw, 1)
            A.activation(sc2[:], sc2[:], ACT.Sqrt).then_inc(pw, 1)
            act.wait_ge(pre, 120)
            act.sem_inc(a1_ok, 1)
            act.sem_inc(h2_ok, 1)
            with act.Fori(0, TURNS) as i:
                act.wait_ge(c1_max, i * 8 + 8)
                A.activation(a1r[:, 1:L1 + 1], a1[:], ACT.Relu, bias=bias1[:, 1:2]).then_inc(a1_ok, 1)
                act.wait_ge(c2_max, i * 4 + 4)
                A.activation(h2[:], a2[:], ACT.Relu, bias=bias2[:, 1:2]).then_inc(h2_ok, 1)
                act.wait_ge(qk_mm, i * 2 + 2)
                A.activation(q[:], qk_ps[:, 0, :], ACT.Identity, bias=bqk_s[:, 0:1]).then_inc(qk_ok, 1)
                A.activation(k[:], qk_ps[:, 1, :], ACT.Identity, bias=bqk_s[:, 1:2]).then_inc(qk_ok, 1)
                act.wait_ge(v_mm, i + 1)
                A.activation(vT[:], v_ps[:].rearrange("p (a k) -> p a k", k=128), ACT.Copy).then_inc(v_ok, 1)
                act.wait_ge(mx_ok, i + 1)
                for r in range(8):
                    A.activation(p[:, r, :], e_ps[:, r // 4, (r % 4) * 128:(r % 4 + 1) * 128], ACT.Exp,
                                 bias=mx[:, r:r + 1], accum_out=sums[:, r:r + 1]).then_inc(exp_ok, 1)
                act.wait_ge(pT_mm, i + 1)
                A.activation(pT[:, 4:8, :], pT_ps[:, 1, :].rearrange("p (a k) -> p a k", k=128), ACT.Copy).then_inc(pT_ok, 1)
                act.wait_ge(o_mm, i + 1)
                A.activation(og[:], o_ps[:].rearrange("p (a k) -> p a k", k=128), ACT.Identity, bias=gbv[:], scale=pv_s[:, 0:1]).then_inc(og_ok, 1)
                act.wait_ge(c3_mm, i * 2 + 2)
                act.wait_ge(stored, i * 32)
                for u in range(2):
                    A.activation(h0[:, :, u, :], conv_ps[:, u, 0:256].rearrange("p (a k) -> p a k", k=64), ACT.Identity,
                                 bias=bias3[:, 1:2], scale=bias3[:, 0:1]).then_inc(h0_ok, 1)
                act.wait_ge(h0_ok, i * 2 + 2)
                for u in range(2):
                    act.dma_start(ho[:, bass.ds(i, 1), :, u, :], h0[:, :, u, :].rearrange("p (o a) n -> p o a n", o=1)).then_inc(stored, 16)
            act.wait_ge(stored, TURNS * 32)

        @block.tensor
        def _(pe):
            M = nc.tensor.matmul
            pe.sem_inc(c1_mm, 8)
            pe.wait_ge(pre, 120)
            pe.wait_ge(ident_ok, 3)
            with pe.Fori(0, TURNS) as i:
                pe.wait_ge(x_in, i * 48 + 48)
                pe.wait_ge(h0_ok, i * 2)
                for c in range(8):
                    if c >= 2:
                        pe.wait_ge(c1_max, i * 8 + (c - 1))
                    M(conv_ps[:, c % 2, :], w1[:], xin[:, c * 512:(c + 1) * 512], start=True, stop=True).then_inc(c1_mm, 1)
                pe.wait_ge(c1_max, i * 8 + 8)
                pe.wait_ge(a1_ok, i + 2)
                for pr in range(4):
                    if pr >= 2:
                        pe.wait_ge(c2_max, i * 4 + (pr - 1))
                    for t in range(3):
                        mm = M(conv_ps[:, pr % 2, :], w2[:, pr * 3 + t, :], a1r[:, t:t + L1], start=(t == 0), stop=(t == 2))
                    mm.then_inc(c2_mm, 1)
                pe.wait_ge(h2_ok, i + 2)
                hh = h2[:].rearrange("p a k -> p (a k)")
                M(qk_ps[:, 0, :], wq_s[:], hh, start=True, stop=True).then_inc(qk_mm, 1)
                M(qk_ps[:, 1, :], wk_s[:], hh, start=True, stop=True).then_inc(qk_mm, 1)
                for pr in range(4):
                    mm = M(v_ps[:, pr * 128:(pr + 1) * 128], h2[:, pr, :], wv_s[:], start=True, stop=True)
                mm.then_inc(v_mm, 1)
                pe.wait_ge(qk_ok, i * 2 + 2)
                for u in range(2):
                    for pr in range(4):
                        s = slice(pr * 128, (pr + 1) * 128)
                        mm = M(e_ps[:, u, s], q[32 * u:32 * u + 8, s], k[32 * u:32 * u + 8, s], start=True, stop=True)
                mm.then_inc(e_mm, 1)
                pe.wait_ge(soft, i * 2 + 2)
                for r in range(8):
                    mm = nc.tensor.transpose(pT_ps[:, r // 4, (r % 4) * 128:(r % 4 + 1) * 128], pn[:, r, :], ident[:])
                mm.then_inc(pT_mm, 1)
                pe.wait_ge(pT_ok, i * 2 + 2)
                pe.wait_ge(v_ok, i + 1)
                for u in range(2):
                    for pr in range(4):
                        mm = M(o_ps[64 * u:64 * u + 64, pr * 128:(pr + 1) * 128], vT[:, pr, 64 * u:64 * u + 64],
                               pT[:, u * 4 + pr, :], start=True, stop=True)
                mm.then_inc(o_mm, 1)
                pe.wait_ge(h3_ok, i + 1)
                for u in range(2):
                    for t in range(4):
                        mm = M(conv_ps[:, u, 0:256], w3[:, u, t, :], h3[:, :, t:t + 127:2],
                               start=(t == 0), stop=(t == 3))
                    mm.then_inc(c3_mm, 1)


def lay_tokenizer(inp):
    g = lambda n: np.asarray(inp["L0_tok_" + n])
    w1, w2, w3 = g("w1"), g("w2"), g("w3")
    wc1 = np.zeros((96, 128), np.float32)
    for t in range(3):
        for b in range(8):
            wc1[32 * t + 2 * b:32 * t + 2 * b + 2, 16 * b:16 * b + 16] = w1[:, :, t].T
    wc2 = np.zeros((128, 12, 128), np.float32)
    for pr in range(4):
        for t in range(3):
            for u in range(2):
                b = 2 * pr + u
                wc2[16 * b:16 * b + 16, pr * 3 + t, 64 * u:64 * u + 64] = w2[:, :, t].T
    row = lambda n, r, parts: np.ascontiguousarray(np.broadcast_to(np.stack([np.tile(g("g" + n), r), np.tile(g("v" + n), r)]), (parts, 2, 128)))
    col = lambda n, r: np.stack([np.tile(g(a + n), r) for a in ("b", "m", "g", "be", "v")], axis=1)
    wq = np.zeros((128, 64), np.float32); wk = np.zeros((128, 64), np.float32); wv = np.zeros((128, 128), np.float32)
    bqk = np.zeros((64, 2), np.float32)
    for u in range(2):
        wq[64 * u:64 * u + 64, 32 * u:32 * u + 8] = g("wq").T
        wk[64 * u:64 * u + 64, 32 * u:32 * u + 8] = g("wk").T
        wv[64 * u:64 * u + 64, 64 * u:64 * u + 64] = g("wv").T
        bqk[32 * u:32 * u + 8, 0] = g("bq")
        bqk[32 * u:32 * u + 8, 1] = g("bk")
    pv = np.stack([np.broadcast_to(g("gamma"), (128,)), np.tile(g("bv"), 2)], axis=1)
    wc3 = np.zeros((128, 2, 4, 128), np.float32)
    for u in range(2):
        wc3[64 * u:64 * u + 64, u] = np.transpose(w3, (1, 2, 0))
    return dict(tk_wc1=wc1, tk_p1row=row("1", 8, 96), tk_p1col=col("1", 8), tk_wc2=wc2, tk_p2row=row("2", 2, 128),
                tk_p2col=col("2", 2), tk_wq=wq, tk_wk=wk, tk_bqk=bqk, tk_wv=wv, tk_pv=pv, tk_wc3=wc3, tk_p3col=col("3", 1))


D = 64
LN_EPS = 1e-5


def turns(eng, n, body):
    with eng.Fori(0, n - 1) as i:
        body(i, True)
    body(n - 1, False)


def bc(t, shape):
    return t.rearrange("p (a o) -> p a o", o=1).to_broadcast(shape)


class LayerNorm:
    STEPS = 5

    def __init__(self, nc, sb, sem, G, copies=1, name="ln"):
        self.nc, self.G, self.copies = nc, G, copies
        self.x = sb(name + "_x", [128, G, D]); self.sq = sb(name + "_sq", [128, G, D])
        self.mu = sb(name + "_mu", [128, G]); self.var = sb(name + "_var", [128, G]); self.rstd = sb(name + "_rstd", [128, G])
        self.minus_half = sb(name + "_half", [128, G])
        self.out = sb(name + "_out", [128, G, copies, D])
        self.loaded, self.step, self.rs = sem(name + "_loaded"), sem(name + "_step"), sem(name + "_rs")

    def load(self, sp, turn, src):
        self.ready(sp, turn - 1)
        sp.dma_start(self.x[:], src).then_inc(self.loaded, 16)

    def start(self):
        self.nc.vector.memset(self.minus_half[:], -0.5).then_inc(self.step, 1)

    def vector(self, dve, turn, loaded=True):
        V, s, G = self.nc.vector, Steps(self.step, self.STEPS, turn), self.G
        wait = lambda n: dve.wait_ge(self.step, turn * self.STEPS + n + 1)
        if loaded:
            dve.wait_ge(self.loaded, turn * 16 + 16)
        s.did(V.tensor_reduce(self.mu[:], self.x[:], AX, ALU.add)); wait(1)
        s.did(V.tensor_scalar(self.mu[:], self.mu[:], 1.0 / D, None, ALU.mult)); wait(2)
        s.did(V.tensor_tensor(self.x[:], self.x[:], bc(self.mu[:], [128, G, D]), ALU.subtract)); wait(3)
        s.did(V.tensor_tensor(self.sq[:], self.x[:], self.x[:], ALU.mult)); wait(4)
        V.tensor_reduce(self.var[:], self.sq[:], AX, ALU.add).then_inc(self.rs, 1)
        dve.wait_ge(self.rs, turn * 3 + 1)
        V.tensor_scalar(self.var[:], self.var[:], 1.0 / D, LN_EPS, ALU.mult, ALU.add).then_inc(self.rs, 1)
        dve.wait_ge(self.rs, turn * 3 + 3)
        for c in range(self.copies - 1):
            V.tensor_tensor(self.out[:, :, c, :], self.x[:], bc(self.rstd[:], [128, G, D]), ALU.mult)
        s.did(V.tensor_tensor(self.out[:, :, self.copies - 1, :], self.x[:], bc(self.rstd[:], [128, G, D]), ALU.mult))
        assert s.n == self.STEPS

    def gpsimd(self, pool, turn):
        pool.wait_ge(self.rs, turn * 3 + 2)
        self.nc.gpsimd.tensor_tensor(self.rstd[:], self.var[:], self.minus_half[:], ALU.pow).then_inc(self.rs, 1)

    def ready(self, eng, turn):
        eng.wait_ge(self.step, turn * self.STEPS + self.STEPS + 1)


def make_identity(nc, pool, ident, sem, n=128):
    nc.gpsimd.memset(ident[:], 0.0).then_inc(sem, 1)
    pool.wait_ge(sem, 1)
    nc.gpsimd.affine_select(out=ident[:], in_=ident[:], compare_op=ALU.not_equal, fill=1.0, base=0,
                            pattern=[[-1, n]], channel_multiplier=1).then_inc(sem, 1)


def linear_attention(nc, h_in, wq, we, h_out):
    B, T, _ = h_in.shape
    G, H = 4, 8
    TURNS = B // G
    with ExitStack() as ctx:
        sb = lambda n, s, d=F32: ctx.enter_context(nc.sbuf_tensor("las_" + n, s, d))
        pb = lambda n, s, d=F32: ctx.enter_context(nc.psum_tensor("lap_" + n, s, d))
        sem = ctx.enter_context(semaphores(nc, "lam_"))
        ln = LayerNorm(nc, sb, sem, G, copies=2)
        w_q = sb("wq", [128, H * 64]); w_e = sb("we", [128, H * 64])
        ident = sb("ident", [128, 128]); tri = sb("tri", [128, 128])
        res = sb("res", [128, G, D]); new = sb("new", [128, G, D])
        sT = sb("sT", [128, 2, G * 128]); qs = sb("qs", [128, 4, G * 128]); es = sb("es", [128, G, H * 64 + 64])
        om = sb("om", [128, 2, 2, 512])
        sT_ps = pb("sT", [128, 512]); ev_ps = pb("ev", [128, 2, 512]); om_ps = pb("om", [128, 2, 2, 512]); r_ps = pb("r", [128, G, 2 * D])
        w_in = sem("w_in"); const = sem("const"); tri_ok = sem("tri_ok"); zeroed = sem("zeroed"); res_in = sem("res_in"); stored = sem("stored")
        sT_mm = sem("sT_mm"); sT_ok = sem("sT_ok"); ev_mm = sem("ev_mm"); ev_ok = sem("ev_ok")
        om_mm = sem("om_mm"); om_ok = sem("om_ok"); r_mm = sem("r_mm"); new_ok = sem("new_ok")
        hi = h_in.rearrange("b t n -> t b n"); ho = h_out.rearrange("b t n -> t b n")
        block = ctx.enter_context(nc.Block())

        @block.sync
        def _(sp):
            sp.dma_start(w_q[:], wq).then_inc(w_in, 16)
            sp.dma_start(w_e[:], we).then_inc(w_in, 16)
            ln.load(sp, 0, hi[:, 0:G, :])

            def turn(i, more):
                sp.wait_ge(new_ok, i + 1)
                sp.dma_start(res[:], hi[:, bass.ds(i * G, G), :]).then_inc(res_in, 16)
                if more:
                    ln.load(sp, i + 1, hi[:, bass.ds(i * G + G, G), :])
            turns(sp, TURNS, turn)

        @block.gpsimd
        def _(pool):
            make_identity(nc, pool, ident, const)
            nc.gpsimd.memset(tri[:], 1.0).then_inc(tri_ok, 1)
            pool.wait_ge(tri_ok, 1)
            nc.gpsimd.affine_select(out=tri[:], in_=tri[:], compare_op=ALU.is_ge, fill=0.0, base=0,
                                    pattern=[[1, 128]], channel_multiplier=-1).then_inc(tri_ok, 1)
            ln.gpsimd(pool, 0)

            def turn(i, more):
                if more:
                    ln.gpsimd(pool, i + 1)
            turns(pool, TURNS, turn)

        @block.vector
        def _(dve):
            V = nc.vector
            ln.start()
            V.memset(sT[:], 0.0).then_inc(zeroed, 1)
            V.memset(es[:], 0.0).then_inc(zeroed, 1)
            dve.sem_inc(new_ok, 1)
            ln.vector(dve, 0)
            dve.wait_ge(tri_ok, 2)

            def turn(i, more):
                if more:
                    dve.wait_ge(sT_mm, i + 1)
                    ln.vector(dve, i + 1)
                for b in range(G):
                    if b >= 2:
                        dve.wait_ge(r_mm, i * G + (b - 1))
                    dve.wait_ge(om_mm, i * G + (b + 1))
                    V.tensor_tensor(om[:, b % 2].rearrange("p u (h t) -> p (u h) t", t=128),
                                    om_ps[:, b % 2].rearrange("p u (h t) -> p (u h) t", t=128),
                                    tri[:].rearrange("p (o t) -> p o t", o=1).to_broadcast([128, 8, 128]), ALU.mult).then_inc(om_ok, 1)
                dve.wait_ge(r_mm, i * G + G)
                dve.wait_ge(res_in, i * 16 + 16)
                dve.wait_ge(stored, i * 16 + 16)
                V.tensor_tensor(new[:], res[:], r_ps[:, :, 0:D], ALU.add).then_inc(new_ok, 1)
            turns(dve, TURNS, turn)

        @block.scalar
        def _(act):
            A = nc.scalar
            act.wait_ge(zeroed, 2)
            act.sem_inc(stored, 16)

            def turn(i, more):
                act.wait_ge(sT_mm, i + 1)
                A.activation(sT[0:64, 0, :], sT_ps[0:64, :], ACT.Copy).then_inc(sT_ok, 1)
                A.activation(sT[64:128, 1, :], sT_ps[64:128, :], ACT.Copy).then_inc(sT_ok, 1)
                for e in range(8):
                    act.wait_ge(ev_mm, i * 8 + (e + 1))
                    A.activation(qs[:, e, :] if e < 4 else es[:, e - 4, 0:H * 64], ev_ps[:, e % 2, :], ACT.Copy).then_inc(ev_ok, 1)
                act.wait_ge(new_ok, i + 2)
                act.dma_start(ho[:, bass.ds(i * G, G), :], new[:]).then_inc(stored, 16)
            turns(act, TURNS, turn)
            act.wait_ge(stored, TURNS * 16 + 16)

        @block.tensor
        def _(pe):
            M = nc.tensor.matmul
            pe.wait_ge(w_in, 32)
            pe.wait_ge(const, 2)
            pe.wait_ge(zeroed, 2)

            def turn(i, more):
                ln.ready(pe, i)
                for b in range(G):
                    mm = nc.tensor.transpose(sT_ps[:, b * 128:(b + 1) * 128], ln.out[:, b].rearrange("p c n -> p (c n)"), ident[:])
                mm.then_inc(sT_mm, 1)
                pe.wait_ge(sT_ok, i * 2 + 2)
                for e in range(8):
                    if e >= 2:
                        pe.wait_ge(ev_ok, i * 8 + (e - 1))
                    if e < 4:
                        mm = M(ev_ps[:, e % 2, :], w_q[:, e * 128:(e + 1) * 128], sT[:, 0, :], start=True, stop=True)
                    else:
                        b = e - 4
                        mm = M(ev_ps[:, e % 2, :], sT[:, 0, b * 128:(b + 1) * 128], w_e[:], start=True, stop=True)
                    mm.then_inc(ev_mm, 1)
                pe.wait_ge(ev_ok, i * 8 + 8)

                def omega(b):
                    if b >= 2:
                        pe.wait_ge(om_ok, i * G + (b - 1))
                    s = slice(b * 128, (b + 1) * 128)
                    for u in range(2):
                        mm = M(om_ps[:, b % 2, u, :], sT[:, u, s], qs[:, :, s], start=True, stop=True)
                    mm.then_inc(om_mm, 1)

                def retrieve(b):
                    pe.wait_ge(om_ok, i * G + (b + 1))
                    if b == 0:
                        pe.wait_ge(new_ok, i + 1)
                    for u in range(2):
                        for hp in range(4):
                            h = 2 * hp + u
                            mm = M(r_ps[:, b, :], om[:, b % 2, u, hp * 128:(hp + 1) * 128], es[:, b, h * 64:(h + 2) * 64],
                                   start=(u == 0 and hp == 0), stop=(u == 1 and hp == 3))
                    mm.then_inc(r_mm, 1)
                omega(0)
                omega(1)
                retrieve(0)
                omega(2)
                retrieve(1)
                omega(3)
                retrieve(2)
                retrieve(3)
            turns(pe, TURNS, turn)


def lay_linear_attention(inp):
    Q, E = np.asarray(inp["L0_attn_Q"]), np.asarray(inp["L0_attn_E"])
    pad = lambda a: np.concatenate([a.reshape(64, 512), np.zeros((64, 512), np.float32)])
    return dict(la_wq=pad(np.transpose(Q, (1, 0, 2))), la_we=pad(np.transpose(E, (2, 0, 1))))


class Gate:
    STEPS = 12

    def __init__(self, nc, sb, sem, G, W):
        self.nc, self.G, self.W = nc, G, W
        self.logits = sb("gt_logits", [128, G, W]); self.top = sb("gt_top", [128, G, 8]); self.at = sb("gt_at", [128, G, 8], U32)
        self.atf = sb("gt_atf", [128, G, 2]); self.w = sb("gt_w", [128, G, 2]); self.e = sb("gt_e", [128, G]); self.pad = sb("gt_pad", [128, 1])
        self.iota = sb("gt_iota", [128, W]); self.one = sb("gt_one", [128, G, W]); self.gates = sb("gt_gates", [128, G, W])
        self.step, self.exp_ok, self.iota_ok = sem("gt_step"), sem("gt_exp"), sem("gt_iota")

    def start(self):
        self.nc.gpsimd.iota(self.iota[:], pattern=[[1, self.W]], base=0, channel_multiplier=0,
                            allow_small_or_imprecise_dtypes=True).then_inc(self.iota_ok, 1)

    def first(self, dve, turn):
        V, G = self.nc.vector, self.G
        base = turn * self.STEPS
        V.memset(self.pad[:], 0.0)
        for g in range(G):
            ins = V.max(self.top[:, g, :], self.logits[:, g, :])
        ins.then_inc(self.step, 1)
        dve.wait_ge(self.step, base + 1)
        V.memset(self.pad[:], 0.0)
        for g in range(G):
            ins = V.max_index(self.at[:, g, :], self.top[:, g, :], self.logits[:, g, :])
        ins.then_inc(self.step, 1)
        V.tensor_tensor(self.e[:], self.top[:, :, 1], self.top[:, :, 0], ALU.subtract).then_inc(self.step, 1)
        dve.wait_ge(self.step, base + 3)
        V.tensor_copy(self.atf[:], self.at[:, :, 0:2]).then_inc(self.step, 1)

    def scalar(self, act, turn):
        act.wait_ge(self.step, turn * self.STEPS + 3)
        self.nc.scalar.activation(self.e[:], self.e[:], ACT.Exp).then_inc(self.exp_ok, 1)

    def second(self, dve, turn):
        V, G, W = self.nc.vector, self.G, self.W
        base, n = turn * self.STEPS, 4

        def did(ins):
            nonlocal n
            n += 1
            ins.then_inc(self.step, 1)
            dve.wait_ge(self.step, base + n)
        dve.wait_ge(self.exp_ok, turn + 1)
        did(V.tensor_scalar(self.w[:, :, 0], self.e[:], 1.0, None, ALU.add))
        did(V.reciprocal(self.w[:, :, 0], self.w[:, :, 0]))
        did(V.tensor_tensor(self.w[:, :, 1], self.w[:, :, 0], self.e[:], ALU.mult))
        wide = [128, G, W]
        iota = self.iota[:].rearrange("p (o w) -> p o w", o=1).to_broadcast(wide)
        did(V.tensor_tensor(self.gates[:], iota, self.atf[:, :, 0:1].to_broadcast(wide), ALU.is_equal))
        did(V.tensor_tensor(self.gates[:], self.gates[:], self.w[:, :, 0:1].to_broadcast(wide), ALU.mult))
        did(V.tensor_tensor(self.one[:], iota, self.atf[:, :, 1:2].to_broadcast(wide), ALU.is_equal))
        did(V.tensor_tensor(self.one[:], self.one[:], self.w[:, :, 1:2].to_broadcast(wide), ALU.mult))
        V.tensor_tensor(self.gates[:], self.gates[:], self.one[:], ALU.add).then_inc(self.step, 1)
        n += 1
        assert n == self.STEPS

    def ready(self, eng, turn):
        eng.wait_ge(self.step, turn * self.STEPS + self.STEPS)


def experts16(nc, h_in, wg, gb, w1, b1, w2, b2, post, h_out):
    B, T, _ = h_in.shape
    G, E = 4, 16
    TURNS = B // G
    with ExitStack() as ctx:
        sb = lambda n, s, d=F32: ctx.enter_context(nc.sbuf_tensor("mos_" + n, s, d))
        pb = lambda n, s, d=F32: ctx.enter_context(nc.psum_tensor("mop_" + n, s, d))
        sem = ctx.enter_context(semaphores(nc, "mom_"))
        ln = LayerNorm(nc, sb, sem, G, copies=2)
        ln2 = LayerNorm(nc, sb, sem, G, name="ln2")
        gt = Gate(nc, sb, sem, G, E)
        wg_s = sb("wg", [128, E]); gb_s = sb("gb", [128, E]); w1_s = sb("w1", [128, E * 128]); b1_s = sb("b1", [128, E])
        w2_s = sb("w2", [128, E * D + D]); b2_s = sb("b2", [64, G * D]); post_s = sb("post", [128, 2, D])
        ident = sb("ident", [128, 128])
        res = sb("res", [128, G, D]); new = sb("new", [128, G, D])
        sT = sb("sT", [128, G * 128]); hid = sb("hid", [128, 2, G * 128]); part = sb("part", [128, 2, G, D])
        gT = sb("gT", [64, 128])
        acc = ln2.x
        sT_ps = pb("sT", [128, 512]); g_ps = pb("g", [128, 512]); hid_ps = pb("hid", [128, 3, 512]); y_ps = pb("y", [128, 3, G, 2 * D])
        w_in = sem("w_in"); const = sem("const"); w2_pad = sem("w2_pad"); res_in = sem("res_in"); stored = sem("stored")
        sT_mm = sem("sT_mm"); sT_ok = sem("sT_ok"); lg_mm = sem("lg_mm"); lg_ok = sem("lg_ok")
        hid_mm = sem("hid_mm"); hid_ok = sem("hid_ok"); y_mm = sem("y_mm"); part_ok = sem("part_ok"); acc_ok = sem("acc_ok")
        gT_mm = sem("gT_mm"); gT_ok = sem("gT_ok"); b2_mm = sem("b2_mm"); fin = sem("fin"); parts_done = sem("parts_done"); new_st = sem("new_st"); new_ok = sem("new_ok")
        hi = h_in.rearrange("b t n -> t b n"); ho = h_out.rearrange("b t n -> t b n")
        loads = [(wg_s[:], wg), (gb_s[:], gb), (w1_s[:], w1), (b1_s[:], b1), (w2_s[:, 0:E * D], w2), (b2_s[:], b2), (post_s[:], post)]
        NB = E + 1
        block = ctx.enter_context(nc.Block())

        @block.sync
        def _(sp):
            for dst, src in loads:
                sp.dma_start(dst, src).then_inc(w_in, 16)
            sp.wait_ge(ln.step, 1)
            sp.dma_start(ln.x[:], hi[:, 0:G, :]).then_inc(ln.loaded, 16)

            def turn(i, more):
                sp.wait_ge(new_ok, i + 1)
                sp.dma_start(res[:], hi[:, bass.ds(i * G, G), :]).then_inc(res_in, 16)
                if more:
                    ln.load(sp, i + 1, hi[:, bass.ds(i * G + G, G), :])
            turns(sp, TURNS, turn)

        @block.gpsimd
        def _(pool):
            make_identity(nc, pool, ident, const)
            gt.start()
            ln.gpsimd(pool, 0)
            pool.sem_inc(acc_ok, 1)

            def turn(i, more):
                for e in range(NB):
                    pool.wait_ge(part_ok, i * NB + (e + 1))
                    if e == 0:
                        pool.wait_ge(fin, i + 1)
                        first = ln.out[:, :, 0, :]
                    else:
                        pool.wait_ge(acc_ok, i * NB + (e + 1))
                        first = acc[:]
                    nc.gpsimd.tensor_tensor(acc[:], first, part[:, e % 2], ALU.add).then_inc(acc_ok, 1)
                    if e == 1 and more:
                        ln.gpsimd(pool, i + 1)
                ln2.gpsimd(pool, i)
            turns(pool, TURNS, turn)

        @block.vector
        def _(dve):
            V = nc.vector
            ln.start()
            ln2.start()
            V.memset(w2_s[:, E * D:], 0.0).then_inc(w2_pad, 1)
            dve.sem_inc(new_ok, 1)
            dve.sem_inc(fin, 1)
            dve.sem_inc(parts_done, 1)
            ln.vector(dve, 0)
            dve.wait_ge(w_in, 16 * len(loads))
            dve.wait_ge(gt.iota_ok, 1)

            def turn(i, more):
                dve.wait_ge(lg_mm, i + 1)
                V.tensor_tensor(gt.logits[:], g_ps[:, 0:G * E].rearrange("p (g e) -> p g e", e=E),
                                gb_s[:].rearrange("p (o e) -> p o e", o=1).to_broadcast([128, G, E]), ALU.add).then_inc(lg_ok, 1)
                dve.wait_ge(lg_ok, i + 1)
                gt.first(dve, i)
                gt.second(dve, i)
                gt.ready(dve, i)
                for e in range(NB):
                    dve.wait_ge(acc_ok, i * NB + max(e, 1))
                    if e < E:
                        dve.wait_ge(y_mm, i * E + (e + 1))
                        V.tensor_tensor(part[:, e % 2], y_ps[:, e % 3, :, 0:D], gt.gates[:, :, e:e + 1].to_broadcast([128, G, D]),
                                        ALU.mult).then_inc(part_ok, 1)
                    else:
                        dve.wait_ge(b2_mm, i + 1)
                        V.tensor_copy(part[:, e % 2], g_ps[:, 256:512].rearrange("p (g n) -> p g n", n=D)).then_inc(part_ok, 1)
                    if e == 3 and more:
                        ln.vector(dve, i + 1)
                dve.wait_ge(part_ok, i * NB + NB)
                dve.sem_inc(parts_done, 1)
                dve.wait_ge(acc_ok, i * NB + NB + 1)
                ln2.vector(dve, i, loaded=False)
                ln2.ready(dve, i)
                y2 = ln2.out[:, :, 0, :]
                pr = lambda k: post_s[:, k:k + 1, :].to_broadcast([128, G, D])
                V.tensor_tensor(y2, y2, pr(0), ALU.mult).then_inc(fin, 1)
                dve.wait_ge(fin, i + 2)
                V.tensor_tensor(y2, y2, pr(1), ALU.add).then_inc(new_st, 1)
                dve.wait_ge(new_st, i + 1)
                dve.wait_ge(res_in, i * 16 + 16)
                dve.wait_ge(stored, i * 16 + 16)
                V.tensor_tensor(new[:], y2, res[:], ALU.add).then_inc(new_ok, 1)
            turns(dve, TURNS, turn)

        @block.scalar
        def _(act):
            A = nc.scalar
            act.sem_inc(stored, 16)
            act.wait_ge(w_in, 16 * len(loads))

            def turn(i, more):
                act.wait_ge(sT_mm, i + 1)
                A.activation(sT[:], sT_ps[:], ACT.Copy).then_inc(sT_ok, 1)
                gt.scalar(act, i)
                for e in range(E):
                    act.wait_ge(hid_mm, i * E + (e + 1))
                    if e >= 2:
                        act.wait_ge(y_mm, i * E + (e - 1))
                    A.activation(hid[:, e % 2, :], hid_ps[:, e % 3, :], ACT.Relu, bias=b1_s[:, e:e + 1]).then_inc(hid_ok, 1)
                    if e == 4:
                        act.wait_ge(gT_mm, i + 1)
                        A.activation(gT[:], g_ps[0:64, 64:192], ACT.Copy).then_inc(gT_ok, 1)
                act.wait_ge(new_ok, i + 2)
                act.dma_start(ho[:, bass.ds(i * G, G), :], new[:]).then_inc(stored, 16)
            turns(act, TURNS, turn)
            act.wait_ge(stored, TURNS * 16 + 16)

        @block.tensor
        def _(pe):
            M = nc.tensor.matmul
            pe.wait_ge(w_in, 16 * len(loads))
            pe.wait_ge(const, 2)
            pe.wait_ge(w2_pad, 1)

            def turn(i, more):
                ln.ready(pe, i)
                for b in range(G):
                    mm = nc.tensor.transpose(sT_ps[:, b * 128:(b + 1) * 128], ln.out[:, b].rearrange("p c n -> p (c n)"), ident[:])
                mm.then_inc(sT_mm, 1)
                pe.wait_ge(sT_ok, i + 1)
                pe.wait_ge(parts_done, i + 1)
                for b in range(G):
                    mm = M(g_ps[:, b * E:(b + 1) * E], sT[:, b * 128:(b + 1) * 128], wg_s[:], start=True, stop=True)
                mm.then_inc(lg_mm, 1)

                def hidden(e):
                    if e >= 3:
                        pe.wait_ge(hid_ok, i * E + (e - 2))
                    M(hid_ps[:, e % 3, :], w1_s[:, e * 128:(e + 1) * 128], sT[:], start=True, stop=True).then_inc(hid_mm, 1)

                def output(e):
                    pe.wait_ge(hid_ok, i * E + (e + 1))
                    if e >= 3:
                        pe.wait_ge(part_ok, i * NB + (e - 2))
                    for b in range(G):
                        mm = M(y_ps[:, e % 3, b, :], hid[:, e % 2, b * 128:(b + 1) * 128], w2_s[:, e * D:(e + 2) * D], start=True, stop=True)
                    mm.then_inc(y_mm, 1)
                hidden(0)
                hidden(1)
                for e in range(E):
                    if e == 3:
                        gt.ready(pe, i)
                    output(e)
                    if e + 2 < E:
                        hidden(e + 2)
                    if e == 3:
                        nc.tensor.transpose(g_ps[0:64, 64:192], gt.gates[:].rearrange("p g e -> p (g e)"), ident[:]).then_inc(gT_mm, 1)
                    if e == 6:
                        pe.wait_ge(gT_ok, i + 1)
                        M(g_ps[:, 256:512], gT[:], b2_s[:], start=True, stop=True).then_inc(b2_mm, 1)
            turns(pe, TURNS, turn)


def lay_experts16(inp):
    g = lambda n: np.asarray(inp["L0_ffn_" + n])
    E, H, F = g("w1").shape
    z = np.zeros((64, E * F), np.float32)
    w1 = np.concatenate([np.transpose(g("w1"), (1, 0, 2)).reshape(H, E * F), z])
    b2 = np.zeros((64, 256), np.float32)
    for b in range(4):
        b2[16 * b:16 * b + 16, 64 * b:64 * b + 64] = g("b2")
    return dict(mo_wg=np.concatenate([g("gate_w"), np.zeros((64, E), np.float32)]), mo_gb=np.broadcast_to(g("gate_b"), (128, E)),
                mo_w1=w1, mo_b1=g("b1").T, mo_w2=np.transpose(g("w2"), (1, 0, 2)).reshape(F, E * H), mo_b2=b2,
                mo_post=np.broadcast_to(np.stack([g("gamma"), g("beta")]), (128, 2, 64)))


RMS_EPS = 1.1920929e-07
MASKED = -1e30


def rope_attention(nc, h_in, wq, wk, wv, wo, norms, cs_head, cs_tok, h_out):
    B, T, _ = h_in.shape
    G, H, U = 4, 16, 8
    TURNS = B // G
    with ExitStack() as ctx:
        sb = lambda n, s, d=F32: ctx.enter_context(nc.sbuf_tensor("ras_" + n, s, d))
        pb = lambda n, s, d=F32: ctx.enter_context(nc.psum_tensor("rap_" + n, s, d))
        sem = ctx.enter_context(semaphores(nc, "ram_"))
        ln = LayerNorm(nc, sb, sem, G, copies=2)
        wq_s = sb("wq", [128, H * 64]); wk_s = sb("wk", [128, 64]); wv_s = sb("wv", [64, 128]); wo_s = sb("wo", [64, H * 64])
        wvo = sb("wvo", [128, H * 64]); nrm = sb("nrm", [128, 2, 64]); csh = sb("csh", [128, 2, 128]); cst = sb("cst", [128, 2, 64])
        ident = sb("ident", [128, 128]); identb = sb("identb", [128, 128], BF16); mask = sb("mask", [128, 512], BF16)
        sel = sb("sel", [128, 8, 16])
        res = sb("res", [128, G, D]); new = sb("new", [128, G, D])
        sT = sb("sT", [128, 512])
        sq = sb("sq", [128, 2, 512]); raw = sb("raw", [128, 2, 512]); sh = sb("sh", [128, 2, 512]); t1 = sb("t1", [128, 2, 512]); qr = sb("qr", [128, 8, 512])
        ssq = sb("ssq", [16, 512]); rq = sb("rq", [128, G, H])
        kc = sb("kc", [128, G, 64]); ks = sb("ks", [128, G, 64]); kr = sb("kr", [128, G, 64]); kv = sb("kv", [128, G]); kh = sb("kh", [128, G])
        kn = sb("kn", [128, G, 2, 64]); kz = sb("kz", [128, G, 2, 128])
        vwo = sb("vwo", [128, G, H * 64 + 64])
        m8 = sb("m8", [128, 2, 8]); nm = sb("nm", [128, 2, 8]); sm = sb("sm", [128, 2, 8]); rs = sb("rs", [128, 2, 8])
        p = sb("p", [128, 2, 8, 128]); pn = sb("pn", [128, 2, 8, 128]); pT = sb("pT", [128, 2, 8, 128])
        sc_ps = pb("sc", [128, 2, 2, 512]); pT_ps = pb("pT", [128, 2, 512]); y_ps = pb("y", [128, G, 2 * D]); misc = pb("misc", [128, 512])
        pj_ps, ss_ps = pT_ps, y_ps
        rqT_v = y_ps[:].rearrange("p g n -> p (g n)")
        ss_v = y_ps[0:16].rearrange("p g n -> p (g n)")

        w_in = sem("w_in"); const = sem("const"); mk = sem("mk"); sel_ok = sem("sel_ok"); pad_ok = sem("pad_ok"); wvo_mm = sem("wvo_mm"); wvo_ok = sem("wvo_ok")
        res_in = sem("res_in"); stored = sem("stored"); new_ok = sem("new_ok")
        sT_mm = sem("sT_mm"); sT_ok = sem("sT_ok"); k_mm = sem("k_mm"); pj_mm = sem("pj_mm"); sq_ok = sem("sq_ok")
        rot = sem("rot"); raw_ok = sem("raw_ok"); swapped = sem("swapped"); t1_ok = sem("t1_ok"); qr_ok = sem("qr_ok"); ss_mm = sem("ss_mm"); ss_ok = sem("ss_ok")
        rqT_mm = sem("rqT_mm"); rq_st = sem("rq_st"); rq_ok = sem("rq_ok"); k_st = sem("k_st"); k_pow = sem("k_pow"); kT_mm = sem("kT_mm"); kz_ok = sem("kz_ok")
        vw_mm = sem("vw_mm"); vw_ok = sem("vw_ok")
        sc_mm = sem("sc_mm"); mx_st = sem("mx_st"); exp_ok = sem("exp_ok"); rec_ok = sem("rec_ok"); pn_ok = sem("pn_ok")
        pT_mm = sem("pT_mm"); pT_a = sem("pT_a"); pT_v = sem("pT_v"); pv_mm = sem("pv_mm")
        hi = h_in.rearrange("b t n -> t b n"); ho = h_out.rearrange("b t n -> t b n")
        loads = [(wq_s, wq), (wk_s, wk), (wv_s, wv), (wo_s, wo), (nrm, norms), (csh, cs_head), (cst, cs_tok)]
        KST = 9
        swap = [x ^ 1 for x in range(32)]
        four = lambda ap: ap.rearrange("p (g t) -> p g t", g=G)
        over = lambda ap, shape: ap.rearrange("p (o t) -> p o t", o=1).to_broadcast(shape)
        block = ctx.enter_context(nc.Block())

        @block.sync
        def _(sp):
            for dst, src in loads:
                sp.dma_start(dst[:], src).then_inc(w_in, 16)
            sp.wait_ge(ln.step, 1)
            sp.dma_start(ln.x[:], hi[:, 0:G, :]).then_inc(ln.loaded, 16)

            def turn(i, more):
                sp.wait_ge(new_ok, i + 1)
                sp.dma_start(res[:], hi[:, bass.ds(i * G, G), :]).then_inc(res_in, 16)
                if more:
                    ln.load(sp, i + 1, hi[:, bass.ds(i * G + G, G), :])
            turns(sp, TURNS, turn)

        @block.gpsimd
        def _(pool):
            P = nc.gpsimd
            make_identity(nc, pool, ident, const)
            P.memset(identb[:], 0.0).then_inc(mk, 1)
            P.memset(mask[:], 0.0).then_inc(mk, 1)
            pool.wait_ge(mk, 2)
            P.affine_select(out=identb[:], in_=identb[:], compare_op=ALU.not_equal, fill=1.0, base=0,
                            pattern=[[-1, 128]], channel_multiplier=1).then_inc(mk, 1)
            P.affine_select(out=mask[:].rearrange("p (g t) -> p g t", g=4), in_=mask[:].rearrange("p (g t) -> p g t", g=4),
                            compare_op=ALU.is_ge, fill=MASKED, base=0, pattern=[[0, 4], [-1, 128]], channel_multiplier=1).then_inc(mk, 1)
            pool.wait_ge(w_in, 16 * len(loads))
            ln.gpsimd(pool, 0)

            def turn(i, more):
                for blk in range(8):
                    s = blk % 2
                    pool.wait_ge(swapped, i * 8 + (blk + 1))
                    P.tensor_tensor(four(sh[:, s, :]), four(sh[:, s, :]), over(csh[:, 1, :], [128, G, 128]), ALU.mult).then_inc(rot, 1)
                    pool.wait_ge(rot, i * 8 + (blk + 1))
                    pool.wait_ge(t1_ok, i * 8 + (blk + 1))
                    P.tensor_tensor(qr[:, blk, :], sh[:, s, :], t1[:, s, :], ALU.add).then_inc(qr_ok, 1)
                pool.wait_ge(k_st, i * KST + 7)
                P.tensor_tensor(kv[:], kv[:], kh[:], ALU.pow).then_inc(k_pow, 1)
                if more:
                    ln.gpsimd(pool, i + 1)
                for n in range(U):
                    s = n % 2
                    pool.wait_ge(rec_ok, i * U + (n + 1))
                    if n >= 2:
                        pool.wait_ge(pT_mm, i * U + (n - 1))
                    P.tensor_tensor(pn[:, s], p[:, s], bc(rs[:, s, :], [128, 8, 128]), ALU.mult).then_inc(pn_ok, 1)
            turns(pool, TURNS, turn)

        @block.vector
        def _(dve):
            V = nc.vector
            ln.start()
            V.memset(sel[:], 0.0).then_inc(sel_ok, 1)
            V.memset(kh[:], -0.5).then_inc(sel_ok, 1)
            dve.wait_ge(sel_ok, 2)
            for u in range(2):
                for blk in range(8):
                    ins = V.memset(sel[64 * u:64 * u + 64, blk, 2 * blk + u:2 * blk + u + 1], 1.0)
            ins.then_inc(sel_ok, 1)
            V.memset(kz[:], 0.0).then_inc(pad_ok, 1)
            V.memset(vwo[:, :, H * 64:], 0.0).then_inc(pad_ok, 1)
            V.memset(wvo[:], 0.0).then_inc(pad_ok, 1)
            dve.wait_ge(w_in, 16 * len(loads))
            V.scalar_tensor_tensor(nrm[:, 0, :], nrm[:, 0, :], 0.125, nrm[:, 1, :], ALU.mult, ALU.mult).then_inc(pad_ok, 1)
            dve.sem_inc(new_ok, 1)
            ln.vector(dve, 0)
            dve.wait_ge(pad_ok, 4)

            def turn(i, more):
                for blk in range(8):
                    s = blk % 2
                    dve.wait_ge(raw_ok, i * 8 + (blk + 1))
                    if blk >= 2:
                        dve.wait_ge(qr_ok, i * 8 + (blk - 1))
                    V.tensor_tensor(four(t1[:, s, :]), four(raw[:, s, :]), over(csh[:, 0, :], [128, G, 128]), ALU.mult).then_inc(t1_ok, 1)
                    V.stream_shuffle(sh[:, s, :], raw[:, s, :], swap).then_inc(swapped, 1)
                st = Steps(k_st, KST, i)
                dve.wait_ge(k_mm, i + 1)
                kp = misc[:, 0:256].rearrange("p (g n) -> p g n", n=64)
                st.did(V.tensor_tensor(kc[:], kp, over(cst[:, 0, :], [128, G, 64]), ALU.mult))
                st.chain(dve, V.tensor_tensor(ks[:], kp, over(cst[:, 1, :], [128, G, 64]), ALU.mult))
                pair = lambda t, o: t[:, :, o:64:2]
                st.did(V.tensor_tensor(pair(kr, 0), pair(kc, 0), pair(ks, 1), ALU.subtract))
                st.chain(dve, V.tensor_tensor(pair(kr, 1), pair(ks, 0), pair(kc, 1), ALU.add))
                st.chain(dve, V.tensor_tensor(kc[:], kr[:], kr[:], ALU.mult))
                st.chain(dve, V.tensor_reduce(kv[:], kc[:], AX, ALU.add))
                st.did(V.tensor_scalar(kv[:], kv[:], 1.0 / 64, RMS_EPS, ALU.mult, ALU.add))
                dve.wait_ge(rqT_mm, i + 1)
                rqv = rq[:].rearrange("p g h -> p (g h)")
                V.tensor_scalar(rqv, rqT_v[:, 0:64], 1.0 / 64, RMS_EPS, ALU.mult, ALU.add).then_inc(rq_st, 1)
                dve.wait_ge(rq_st, i * 2 + 1)
                V.reciprocal(rqv, rqv).then_inc(rq_st, 1)
                dve.wait_ge(k_pow, i + 1)
                st.chain(dve, V.tensor_tensor(kr[:], kr[:], bc(kv[:], [128, G, 64]), ALU.mult))
                V.tensor_tensor(kn[:, :, 0, :], kr[:], over(nrm[:, 0, :], [128, G, 64]), ALU.mult)
                st.did(V.tensor_tensor(kn[:, :, 1, :], kr[:], over(nrm[:, 0, :], [128, G, 64]), ALU.mult))
                st.close()
                if more:
                    dve.wait_ge(sT_mm, i + 1)
                    ln.vector(dve, i + 1)
                for n in range(U + 1):
                    s = n % 2
                    if n < U:
                        dve.wait_ge(sc_mm, i * U + (n + 1))
                        V.tensor_reduce(m8[:, s, :], sc_ps[:, s].rearrange("p k (h t) -> p (k h) t", t=128), AX, ALU.max).then_inc(mx_st, 1)
                        dve.wait_ge(mx_st, i * 2 * U + (2 * n + 1))
                        if n == 0:
                            dve.wait_ge(rq_ok, i + 1)
                        b, g2 = n // 2, n % 2
                        V.scalar_tensor_tensor(nm[:, s, :], m8[:, s, :], -1.0, rq[:, b, 8 * g2:8 * g2 + 8], ALU.mult, ALU.mult).then_inc(mx_st, 1)
                    if n >= 1:
                        m, s = n - 1, (n - 1) % 2
                        dve.wait_ge(exp_ok, i * 8 * U + 8 * (m + 1))
                        V.reciprocal(rs[:, s, :], sm[:, s, :]).then_inc(rec_ok, 1)
                        dve.wait_ge(pT_mm, i * U + (m + 1))
                        if m >= 2:
                            dve.wait_ge(pv_mm, i * U + (m - 1))
                        V.tensor_copy(pT[:, s, 4:8, :], pT_ps[:, 1, :].rearrange("p (h t) -> p h t", t=128)).then_inc(pT_v, 1)
                dve.wait_ge(pv_mm, i * U + U)
                dve.wait_ge(res_in, i * 16 + 16)
                dve.wait_ge(stored, i * 16 + 16)
                V.tensor_tensor(new[:], res[:], y_ps[:, :, 0:D], ALU.add).then_inc(new_ok, 1)
            turns(dve, TURNS, turn)

        @block.scalar
        def _(act):
            A = nc.scalar
            act.sem_inc(stored, 16)
            act.wait_ge(wvo_mm, 2)
            act.wait_ge(pad_ok, 4)
            for c in range(2):
                A.activation(wvo[0:64, c * 512:(c + 1) * 512], pj_ps[0:64, c, :], ACT.Copy).then_inc(wvo_ok, 1)

            def turn(i, more):
                act.wait_ge(sT_mm, i + 1)
                A.activation(sT[:], misc[:], ACT.Copy).then_inc(sT_ok, 1)
                for blk in range(8):
                    s = blk % 2
                    act.wait_ge(pj_mm, i * 8 + (blk + 1))
                    if blk >= 2:
                        act.wait_ge(ss_mm, i * 8 + (blk - 1))
                        act.wait_ge(swapped, i * 8 + (blk - 1))
                    A.activation(raw[:, s, :], pj_ps[:, s, :], ACT.Copy).then_inc(raw_ok, 1)
                    A.activation(sq[:, s, :], pj_ps[:, s, :], ACT.Square).then_inc(sq_ok, 1)
                act.wait_ge(ss_mm, i * 8 + 8)
                A.activation(ssq[:], ss_v, ACT.Copy).then_inc(ss_ok, 1)
                for c in range(8):
                    act.wait_ge(vw_mm, i * 8 + (c + 1))
                    A.activation(vwo[:, c // 2, (c % 2) * 512:(c % 2 + 1) * 512], pj_ps[:, c % 2, :], ACT.Copy).then_inc(vw_ok, 1)
                act.wait_ge(rq_st, i * 2 + 2)
                rqv = rq[:].rearrange("p g h -> p (g h)")
                A.activation(rqv, rqv, ACT.Sqrt).then_inc(rq_ok, 1)
                act.wait_ge(kT_mm, i + 1)
                for u in range(2):
                    A.activation(kz[64 * u:64 * u + 64, :, u, :], misc[64 * u:64 * u + 64, :].rearrange("p (g s) -> p g s", g=G), ACT.Copy).then_inc(kz_ok, 1)
                for n in range(U + 1):
                    if n < U:
                        s, b, g2 = n % 2, n // 2, n % 2
                        act.wait_ge(mx_st, i * 2 * U + (2 * n + 2))
                        if n >= 2:
                            act.wait_ge(pn_ok, i * U + (n - 1))
                        for h in range(8):
                            A.activation(p[:, s, h, :], sc_ps[:, s, h // 4, (h % 4) * 128:(h % 4 + 1) * 128], ACT.Exp,
                                         bias=nm[:, s, h:h + 1], scale=rq[:, b, 8 * g2 + h:8 * g2 + h + 1],
                                         accum_out=sm[:, s, h:h + 1]).then_inc(exp_ok, 1)
                    if n >= 1:
                        m, s = n - 1, (n - 1) % 2
                        act.wait_ge(pT_mm, i * U + (m + 1))
                        if m >= 2:
                            act.wait_ge(pv_mm, i * U + (m - 1))
                        A.activation(pT[:, s, 0:4, :], pT_ps[:, 0, :].rearrange("p (h t) -> p h t", t=128), ACT.Copy).then_inc(pT_a, 1)
                act.wait_ge(new_ok, i + 2)
                act.dma_start(ho[:, bass.ds(i * G, G), :], new[:]).then_inc(stored, 16)
            turns(act, TURNS, turn)
            act.wait_ge(stored, TURNS * 16 + 16)

        @block.tensor
        def _(pe):
            M, X = nc.tensor.matmul, nc.tensor.transpose
            pe.wait_ge(w_in, 16 * len(loads))
            pe.wait_ge(const, 2)
            pe.wait_ge(mk, 4)
            pe.wait_ge(sel_ok, 3)
            pe.wait_ge(pad_ok, 4)
            for c in range(2):
                M(pj_ps[:, c, :], wv_s[:], wo_s[:, c * 512:(c + 1) * 512], start=True, stop=True).then_inc(wvo_mm, 1)
            pe.wait_ge(wvo_ok, 2)

            def turn(i, more):
                ln.ready(pe, i)
                pe.wait_ge(new_ok, i + 1)
                for b in range(G):
                    mm = X(misc[:, b * 128:(b + 1) * 128], ln.out[:, b].rearrange("p c n -> p (c n)"), ident[:])
                mm.then_inc(sT_mm, 1)
                pe.wait_ge(sT_ok, i + 1)
                for b in range(G):
                    mm = M(misc[:, b * 64:(b + 1) * 64], sT[:, b * 128:(b + 1) * 128], wk_s[:], start=True, stop=True)
                mm.then_inc(k_mm, 1)

                def proj(blk):
                    if blk >= 2:
                        pe.wait_ge(sq_ok, i * 8 + (blk - 1))
                    M(pj_ps[:, blk % 2, :], wq_s[:, blk * 128:(blk + 1) * 128], sT[:], start=True, stop=True).then_inc(pj_mm, 1)

                def sumsq(blk):
                    pe.wait_ge(sq_ok, i * 8 + (blk + 1))
                    M(ss_v, sel[:, blk, :], sq[:, blk % 2, :], start=(blk == 0), stop=(blk == 7)).then_inc(ss_mm, 1)
                proj(0)
                proj(1)
                for blk in range(8):
                    sumsq(blk)
                    if blk + 2 < 8:
                        proj(blk + 2)
                for c in range(8):
                    if c < 2:
                        pe.wait_ge(sq_ok, i * 8 + (7 + c))
                    else:
                        pe.wait_ge(vw_ok, i * 8 + (c - 1))
                    b = c // 2
                    if c == 1:
                        pe.wait_ge(ss_ok, i + 1)
                    M(pj_ps[:, c % 2, :], sT[:, b * 128:(b + 1) * 128], wvo[:, (c % 2) * 512:(c % 2 + 1) * 512], start=True, stop=True).then_inc(vw_mm, 1)
                    if c == 1:
                        for b in range(G):
                            mm = X(rqT_v[:, b * 16:(b + 1) * 16], ssq[:, b * 128:(b + 1) * 128], ident[0:16, 0:16])
                        mm.then_inc(rqT_mm, 1)
                pe.wait_ge(k_st, i * KST + KST)
                pe.wait_ge(rq_st, i * 2 + 1)
                for b in range(G):
                    mm = X(misc[:, b * 128:(b + 1) * 128], kn[:, b].rearrange("p c n -> p (c n)"), ident[:])
                mm.then_inc(kT_mm, 1)
                pe.wait_ge(kz_ok, i * 2 + 2)
                pe.wait_ge(qr_ok, i * 8 + 8)
                pe.wait_ge(vw_ok, i * 8 + 8)

                def scores(n):
                    s, b, g2 = n % 2, n // 2, n % 2
                    if n >= 2:
                        pe.wait_ge(exp_ok, i * 8 * U + 8 * (n - 1))
                    for k in range(2):
                        M(sc_ps[:, s, k, :], identb[:], mask[:], start=True, stop=False)
                    for j in range(4):
                        mm = M(sc_ps[:, s, j // 2, (j % 2) * 256:(j % 2 + 1) * 256], qr[:, 4 * g2 + j, b * 128:(b + 1) * 128],
                               kz[:, b].rearrange("p u s -> p (u s)"), start=False, stop=(j % 2 == 1))
                    mm.then_inc(sc_mm, 1)

                def attend(n):
                    s, b, g2 = n % 2, n // 2, n % 2
                    pe.wait_ge(pn_ok, i * U + (n + 1))
                    if n >= 1:
                        pe.wait_ge(pT_a, i * U + n)
                        pe.wait_ge(pT_v, i * U + n)
                    for h in range(8):
                        mm = X(pT_ps[:, h // 4, (h % 4) * 128:(h % 4 + 1) * 128], pn[:, s, h, :], ident[:])
                    mm.then_inc(pT_mm, 1)
                    pe.wait_ge(pT_a, i * U + (n + 1))
                    pe.wait_ge(pT_v, i * U + (n + 1))
                    for h in range(8):
                        hh = 8 * g2 + h
                        mm = M(y_ps[:, b, :], pT[:, s, h, :], vwo[:, b, hh * 64:(hh + 2) * 64], start=(hh == 0), stop=(hh == 15))
                    mm.then_inc(pv_mm, 1)
                scores(0)
                scores(1)
                for n in range(U):
                    attend(n)
                    if n + 2 < U:
                        scores(n + 2)
            turns(pe, TURNS, turn)


def lay_rope_attention(inp):
    g = lambda n: np.asarray(inp["L1_attn_" + n])
    wq, wkv, wo = g("wq"), g("wkv"), g("wo")
    z = lambda a: np.concatenate([a, np.zeros_like(a)])
    T, d = 128, 64
    freqs = (10000.0 ** (-2.0 * np.arange(d // 2, dtype=np.float32) / d)).astype(np.float32)
    theta = np.arange(T, dtype=np.float32)[:, None] * freqs[None, :]
    cos, sin = np.repeat(np.cos(theta), 2, axis=1), np.repeat(np.sin(theta), 2, axis=1)
    signed = sin * np.tile(np.array([-1.0, 1.0], np.float32), 32)
    csh = np.stack([np.tile(cos.T, (2, 1)), np.tile(signed.T, (2, 1))], axis=1).astype(np.float32)
    cst = np.stack([cos, sin], axis=1).astype(np.float32)
    wv = wkv[64:128]
    return dict(ra_wq=z(wq.T), ra_wk=z(wkv[0:64].T), ra_wv=np.concatenate([wv, np.zeros_like(wv)], axis=1),
                ra_wo=np.transpose(wo.reshape(64, 16, 64), (2, 1, 0)).reshape(64, 1024),
                ra_norms=np.broadcast_to(np.stack([g("q_norm_w"), g("k_norm_w")]), (128, 2, 64)), ra_csh=csh, ra_cst=cst)


NODE_BITS = 14
SELF_BIT = 14
DST_SHIFT = 15
KEY_BIT = 29
LIVE_BIT = 20


def exchange_steps(bits, cols, whole):
    out = []
    for k in (range(1, bits + 1) if whole else [bits]):
        if whole:
            out.append(("flip", k - 1))
        if k > cols:
            out.append(("turn", None))
            out += [("swap", 1 << (j - cols)) for j in range(k - 1, cols - 1, -1)]
            out.append(("turn", None))
        out += [("swap", 1 << j) for j in range(min(k, cols) - 1, -1, -1)]
    return out


def sort_edges(nc, edges, srt, comp, src_out, start_out, row_out, end_out):
    E = edges.shape[1]
    NODES = 1 << NODE_BITS
    TOTAL = E + NODES
    C = TOTAL // 128
    HALO = 128
    CH = C + HALO
    CB = C // 128
    with ExitStack() as ctx:
        sb = lambda n, s, d=F32: ctx.enter_context(nc.sbuf_tensor("sos_" + n, s, d))
        pb = lambda n, s, d=F32: ctx.enter_context(nc.psum_tensor("sop_" + n, s, d))
        sem = ctx.enter_context(semaphores(nc, "som_"))
        big = [sb("big0", [128, 2048]), sb("big1", [128, 2048])]
        small = [sb("small0", [128, 128]), sb("small1", [128, 128])]
        ident = sb("ident", [128, 128])
        sgn = sb("sgn", [128, 9]); pid = sb("pid", [128, 1], I32); bit = sb("bit", [128, 9], I32); pf = sb("pf", [128, 2])
        own = sb("own", [128, 128], I32); tail = sb("tail", [128, 128])
        keys = sb("keys", [128, CH + 1], I32); tmp = sb("tmp", [128, CH], I32); tmp2 = sb("tmp2", [128, CH], I32)
        w = [sb("w0", [128, CH], I32), sb("w1", [128, CH], I32)]
        posn = sb("posn", [128, CH], I32)
        fl = sb("fl", [128, C]); fl2 = sb("fl2", [128, C]); rowv = sb("rowv", [128, C])
        stop = sb("stop", [1, HALO + 1], I32); node = sb("node", [128, 128], I32); ends = sb("ends", [128, 128], I32)
        ps = pb("ps", [128, 5, 512])
        ident_ok = sem("ident_ok"); consts = sem("consts"); e_in = sem("e_in"); st = sem("st")
        turn_src = sem("turn_src"); turn_mm = sem("turn_mm"); turn_a = sem("turn_a")
        a_out = sem("a_out"); tail_in = sem("tail_in"); lo_ok = sem("lo_ok"); lo_out = sem("lo_out"); l_in = sem("l_in")
        fin_ok = sem("fin_ok"); s_out = sem("s_out"); k_in = sem("k_in"); o_ok = sem("o_ok"); outs = sem("outs")
        c_ok = sem("c_ok"); c_out = sem("c_out"); c_in = sem("c_in"); cT_mm = sem("cT_mm"); end_ok = sem("end_ok")
        AS_I = lambda t: t[:].bitcast(I32)
        srt_f = srt.bitcast(F32)
        rows = lambda ap, n: ap.rearrange("(p c) -> p c", p=n)
        WHOLE = exchange_steps(18, 11, True)
        MERGE = exchange_steps(18, 11, False)
        MERGE_TAIL = exchange_steps(14, 7, False)
        runs = [(WHOLE, big, 16), (MERGE, big, 16), (MERGE_TAIL, small, 1)]
        places = []
        cur = {id(big): 0, id(small): 0}
        for steps, tiles, nb in runs:
            begin = cur[id(tiles)]
            moves = sum(1 for kind, _ in steps if kind != "flip")
            places.append((begin, (begin + moves) % 2))
            cur[id(tiles)] = (begin + moves) % 2
            if steps is WHOLE:
                cur[id(tiles)] = 0
        block = ctx.enter_context(nc.Block())

        def each_turn():
            n = 0
            for (steps, tiles, nb), (at, _) in zip(runs, places):
                for kind, _ in steps:
                    if kind == "turn":
                        yield n, tiles[at], tiles[1 - at], nb
                        n += 1
                    if kind != "flip":
                        at = 1 - at

        @block.sync
        def _(sp):
            sp.dma_start(AS_I(big[0]), rows(edges[1, :], 128)).then_inc(e_in, 16)
            sp.dma_start(tmp[:, 0:2048], rows(edges[0, :], 128)).then_inc(e_in, 16)
            sp.wait_ge(fin_ok, 1)
            sp.dma_start(rows(srt_f[0:E], 128), big[places[0][1]][:]).then_inc(a_out, 16)
            sp.wait_ge(a_out, 16)
            sp.dma_start(tail[:], rows(srt_f[E - NODES:E], 128)).then_inc(tail_in, 16)
            sp.wait_ge(lo_ok, 2)
            sp.dma_start(rows(srt_f[E - NODES:E], 128), small[1][:]).then_inc(lo_out, 16)
            sp.wait_ge(lo_out, 16)
            sp.dma_start(big[0][:], rows(srt_f[0:E], 128)).then_inc(l_in, 16)
            sp.wait_ge(fin_ok, 2)
            sp.dma_start(rows(srt_f[0:E], 128), big[places[1][1]][:]).then_inc(s_out, 16)
            sp.wait_ge(fin_ok, 3)
            sp.dma_start(rows(srt_f[E:TOTAL], 128), small[places[2][1]][:]).then_inc(s_out, 16)
            sp.wait_ge(consts, 4)
            sp.dma_start(rows(srt[TOTAL:TOTAL + HALO + 1], 1), stop[:]).then_inc(s_out, 16)
            sp.wait_ge(s_out, 48)
            sp.dma_start(keys[0:127, :], bass.AP(srt.tensor, srt.offset, [[C, 127], [1, CH + 1]])).then_inc(k_in, 16)
            sp.dma_start(keys[127:128, :], rows(srt[127 * C:127 * C + CH + 1], 1)).then_inc(k_in, 16)
            sp.wait_ge(o_ok, 1)
            sp.dma_start(src_out.bitcast(I32), tmp2[:, 0:C]).then_inc(outs, 16)
            sp.wait_ge(o_ok, 2)
            sp.dma_start(start_out, fl[:]).then_inc(outs, 16)
            sp.wait_ge(o_ok, 3)
            sp.dma_start(row_out, rowv[:]).then_inc(outs, 16)
            sp.wait_ge(c_ok, 1)
            sp.dma_start(rows(comp, 128), fl2[:]).then_inc(c_out, 16)
            sp.wait_ge(c_out, 16)
            sp.dma_start(fl[:].rearrange("p (a k) -> p a k", k=128), comp.rearrange("(a p k) -> p a k", p=128, k=128)).then_inc(c_in, 16)
            sp.wait_ge(end_ok, 1)
            sp.dma_start(end_out.bitcast(I32), ends[:]).then_inc(outs, 16)
            sp.wait_ge(outs, 64)

        @block.gpsimd
        def _(pool):
            P = nc.gpsimd
            make_identity(nc, pool, ident, ident_ok)
            P.iota(pid[:], pattern=[[0, 1]], base=0, channel_multiplier=1).then_inc(consts, 1)
            P.iota(own[:], pattern=[[-1, 128]], base=NODES - 1, channel_multiplier=-128).then_inc(consts, 1)
            P.iota(node[:], pattern=[[128, 128]], base=0, channel_multiplier=1).then_inc(consts, 1)
            P.memset(stop[:, 1:], (1 << KEY_BIT) | (1 << SELF_BIT))
            P.memset(stop[:, 0:1], 1 << KEY_BIT).then_inc(consts, 1)
            P.iota(posn[:], pattern=[[1, CH]], base=0, channel_multiplier=C).then_inc(consts, 1)

        @block.tensor
        def _(pe):
            pe.wait_ge(ident_ok, 2)
            for n, src, dst, nb in each_turn():
                pe.wait_ge(turn_src, n + 1)
                for c in range(nb):
                    mm = nc.tensor.transpose(ps[:, c // 4, (c % 4) * 128:(c % 4 + 1) * 128], src[:, c * 128:(c + 1) * 128], ident[:])
                mm.then_inc(turn_mm, 1)
            pe.wait_ge(c_in, 16)
            for c in range(CB):
                mm = nc.tensor.transpose(ps[:, c // 4, (c % 4) * 128:(c % 4 + 1) * 128], fl[:, c * 128:(c + 1) * 128], ident[:])
            mm.then_inc(cT_mm, 1)

        @block.scalar
        def _(act):
            for n, src, dst, nb in each_turn():
                act.wait_ge(turn_mm, n + 1)
                if nb == 1:
                    nc.scalar.activation(dst[:], ps[:, 0, 0:128], ACT.Copy).then_inc(turn_a, 1)
                else:
                    nc.scalar.activation(dst[:, 0:1024], ps[:, 0:2, :].rearrange("p a k -> p (a k)"), ACT.Copy).then_inc(turn_a, 1)

        @block.vector
        def _(dve):
            V = nc.vector
            s = Steps(st, None, None)
            go = lambda ins: s.chain(dve, ins)
            dve.wait_ge(consts, 5)
            for b in range(8):
                go(V.tensor_scalar(bit[:, b:b + 1], pid[:], b, 1, ALU.logical_shift_right, ALU.bitwise_and))
            go(V.tensor_copy(sgn[:, 0:8], bit[:, 0:8]))
            go(V.tensor_scalar(sgn[:, 0:8], sgn[:, 0:8], -2.0, 1.0, ALU.mult, ALU.add))
            go(V.tensor_copy(pf[:, 0:1], pid[:]))
            go(V.tensor_scalar(pf[:, 1:2], pf[:, 0:1], -1.0, 128.0, ALU.mult, ALU.add))
            flips = sb("flips", [128, 7])
            go(V.tensor_tensor(flips[:], sgn[:, 0:7], sgn[:, 1:8], ALU.mult))
            dve.wait_ge(e_in, 32)
            k0 = AS_I(big[0])
            go(V.tensor_scalar(k0, k0, DST_SHIFT, (1 << KEY_BIT) | (1 << SELF_BIT), ALU.logical_shift_left, ALU.bitwise_or))
            go(V.tensor_tensor(k0, k0, tmp[:, 0:2048], ALU.bitwise_or))
            turn_no = 0
            for r, ((steps, tiles, nb), (at, end)) in enumerate(zip(runs, places)):
                if r == 1:
                    go(V.tensor_scalar(tmp[:, 0:128], own[:], DST_SHIFT, 1 << KEY_BIT, ALU.logical_shift_left, ALU.bitwise_or))
                    go(V.tensor_tensor(own[:], own[:], tmp[:, 0:128], ALU.bitwise_or))
                    dve.wait_ge(tail_in, 16)
                    V.tensor_tensor(small[0][:], tail[:], own[:].bitcast(F32), ALU.max).then_inc(lo_ok, 1)
                    V.tensor_tensor(small[1][:], tail[:], own[:].bitcast(F32), ALU.min).then_inc(lo_ok, 1)
                    dve.wait_ge(lo_ok, 2)
                    dve.wait_ge(l_in, 16)
                for x, (kind, arg) in enumerate(steps):
                    t = tiles[at]
                    if kind == "flip":
                        k = arg
                        if k == 0:
                            v = t[:].rearrange("p (a y b) -> p a y b", y=2, b=2)
                            go(V.tensor_scalar(v[:, :, 1, :], v[:, :, 1, :], -1.0, None, ALU.mult))
                        elif k < 10:
                            v = t[:].rearrange("p (a y b) -> p a y b", y=4, b=1 << k)
                            s.did(V.tensor_scalar(v[:, :, 1, :], v[:, :, 1, :], -1.0, None, ALU.mult))
                            go(V.tensor_scalar(v[:, :, 2, :], v[:, :, 2, :], -1.0, None, ALU.mult))
                        elif k == 10:
                            s.did(V.tensor_scalar(t[:, 0:1024], t[:, 0:1024], sgn[:, 0:1], None, ALU.mult))
                            go(V.tensor_scalar(t[:, 1024:2048], t[:, 1024:2048], sgn[:, 0:1], -1.0, ALU.mult, ALU.mult))
                        else:
                            go(V.tensor_scalar(t[:], t[:], flips[:, k - 11:k - 10], None, ALU.mult))
                        continue
                    d = tiles[1 - at]
                    if kind == "turn":
                        dve.sem_inc(turn_src, 1)
                        turn_no += 1
                        if nb > 1:
                            dve.wait_ge(turn_mm, turn_no)
                            go(V.tensor_copy(d[:, 1024:2048], ps[:, 2:4, :].rearrange("p a k -> p (a k)")))
                        dve.wait_ge(turn_a, turn_no)
                    else:
                        a = t[:].rearrange("p (a y b) -> p a y b", y=2, b=arg)
                        z = d[:].rearrange("p (a y b) -> p a y b", y=2, b=arg)
                        s.did(V.tensor_tensor(z[:, :, 0, :], a[:, :, 0, :], a[:, :, 1, :], ALU.min))
                        go(V.tensor_tensor(z[:, :, 1, :], a[:, :, 0, :], a[:, :, 1, :], ALU.max))
                    at = 1 - at
                assert at == end
                dve.sem_inc(fin_ok, 1)
            dve.wait_ge(k_in, 32)
            V.tensor_scalar(tmp2[:, 0:C], keys[:, 0:C], NODES - 1, None, ALU.bitwise_and).then_inc(o_ok, 1)
            go(V.tensor_scalar(w[0][:], keys[:, 0:CH], SELF_BIT, 1, ALU.logical_shift_right, ALU.bitwise_and))
            go(V.tensor_scalar(tmp[:], w[0][:], 1, None, ALU.bitwise_xor))
            V.tensor_copy(fl[:], tmp[:, 0:C]).then_inc(o_ok, 1)
            dve.wait_ge(o_ok, 2)
            go(V.tensor_tensor_scan(fl2[:], fl[:], fl[:], 0.0, ALU.max, ALU.max))
            V.tensor_scalar(rowv[:], fl2[:], pf[:, 1:2], pf[:, 0:1], ALU.mult, ALU.add).then_inc(o_ok, 1)
            go(V.tensor_scalar(tmp[:], keys[:, 1:CH + 1], SELF_BIT, 1, ALU.logical_shift_right, ALU.bitwise_and))
            go(V.tensor_scalar(w[1][:], keys[:, 0:CH], DST_SHIFT, NODES - 1, ALU.logical_shift_right, ALU.bitwise_and))
            go(V.tensor_tensor(w[1][:], posn[:], w[1][:], ALU.subtract))
            go(V.tensor_scalar(w[1][:], w[1][:], float(1 << LIVE_BIT), None, ALU.add))
            go(V.tensor_scalar(tmp[:], tmp[:], -1.0, None, ALU.add))
            go(V.tensor_tensor(w[0][:], w[1][:], tmp[:], ALU.bitwise_and))

            def pull(j, shift, n):
                a, b = w[0], w[1]
                go(V.tensor_scalar(tmp[:, 0:n], a[:, 0:n], 31 - j, 31, ALU.logical_shift_left, ALU.arith_shift_right))
                go(V.tensor_tensor(tmp[:, 0:n], tmp[:, 0:n], a[:, 0:n], ALU.bitwise_and))
                go(V.tensor_tensor(a[:, 0:n], a[:, 0:n], tmp[:, 0:n], ALU.bitwise_xor))
                go(V.tensor_tensor(a[:, 0:n - shift], a[:, 0:n - shift], tmp[:, shift:n], ALU.bitwise_or))
            dve.wait_ge(o_ok, 3)
            for j in range(7):
                pull(j, 1 << j, CH)
            V.tensor_copy(fl2[:], w[0][:, 0:C]).then_inc(c_ok, 1)
            dve.wait_ge(cT_mm, 1)
            go(V.tensor_copy(w[0][:, 0:C], ps[:].rearrange("p a k -> p (a k)")[:, 0:C]))
            for j in range(7, 19):
                pull(j, 1 << (j - 7), C)
            go(V.tensor_scalar(ends[:], w[0][:, 0:128], (1 << LIVE_BIT) - 1, None, ALU.bitwise_and))
            V.tensor_tensor(ends[:], ends[:], node[:], ALU.add).then_inc(end_ok, 1)


LOWEST = -3.0e38
ROW = 24


def node_table(nc, h_in, wg, att, table, sT_out):
    B, T, _ = h_in.shape
    G = 4
    TURNS = B // G
    with ExitStack() as ctx:
        sb = lambda n, s, d=F32: ctx.enter_context(nc.sbuf_tensor("nts_" + n, s, d))
        pb = lambda n, s, d=F32: ctx.enter_context(nc.psum_tensor("ntp_" + n, s, d))
        sem = ctx.enter_context(semaphores(nc, "ntm_"))
        ln = LayerNorm(nc, sb, sem, G, copies=2)
        w = sb("w", [128, 128]); a = sb("a", [128, 2, 16]); prod = sb("prod", [128, 2, 16])
        ident = sb("ident", [128, 128]); sT = sb("sT", [128, 512]); t = sb("t", [128, G, ROW])
        sT_ps = pb("sT", [128, 512]); t_ps = pb("t", [128, G, 128])
        w_in = sem("w_in"); const = sem("const"); w_ok = sem("w_ok"); sT_mm = sem("sT_mm"); sT_ok = sem("sT_ok"); t_mm = sem("t_mm"); t_ok = sem("t_ok")
        out_s = sem("out_s"); out_t = sem("out_t")
        hi = h_in.rearrange("b t n -> t b n"); to = table.rearrange("(b t) n -> t b n", t=T)
        block = ctx.enter_context(nc.Block())

        @block.sync
        def _(sp):
            sp.wait_ge(w_ok, 1)
            sp.dma_start(w[:, 0:16], wg).then_inc(w_in, 16)
            sp.dma_start(a[:], att).then_inc(w_in, 16)
            sp.wait_ge(ln.step, 1)
            sp.dma_start(ln.x[:], hi[:, 0:G, :]).then_inc(ln.loaded, 16)

            def turn(i, more):
                if more:
                    ln.load(sp, i + 1, hi[:, bass.ds(i * G + G, G), :])
                sp.wait_ge(sT_ok, i + 2)
                sp.dma_start(sT_out[:, bass.ds(i * 512, 512)], sT[:]).then_inc(out_s, 16)
                sp.wait_ge(t_ok, i + 2)
                sp.dma_start(to[:, bass.ds(i * G, G), :], t[:]).then_inc(out_t, 16)
            turns(sp, TURNS, turn)
            sp.wait_ge(out_s, TURNS * 16 + 16)
            sp.wait_ge(out_t, TURNS * 16 + 16)

        @block.gpsimd
        def _(pool):
            make_identity(nc, pool, ident, const)
            ln.gpsimd(pool, 0)

            def turn(i, more):
                if more:
                    ln.gpsimd(pool, i + 1)
            turns(pool, TURNS, turn)

        @block.vector
        def _(dve):
            V = nc.vector
            ln.start()
            V.memset(w[:], 0.0).then_inc(w_ok, 1)
            dve.wait_ge(w_in, 32)
            V.tensor_tensor(prod[:], a[:], w[:, 0:16].rearrange("p (o e) -> p o e", o=1).to_broadcast([128, 2, 16]), ALU.mult).then_inc(w_ok, 1)
            dve.wait_ge(w_ok, 2)
            V.tensor_reduce(w[:, 16:24].rearrange("p (a h) -> p a h", a=2), prod[:].rearrange("p a (h e) -> p a h e", e=4), AX, ALU.add).then_inc(w_ok, 1)
            ln.vector(dve, 0)
            dve.sem_inc(t_ok, 1)

            def turn(i, more):
                if more:
                    dve.wait_ge(sT_mm, i + 1)
                    ln.vector(dve, i + 1)
                dve.wait_ge(t_mm, i + 1)
                dve.wait_ge(out_t, i * 16 + 16)
                V.tensor_copy(t[:], t_ps[:, :, 0:ROW]).then_inc(t_ok, 1)
            turns(dve, TURNS, turn)

        @block.scalar
        def _(act):
            act.sem_inc(out_s, 16)
            act.sem_inc(out_t, 16)
            act.sem_inc(sT_ok, 1)

            def turn(i, more):
                act.wait_ge(sT_mm, i + 1)
                act.wait_ge(out_s, i * 16 + 16)
                act.wait_ge(t_ok, i + 1)
                nc.scalar.activation(sT[:], sT_ps[:], ACT.Copy).then_inc(sT_ok, 1)
            turns(act, TURNS, turn)

        @block.tensor
        def _(pe):
            pe.wait_ge(const, 2)
            pe.wait_ge(w_ok, 3)

            def turn(i, more):
                ln.ready(pe, i)
                for b in range(G):
                    mm = nc.tensor.transpose(sT_ps[:, b * 128:(b + 1) * 128], ln.out[:, b].rearrange("p c n -> p (c n)"), ident[:])
                mm.then_inc(sT_mm, 1)
                pe.wait_ge(sT_ok, i + 2)
                pe.wait_ge(t_ok, i + 1)
                for b in range(G):
                    mm = nc.tensor.matmul(t_ps[:, b, :], sT[:, b * 128:(b + 1) * 128], w[:], start=True, stop=True)
                mm.then_inc(t_mm, 1)
            turns(pe, TURNS, turn)


def edge_softmax(nc, table, src, start, row, ends, srt, seg, carry, post, scores):
    C = src.shape[1]
    N = 34
    TURNS = C // (2 * N)
    F = 25
    B = 128
    with ExitStack() as ctx:
        sb = lambda n, s, d=F32: ctx.enter_context(nc.sbuf_tensor("ess_" + n, s, d))
        pb = lambda n, s, d=F32: ctx.enter_context(nc.psum_tensor("esp_" + n, s, d))
        sem = ctx.enter_context(semaphores(nc, "esm_"))
        idx = sb("idx", [128, 2, N], U32); st = sb("st", [128, 2, N]); rw = sb("rw", [128, 2, N])
        keep = sb("keep", [128, N]); neg = sb("neg", [128, N])
        g = sb("g", [128, 2, N, ROW])
        adm = sb("adm", [128, N, 4]); ad = sb("ad", [128, 2, N, 4]); e = sb("e", [128, N, 4]); el = sb("el", [128, N, 4])
        mx = sb("mx", [128, 2, N + 1, 4]); x = sb("x", [128, 2, N, 4]); xe = sb("xe", [128, 2, N, 4])
        v = sb("v", [128, N, 16]); r = sb("r", [128, 2, N, F])
        fidx = sb("fidx", [128, 1], I32); frow = sb("frow", [128, ROW]); dummy = sb("dummy", [128, 1]); dummy2 = sb("dummy2", [128, 1]); poked = sem("poked")
        ident = sb("ident", [128, 128])
        tot = sb("tot", [128, 3, 20]); tt = sb("tt", [20, 3, 128]); cm = sb("cm", [20, B + 1]); cs = sb("cs", [20, B + 1])
        ca = sb("ca", [20, 128]); cb = sb("cb", [20, 128]); ct = sb("ct", [128, 40]); neutral = sb("neutral", [1, 40])
        endi = sb("endi", [128, B], U32); q = sb("q", [128, B, F]); ci = sb("ci", [128, B], U32); z = sb("z", [128, B, 40])
        m2 = sb("m2", [128, B, 4]); w12 = sb("w12", [128, 2, B, 4]); s2 = sb("s2", [128, B, 20]); mu = sb("mu", [128, B]); var = sb("var", [128, B])
        post_s = sb("post", [128, 3, 16]); sc = sb("sc", [128, B, 4])
        tot_ps = pb("tot", [20, 3, 128]); ct_ps = pb("ct", [128, 2, 20])
        idx_in = [sem("idx_in0"), sem("idx_in1")]; g_in = [sem("g_in0"), sem("g_in1")]; done = sem("done"); st_ = sem("st"); ex = sem("ex"); x_ok = sem("x_ok")
        tail_ok = sem("tail_ok"); put = [sem("put0"), sem("put1")]; first = sem("first"); first_in = sem("first_in"); f_ok = sem("f_ok")
        free = [sem("free0"), sem("free1")]; fin2 = sem("fin2"); dmy = sb("dmy", [128, 1])
        const = sem("const"); fin = sem("fin"); tot_ok = sem("tot_ok"); tot_mm = sem("tot_mm"); cexp = sem("cexp"); ct_src = sem("ct_src"); ct_mm = sem("ct_mm"); ct_ok = sem("ct_ok"); ct_put = sem("ct_put")
        q_in = sem("q_in"); ci_ok = sem("ci_ok"); z_in = sem("z_in"); w12_ok = sem("w12_ok"); w12_e = sem("w12_e"); sq_s = sem("sq_s"); sq_e = sem("sq_e"); sc_ok = sem("sc_ok"); p_in = sem("p_in"); out = sem("out")
        seg_v = seg.rearrange("(p c) f -> p (c f)", p=128)
        CHAIN = 12
        block = ctx.enter_context(nc.Block())

        @block.sync
        def _(sp):
            sp.dma_start(post_s[:], post).then_inc(p_in, 16)
            sp.dma_start(endi[:], ends).then_inc(p_in, 16)
            sp.dma_start(fidx[:], srt[0:128 * C].rearrange("(p c) -> p c", p=128)[:, 0:1], allow_slow_non_contiguous=True).then_inc(first, 16)

            def load(i, c):
                s = bass.ds(i * (2 * N) + c * N, N)
                sp.dma_start(idx[:, c, :], src[:, s]).then_inc(idx_in[c], 16)
                sp.dma_start(st[:, c, :], start[:, s]).then_inc(idx_in[c], 16)
                sp.dma_start(rw[:, c, :], row[:, s]).then_inc(idx_in[c], 16)
            for c in range(2):
                load(0, c)

            def turn(i, more):
                for c in range(2):
                    sp.wait_ge(tail_ok, i * 4 + (2 * c + 4))
                    sp.dma_start(seg_v[:, bass.ds(i * (2 * N * F) + c * N * F, N * F)], r[:, c].rearrange("p n f -> p (n f)")).then_inc(put[c], 16)
                    if more:
                        load(i + 1, c)
            turns(sp, TURNS, turn)
            for c in range(2):
                sp.wait_ge(put[c], TURNS * 16 + 16)
            sp.sem_inc(fin, 1)
            sp.wait_ge(ct_ok, 2)
            sp.dma_start(carry[0:128, :], ct[:]).then_inc(ct_put, 16)
            sp.dma_start(carry[128:129, :], neutral[:]).then_inc(ct_put, 16)
            sp.wait_ge(sc_ok, 1)
            sp.dma_start(scores, sc[:]).then_inc(out, 16)
            sp.wait_ge(out, 16)

        @block.gpsimd
        def _(pool):
            P = nc.gpsimd
            make_identity(nc, pool, ident, const)
            P.memset(dummy[:], 0.0).then_inc(const, 1)
            P.memset(neutral[:, 0:20], 0.0).then_inc(const, 1)
            P.memset(neutral[:, 20:40], LOWEST).then_inc(const, 1)
            pool.wait_ge(const, 5)
            pool.wait_ge(f_ok, 1)
            P.indirect_dma_start(frow[:], None, table, bass.IndirectOffsetOnAxis(ap=fidx[:].bitcast(U32), axis=0)).then_inc(first_in, 16)

            pool.sem_inc(poked, 1)

            def turn(i, more):
                for c in range(2):
                    pool.wait_ge(idx_in[c], i * 48 + 48)
                    pool.wait_ge(free[c], i + 1)
                    pool.wait_ge(poked, i * 2 + (c + 1))
                    P.tensor_tensor(dummy2[:], dummy[:], dummy[:], ALU.add).then_inc(poked, 1)
                    for k in range(N):
                        P.indirect_dma_start(g[:, c, k, :], None, table, bass.IndirectOffsetOnAxis(ap=idx[:, c, k:k + 1], axis=0)).then_inc(g_in[c], 16)
            turns(pool, TURNS, turn)
            pool.wait_ge(fin, 1)
            pool.wait_ge(p_in, 32)
            for b in range(B):
                P.indirect_dma_start(q[:, b, :], None, seg, bass.IndirectOffsetOnAxis(ap=endi[:, b:b + 1], axis=0)).then_inc(q_in, 16)
            pool.wait_ge(ci_ok, 1)
            pool.wait_ge(ct_put, 32)
            for b in range(B):
                P.indirect_dma_start(z[:, b, :], None, carry, bass.IndirectOffsetOnAxis(ap=ci[:, b:b + 1], axis=0)).then_inc(z_in, 16)

        @block.scalar
        def _(act):
            A = nc.scalar
            act.sem_inc(put[0], 16)
            act.sem_inc(put[1], 16)
            act.sem_inc(tail_ok, 2)

            def turn(i, more):
                for c in range(2):
                    act.wait_ge(ex, i * 2 + (c + 1))
                    A.activation(xe[:], x[:], ACT.Exp).then_inc(x_ok, 1)
                    act.wait_ge(put[c], i * 16 + 16)
                    A.activation(r[:, c, :, 20:24], mx[:, c, 1:N + 1, :], ACT.Copy).then_inc(tail_ok, 1)
                    act.wait_ge(done, i * 2 + (c + 1))
                    A.activation(r[:, c, :, 24], rw[:, c, :], ACT.Copy).then_inc(tail_ok, 1)
            turns(act, TURNS, turn)
            act.wait_ge(cexp, 1)
            A.activation(ca[:], ca[:], ACT.Exp).then_inc(cexp, 1)
            A.activation(cb[:], cb[:], ACT.Exp).then_inc(cexp, 1)
            act.wait_ge(w12_ok, 1)
            A.activation(w12[:], w12[:], ACT.Exp).then_inc(w12_e, 1)
            act.wait_ge(sq_s, 1)
            A.activation(var[:], var[:], ACT.Sqrt).then_inc(sq_e, 1)

        @block.tensor
        def _(pe):
            pe.wait_ge(const, 2)
            pe.wait_ge(tot_ok, 1)
            for k in range(3):
                mm = nc.tensor.transpose(tot_ps[:, k, :], tot[:, k, :], ident[:])
            mm.then_inc(tot_mm, 1)
            pe.wait_ge(ct_src, 1)
            nc.tensor.transpose(ct_ps[:, 0, :], cs[:, 0:128], ident[0:20, 0:20])
            nc.tensor.transpose(ct_ps[:, 1, :], cm[:, 0:128], ident[0:20, 0:20]).then_inc(ct_mm, 1)

        @block.vector
        def _(dve):
            V = nc.vector
            one = Steps(fin2, None, None)
            go = lambda ins: one.chain(dve, ins)
            dve.wait_ge(first, 16)
            V.tensor_scalar(fidx[:], fidx[:], DST_SHIFT, (1 << NODE_BITS) - 1, ALU.logical_shift_right, ALU.bitwise_and).then_inc(f_ok, 1)
            go(V.memset(mx[:, 1, N, :], LOWEST))
            go(V.memset(r[:, 1, N - 1, 0:20], 0.0))
            dve.wait_ge(first_in, 16)
            go(V.tensor_copy(ad[:, 1, N - 1, :], frow[:, 20:24]))
            dve.sem_inc(free[0], 1)
            dve.sem_inc(free[1], 1)

            def turn(i, more):
                for c in range(2):
                    o = 1 - c
                    s = Steps(st_, 2 * CHAIN, i)
                    s.n = c * CHAIN
                    dve.wait_ge(idx_in[c], i * 48 + 48)
                    s.did(V.tensor_scalar(keep[:], st[:, c, :], -1.0, 1.0, ALU.mult, ALU.add))
                    s.did(V.tensor_scalar(neg[:], st[:, c, :], LOWEST, None, ALU.mult))
                    dve.wait_ge(g_in[c], i * (16 * N) + 16 * N)
                    s.chain(dve, V.tensor_tensor(adm[:], g[:, c, :, 20:24], bc(st[:, c, :], [128, N, 4]), ALU.mult))
                    for h in range(4):
                        ins = V.tensor_tensor_scan(ad[:, c, :, h], keep[:], adm[:, :, h], ad[:, o, N - 1, h:h + 1], ALU.mult, ALU.add)
                    s.chain(dve, ins)
                    s.chain(dve, V.tensor_tensor(e[:], g[:, c, :, 16:20], ad[:, c], ALU.add))
                    s.chain(dve, V.scalar_tensor_tensor(el[:], e[:], 0.2, e[:], ALU.mult, ALU.max))
                    dve.wait_ge(tail_ok, i * 4 + (2 * c + 2))
                    s.chain(dve, V.tensor_copy(mx[:, c, 0, :], mx[:, o, N, :]))
                    for h in range(4):
                        ins = V.tensor_tensor_scan(mx[:, c, 1:N + 1, h], neg[:], el[:, :, h], mx[:, o, N, h:h + 1], ALU.add, ALU.max)
                    s.chain(dve, ins)
                    s.did(V.tensor_tensor(x[:, 1], el[:], mx[:, c, 1:N + 1, :], ALU.subtract))
                    s.chain(dve, V.tensor_tensor(x[:, 0], mx[:, c, 0:N, :], mx[:, c, 1:N + 1, :], ALU.subtract))
                    V.tensor_scalar(x[:, 0], x[:, 0], 0.0, None, ALU.min).then_inc(ex, 1)
                    dve.wait_ge(x_ok, i * 2 + (c + 1))
                    s.did(V.tensor_tensor(xe[:, 0], xe[:, 0], bc(keep[:], [128, N, 4]), ALU.mult))
                    s.chain(dve, V.tensor_tensor(v[:].rearrange("p n (h k) -> p n h k", k=4), g[:, c, :, 0:16].rearrange("p n (h k) -> p n h k", k=4),
                                                 xe[:, 1].rearrange("p n (h o) -> p n h o", o=1).to_broadcast([128, N, 4, 4]), ALU.mult))
                    dve.sem_inc(free[c], 1)
                    dve.wait_ge(put[c], i * 16 + 16)
                    for f in range(20):
                        h = f // 4 if f < 16 else f - 16
                        ins = V.tensor_tensor_scan(r[:, c, :, f], xe[:, 0, :, h], v[:, :, f] if f < 16 else xe[:, 1, :, h],
                                                   r[:, o, N - 1, f:f + 1], ALU.mult, ALU.add)
                    ins.then_inc(done, 1)
                    dve.wait_ge(done, i * 2 + (c + 1))
                    assert s.n == (c + 1) * CHAIN, s.n
            turns(dve, TURNS, turn)
            dve.wait_ge(tail_ok, TURNS * 4 + 2)
            go(V.tensor_copy(tot[:, 0, :], r[:, 1, N - 1, 0:20]))
            go(V.tensor_copy(tot[:, 1, 0:16].rearrange("p (h k) -> p h k", k=4), bc(mx[:, 1, N, :], [128, 4, 4])))
            go(V.tensor_copy(tot[:, 1, 16:20], mx[:, 1, N, :]))
            go(V.tensor_scalar(dmy[:], r[:, 1, N - 1, 24:25], 128.0, None, ALU.is_equal))
            V.tensor_copy(tot[:, 2, :], dmy[:].to_broadcast([128, 20])).then_inc(tot_ok, 1)
            dve.wait_ge(tot_mm, 1)
            go(V.tensor_copy(tt[:], tot_ps[:]))
            go(V.memset(cm[:, 0:1], LOWEST))
            go(V.memset(cs[:, 0:1], 0.0))
            go(V.tensor_scalar(cb[:], tt[:, 2, :], LOWEST, None, ALU.mult))
            go(V.tensor_tensor_scan(cm[:, 1:], cb[:], tt[:, 1, :], LOWEST, ALU.add, ALU.max))
            go(V.tensor_tensor(ca[:], cm[:, 0:B], cm[:, 1:], ALU.subtract))
            go(V.tensor_scalar(ca[:], ca[:], 0.0, None, ALU.min))
            V.tensor_tensor(cb[:], tt[:, 1, :], cm[:, 1:], ALU.subtract).then_inc(cexp, 1)
            dve.wait_ge(cexp, 3)
            go(V.tensor_scalar(tt[:, 2, :], tt[:, 2, :], -1.0, 1.0, ALU.mult, ALU.add))
            go(V.tensor_tensor(ca[:], ca[:], tt[:, 2, :], ALU.mult))
            go(V.tensor_tensor(cb[:], cb[:], tt[:, 0, :], ALU.mult))
            V.tensor_tensor_scan(cs[:, 1:], ca[:], cb[:], 0.0, ALU.mult, ALU.add).then_inc(ct_src, 1)
            dve.wait_ge(ct_mm, 1)
            V.tensor_copy(ct[:].rearrange("p (a f) -> p a f", a=2), ct_ps[:]).then_inc(ct_ok, 1)
            dve.wait_ge(const, 5)
            dve.sem_inc(ct_ok, 1)
            dve.wait_ge(q_in, 16 * B)
            V.tensor_copy(ci[:], q[:, :, 24]).then_inc(ci_ok, 1)
            dve.wait_ge(z_in, 16 * B)
            go(V.tensor_tensor(m2[:], q[:, :, 20:24], z[:, :, 36:40], ALU.max))
            go(V.tensor_tensor(w12[:, 0], q[:, :, 20:24], m2[:], ALU.subtract))
            V.tensor_tensor(w12[:, 1], z[:, :, 36:40], m2[:], ALU.subtract).then_inc(w12_ok, 1)
            dve.wait_ge(w12_e, 1)
            quad = lambda t: t.rearrange("p b (h k) -> p b h k", k=4)
            wide = lambda t: t.rearrange("p b (h o) -> p b h o", o=1).to_broadcast([128, B, 4, 4])
            for t, k in ((q, 0), (z, 1)):
                go(V.tensor_tensor(quad(t[:, :, 0:16]), quad(t[:, :, 0:16]), wide(w12[:, k]), ALU.mult))
                go(V.tensor_tensor(t[:, :, 16:20], t[:, :, 16:20], w12[:, k], ALU.mult))
            go(V.tensor_tensor(s2[:], q[:, :, 0:20], z[:, :, 0:20], ALU.add))
            go(V.tensor_scalar(m2[:], s2[:, :, 16:20], 1e-16, None, ALU.add))
            go(V.reciprocal(m2[:], m2[:]))
            a = s2[:, :, 0:16]
            go(V.tensor_tensor(quad(a), quad(a), wide(m2[:]), ALU.mult))
            over = lambda k: post_s[:, k:k + 1, :].to_broadcast([128, B, 16])
            go(V.tensor_tensor(a, a, over(0), ALU.add))
            go(V.tensor_reduce(mu[:], a, AX, ALU.add))
            go(V.tensor_scalar(mu[:], mu[:], 1.0 / 16, None, ALU.mult))
            go(V.tensor_tensor(a, a, bc(mu[:], [128, B, 16]), ALU.subtract))
            sq = z[:, :, 0:16]
            go(V.tensor_tensor(sq, a, a, ALU.mult))
            go(V.tensor_reduce(var[:], sq, AX, ALU.add))
            go(V.tensor_scalar(var[:], var[:], 1.0 / 16, LN_EPS, ALU.mult, ALU.add))
            V.reciprocal(var[:], var[:]).then_inc(sq_s, 1)
            dve.wait_ge(sq_e, 1)
            go(V.tensor_tensor(a, a, bc(var[:], [128, B, 16]), ALU.mult))
            go(V.tensor_tensor(a, a, over(1), ALU.mult))
            go(V.tensor_tensor(a, a, over(2), ALU.add))
            go(V.tensor_reduce(sc[:], a.rearrange("p b (h k) -> p b k h", k=4), AX, ALU.add))
            V.tensor_scalar(sc[:], sc[:], 0.25, None, ALU.mult).then_inc(sc_ok, 1)


def experts4(nc, h_in, sT_in, scores, w1, b1, w2, b2, h_out):
    B, T, _ = h_in.shape
    G, E = 4, 4
    TURNS = B // G
    with ExitStack() as ctx:
        sb = lambda n, s, d=F32: ctx.enter_context(nc.sbuf_tensor("mgs_" + n, s, d))
        pb = lambda n, s, d=F32: ctx.enter_context(nc.psum_tensor("mgp_" + n, s, d))
        sem = ctx.enter_context(semaphores(nc, "mgm_"))
        gt = Gate(nc, sb, sem, G, 8)
        w1_s = sb("w1", [128, E * 128]); b1_s = sb("b1", [128, E]); w2_s = sb("w2", [128, E * D + D]); b2_s = sb("b2", [128, E, D])
        sT = sb("sT", [128, 2, 512]); res = sb("res", [128, 2, G, D]); acc = sb("acc", [128, 2, G, D]); part = sb("part", [128, G, D])
        sc = sb("sc", [128, G, 4]); hid = sb("hid", [128, 2, 512])
        hid_ps = pb("hid", [128, 3, 512]); y_ps = pb("y", [128, 4, G, 2 * D])
        w_in = sem("w_in"); pad = sem("pad"); in_ = [sem("in0"), sem("in1")]; sc_in = sem("sc_in"); lg = sem("lg"); hid_mm = sem("hid_mm"); hid_ok = sem("hid_ok")
        y_mm = sem("y_mm"); st = sem("st"); acc_ok = sem("acc_ok"); put = [sem("put0"), sem("put1")]
        hi = h_in.rearrange("b t n -> t b n"); ho = h_out.rearrange("b t n -> t b n")
        loads = [(w1_s[:], w1), (b1_s[:], b1), (w2_s[:, 0:E * D], w2), (b2_s[:], b2)]
        HALF = TURNS // 2
        CH = 11
        block = ctx.enter_context(nc.Block())

        @block.sync
        def _(sp):
            for dst, src in loads:
                sp.dma_start(dst, src).then_inc(w_in, 16)

            def turn(i, more):
                for c in range(2):
                    sp.wait_ge(acc_ok, i * 2 + (c + 1))
                    sp.dma_start(sT[:, c, :], sT_in[:, bass.ds(i * 1024 + c * 512, 512)]).then_inc(in_[c], 16)
                    sp.dma_start(res[:, c], hi[:, bass.ds(i * 2 * G + c * G, G), :]).then_inc(in_[c], 16)
                    sp.wait_ge(lg, i * 2 + (c + 2))
                    sp.dma_start(sc[:], scores[:, bass.ds(i * 2 * G + c * G, G), :]).then_inc(sc_in, 16)
            sp.sem_inc(lg, 1)
            turns(sp, HALF, turn)

        @block.gpsimd
        def _(pool):
            gt.start()

        @block.vector
        def _(dve):
            V = nc.vector
            V.memset(w2_s[:, E * D:], 0.0).then_inc(pad, 1)
            V.memset(gt.logits[:], LOWEST).then_inc(pad, 1)
            dve.wait_ge(pad, 2)
            dve.wait_ge(w_in, 16 * len(loads))
            dve.wait_ge(gt.iota_ok, 1)
            dve.sem_inc(acc_ok, 2)
            dve.sem_inc(lg, 1)

            def turn(i, more):
                for c in range(2):
                    k = i * 2 + c
                    dve.wait_ge(sc_in, i * 32 + (16 * c + 16))
                    V.tensor_copy(gt.logits[:, :, 0:4], sc[:]).then_inc(lg, 1)
                    dve.wait_ge(lg, i * 2 + (c + 3))
                    gt.first(dve, k)
                    gt.second(dve, k)
                    gt.ready(dve, k)
                    s = Steps(st, 2 * CH, i)
                    s.n = c * CH
                    dve.wait_ge(in_[c], i * 32 + 32)
                    dve.wait_ge(put[c], i * 16 + 16)
                    for e in range(E):
                        dve.wait_ge(y_mm, i * (2 * E) + (c * E + e + 1))
                        s.chain(dve, V.tensor_tensor(part[:], y_ps[:, e, :, 0:D], b2_s[:, e:e + 1, :].to_broadcast([128, G, D]), ALU.add))
                        s.chain(dve, V.tensor_tensor(part[:], part[:], gt.gates[:, :, e:e + 1].to_broadcast([128, G, D]), ALU.mult))
                        if e < E - 1:
                            s.chain(dve, V.tensor_tensor(acc[:, c], part[:], acc[:, c] if e else res[:, c], ALU.add))
                    V.tensor_tensor(acc[:, c], part[:], acc[:, c], ALU.add).then_inc(acc_ok, 1)
                    assert s.n == (c + 1) * CH
            turns(dve, HALF, turn)

        @block.scalar
        def _(act):
            A = nc.scalar
            act.sem_inc(put[0], 16)
            act.sem_inc(put[1], 16)
            act.wait_ge(w_in, 16 * len(loads))

            def turn(i, more):
                for c in range(2):
                    gt.scalar(act, i * 2 + c)
                    for e in range(E):
                        n = c * E + e
                        act.wait_ge(hid_mm, i * (2 * E) + (n + 1))
                        if n >= 2:
                            act.wait_ge(y_mm, i * (2 * E) + (n - 1))
                        A.activation(hid[:, e % 2, :], hid_ps[:, n % 3, :], ACT.Gelu, bias=b1_s[:, e:e + 1]).then_inc(hid_ok, 1)
                    act.wait_ge(acc_ok, i * 2 + (c + 3))
                    act.dma_start(ho[:, bass.ds(i * 2 * G + c * G, G), :], acc[:, c]).then_inc(put[c], 16)
            turns(act, HALF, turn)
            for c in range(2):
                act.wait_ge(put[c], HALF * 16 + 16)

        @block.tensor
        def _(pe):
            M = nc.tensor.matmul
            pe.wait_ge(w_in, 16 * len(loads))
            pe.wait_ge(pad, 1)

            def turn(i, more):
                def hidden(n):
                    c, e = n // E, n % E
                    if e == 0:
                        pe.wait_ge(in_[c], i * 32 + 32)
                    if n >= 3:
                        pe.wait_ge(hid_ok, i * (2 * E) + (n - 2))
                    M(hid_ps[:, n % 3, :], w1_s[:, e * 128:(e + 1) * 128], sT[:, c, :], start=True, stop=True).then_inc(hid_mm, 1)

                def output(n):
                    c, e = n // E, n % E
                    pe.wait_ge(hid_ok, i * (2 * E) + (n + 1))
                    pe.wait_ge(acc_ok, i * 2 + (c + 2))
                    for b in range(G):
                        mm = M(y_ps[:, e, b, :], hid[:, e % 2, b * 128:(b + 1) * 128], w2_s[:, e * D:(e + 2) * D], start=True, stop=True)
                    mm.then_inc(y_mm, 1)
                hidden(0)
                hidden(1)
                for n in range(2 * E):
                    output(n)
                    if n + 2 < 2 * E:
                        hidden(n + 2)
            turns(pe, HALF, turn)


def lay_gat(inp):
    g = lambda n: np.asarray(inp["L1_ffn_" + n])
    z = lambda a: np.concatenate([a, np.zeros_like(a)])
    att = np.stack([g("att_src").reshape(16), g("att_dst").reshape(16)])
    return dict(ga_wg=z(g("W_gat")), ga_att=np.broadcast_to(att, (128, 2, 16)),
                ga_post=np.broadcast_to(np.stack([g("b_gat"), g("ln_gamma"), g("ln_beta")]), (128, 3, 16)),
                ga_w1=z(np.transpose(g("W1"), (1, 0, 2)).reshape(64, 512)), ga_b1=g("b1").T,
                ga_w2=np.transpose(g("W2"), (1, 0, 2)).reshape(128, 256), ga_b2=np.broadcast_to(g("b2"), (128, 4, 64)),
                ga_edges=g("edge_index"))


def tower(nc, a, out):
    B, N = 128, 128 * 128
    keys = a["ga_edges"].shape[1] + N
    C = keys // 128
    scratch = lambda name, shape, d=F32: nc.dram_tensor(name, shape, d, kind="Internal").ap()
    h = [scratch("h%d_scratch" % k, (B, 128, D)) for k in range(4)]
    tokenizer(nc, a["x"], *[a["tk_" + n] for n in ("wc1", "p1row", "p1col", "wc2", "p2row", "p2col", "wq", "wk", "bqk", "wv", "pv", "wc3", "p3col")], h[0])
    linear_attention(nc, h[0], a["la_wq"], a["la_we"], h[1])
    experts16(nc, h[1], *[a["mo_" + n] for n in ("wg", "gb", "w1", "b1", "w2", "b2", "post")], h[2])
    rope_attention(nc, h[2], *[a["ra_" + n] for n in ("wq", "wk", "wv", "wo", "norms", "csh", "cst")], h[3])
    srt = scratch("sorted_scratch", (keys + 129,), I32)
    comp = scratch("compact_scratch", (keys,))
    src = scratch("source_scratch", (128, C), U32)
    start = scratch("start_scratch", (128, C))
    row = scratch("row_scratch", (128, C))
    ends = scratch("ends_scratch", (128, B), U32)
    sort_edges(nc, a["ga_edges"], srt, comp, src, start, row, ends)
    table = scratch("table_scratch", (N, ROW))
    sT = scratch("sT_scratch", (128, N))
    node_table(nc, h[3], a["ga_wg"], a["ga_att"], table, sT)
    seg = scratch("segment_scratch", (keys, 25))
    carry = scratch("carry_scratch", (129, 40))
    scores = scratch("scores_scratch", (128, B, 4))
    edge_softmax(nc, table, src, start, row, ends, srt, seg, carry, a["ga_post"], scores)
    experts4(nc, h[3], sT, scores, a["ga_w1"], a["ga_b1"], a["ga_w2"], a["ga_b2"], out)


def kernel(**inputs):
    import numpy as _np
    import concourse.bacc as _bacc
    from concourse import mybir as _mybir
    from concourse.bass_utils import run_bass_kernel_spmd as _run

    laid = dict(x=inputs["x"])
    for lay in (lay_tokenizer, lay_linear_attention, lay_experts16, lay_rope_attention, lay_gat):
        laid.update(lay(inputs))
    nc = _bacc.Bacc("TRN2", target_bir_lowering=False, num_devices=1)
    arrays, args = {}, {}
    for name, value in laid.items():
        value = _np.ascontiguousarray(value)
        arrays[name + "_dram"] = value
        args[name] = nc.dram_tensor(name + "_dram", value.shape, _mybir.dt.from_np(value.dtype), kind="ExternalInput").ap()
    out = nc.dram_tensor("out_0_dram", (128, 128, D), _mybir.dt.float32, kind="ExternalOutput").ap()
    tower(nc, args, out)
    r = _run(nc, [arrays], core_ids=[0])
    return r.results[0]["out_0_dram"]
```

```python
import numpy as np
import concourse.bass as bass
from concourse import mybir
from contextlib import ExitStack, contextmanager

F32 = mybir.dt.float32
BF16 = mybir.dt.bfloat16
I32 = mybir.dt.int32
U32 = mybir.dt.uint32
ALU = mybir.AluOpType
ACT = mybir.ActivationFunctionType
AX = mybir.AxisListType.X
BN_EPS = 1e-5


@contextmanager
def semaphores(nc, prefix):
    mine = []

    def one(name):
        mine.append(nc.alloc_semaphore(name=prefix + name))
        return mine[-1]
    yield one
    nc.clear_and_free_semaphores(mine)
    nc.all_engine_barrier()


class Steps:

    def __init__(self, sem, per, turn):
        self.sem, self.per, self.turn, self.n = sem, per, turn, 0

    def did(self, ins):
        ins.then_inc(self.sem, 1)
        self.n += 1
        return self.n

    def wait(self, eng, n=None):
        n = self.n if n is None else n
        eng.wait_ge(self.sem, n if self.turn is None else self.turn * self.per + n)

    def chain(self, eng, ins):
        self.did(ins)
        self.wait(eng)

    def close(self):
        assert self.n == self.per, (self.n, self.per)


def turns(eng, n, body):
    with eng.Fori(0, n - 1) as i:
        body(i, True)
    body(n - 1, False)


def tokenizer(nc, sorter, x, wc1, p1row, p1col, wc2, p2row, p2col, wq, wk, bqk, wv, pv, wc3, p3col, h_out):
    B = x.shape[0]
    L = x.shape[1] // 2
    TURNS = B // 8
    AFTER = 6
    L1, L2 = L // 8, L // 32
    with ExitStack() as ctx:
        sb = lambda n, s, d=F32: ctx.enter_context(nc.sbuf_tensor("tks_" + n, s, d))
        pb = lambda n, s, d=F32: ctx.enter_context(nc.psum_tensor("tkp_" + n, s, d))
        sem = ctx.enter_context(semaphores(nc, "tkm_"))
        xin = sb("xin", [96, L])
        w1 = sb("w1", [96, 128]); r1 = sb("r1", [96, 2, 128]); sc1 = sb("sc1", [96, 128])
        c1 = sb("c1", [128, 5]); bias1 = sb("bias1", [128, 2])
        w2 = sb("w2", [128, 12, 128]); r2 = sb("r2", [128, 2, 128]); sc2 = sb("sc2", [128, 128])
        c2 = sb("c2", [128, 5]); bias2 = sb("bias2", [128, 2])
        c3 = sb("c3", [128, 5]); bias3 = sb("bias3", [128, 2])
        half = sb("half", [128, 128])
        wq_s = sb("wq", [128, 64]); wk_s = sb("wk", [128, 64]); bqk_s = sb("bqk", [64, 2])
        wv_s = sb("wv", [128, 128]); pv_s = sb("pv", [128, 2]); gbv = sb("gbv", [128, 1])
        w3 = sb("w3", [128, 2, 4, 128])
        ident = sb("ident", [128, 128])
        a1 = sb("a1", [128, L1]); a1r = sb("a1r", [128, L1 + 2])
        a2 = sb("a2", [128, 4, L2]); h2 = sb("h2", [128, 4, L2])
        q = sb("q", [64, 4 * L2]); k = sb("k", [64, 4 * L2])
        mx = sb("mx", [128, 8]); sums = sb("sums", [128, 8]); rs = sb("rs", [128, 8])
        p = sb("p", [128, 8, 128]); pn = sb("pn", [128, 8, 128]); pT = sb("pT", [128, 8, 128])
        vT = sb("vT", [128, 4, 128])
        og = sb("og", [128, 4, L2]); h3 = sb("h3", [128, 4, L2 + 2])
        h0 = sb("h0", [128, 4, 2, 64])
        conv_ps = pb("conv_ps", [128, 2, 512])
        qk_ps = pb("qk_ps", [64, 2, 512])
        e_ps = pb("e_ps", [128, 2, 512])
        v_ps = pb("v_ps", [128, 512])
        o_ps = pb("o_ps", [128, 512])
        pT_ps = e_ps

        w_in = sem("w_in"); x_in = sem("x_in"); stored = sem("stored")
        pre = sem("pre"); pw = sem("pw"); rec = sem("rec"); ident_ok = sem("ident_ok"); clean = sem("clean")
        c1_mm = sem("c1_mm"); c1_max = sem("c1_max"); a1_ok = sem("a1_ok")
        c2_mm = sem("c2_mm"); c2_max = sem("c2_max"); h2_ok = sem("h2_ok")
        qk_mm = sem("qk_mm"); qk_ok = sem("qk_ok"); v_mm = sem("v_mm"); v_ok = sem("v_ok")
        e_mm = sem("e_mm"); mx_ok = sem("mx_ok"); exp_ok = sem("exp_ok"); soft = sem("soft")
        pT_mm = sem("pT_mm"); pT_ok = sem("pT_ok")
        o_mm = sem("o_mm"); og_ok = sem("og_ok"); h3_ok = sem("h3_ok"); c3_mm = sem("c3_mm"); h0_ok = sem("h0_ok")
        xr = x.rearrange("b (c l) -> (b c) l", c=2)
        ho = h_out.rearrange("(g p u) t n -> t g p u n", p=4, u=2)
        loads = [(w1, wc1), (r1, p1row), (c1, p1col), (w2, wc2), (r2, p2row), (c2, p2col), (c3, p3col),
                 (wq_s, wq), (wk_s, wk), (bqk_s, bqk), (wv_s, wv), (pv_s, pv), (w3, wc3)]
        block = ctx.enter_context(nc.Block())

        @block.sync
        def _(sp):
            for dst, src in loads:
                sp.dma_start(dst[:], src).then_inc(w_in, 16)
            sorter.load(sp)
            sp.wait_ge(clean, 1)
            with sp.Fori(0, TURNS) as i:
                sp.wait_ge(c1_mm, i * 8 + 8)
                rows = xr[bass.ds(i * 16, 16), :]
                sp.dma_start(xin[0:16, 1:L], rows[:, 0:L - 1]).then_inc(x_in, 16)
                sp.dma_start(xin[32:48, :], rows).then_inc(x_in, 16)
                sp.dma_start(xin[64:80, 0:L - 1], rows[:, 1:L]).then_inc(x_in, 16)

        @block.gpsimd
        def _(pool):
            sorter.gpsimd()
            nc.gpsimd.memset(ident[:], 0.0).then_inc(ident_ok, 1)
            nc.gpsimd.memset(half[:], -0.5).then_inc(ident_ok, 1)
            pool.wait_ge(ident_ok, 2)
            nc.gpsimd.affine_select(out=ident[:], in_=ident[:], compare_op=ALU.not_equal, fill=1.0, base=0,
                                    pattern=[[-1, 128]], channel_multiplier=1).then_inc(ident_ok, 1)
            pool.wait_ge(pre, 5)
            nc.gpsimd.tensor_tensor(bias1[:, 0:1], c1[:, 4:5], half[:, 0:1], ALU.pow).then_inc(pw, 1)
            nc.gpsimd.tensor_tensor(bias2[:, 0:1], c2[:, 4:5], half[:, 0:1], ALU.pow).then_inc(pw, 1)
            nc.gpsimd.tensor_tensor(bias3[:, 0:1], c3[:, 4:5], half[:, 0:1], ALU.pow).then_inc(pw, 1)

        @block.vector
        def _(dve):
            V = nc.vector
            V.memset(xin[:], 0.0).then_inc(clean, 1)
            V.memset(a1r[:], 0.0).then_inc(clean, 1)
            V.memset(h3[:], 0.0).then_inc(clean, 1)
            dve.wait_ge(clean, 3)
            dve.wait_ge(w_in, 16 * len(loads))
            V.tensor_scalar_add(r1[:, 1, :], r1[:, 1, :], BN_EPS).then_inc(pre, 1)
            V.tensor_scalar_add(r2[:, 1, :], r2[:, 1, :], BN_EPS).then_inc(pre, 1)
            dve.wait_ge(pre, 2)
            V.reciprocal(sc1[:], r1[:, 1, :]).then_inc(rec, 1)
            V.reciprocal(sc2[:], r2[:, 1, :]).then_inc(rec, 1)
            for t in (c1, c2, c3):
                V.tensor_scalar_add(t[:, 4:5], t[:, 4:5], BN_EPS).then_inc(pre, 1)
            dve.wait_ge(pw, 5)
            done = Steps(pre, 5, None); done.n = 5
            done.did(V.tensor_tensor(sc1[:], sc1[:], r1[:, 0, :], ALU.mult))
            done.chain(dve, V.tensor_tensor(sc2[:], sc2[:], r2[:, 0, :], ALU.mult))
            done.did(V.tensor_tensor(w1[:], w1[:], sc1[:], ALU.mult))
            done.did(V.tensor_tensor(w2[:], w2[:], sc2[:].rearrange("p (a n) -> p a n", a=1).to_broadcast([128, 12, 128]), ALU.mult))
            for c, bi in ((c1, bias1), (c2, bias2), (c3, bias3)):
                done.chain(dve, V.tensor_tensor(bi[:, 0:1], bi[:, 0:1], c[:, 2:3], ALU.mult))
                done.chain(dve, V.tensor_tensor(bi[:, 1:2], c[:, 0:1], c[:, 1:2], ALU.subtract))
                done.chain(dve, V.tensor_tensor(bi[:, 1:2], bi[:, 1:2], bi[:, 0:1], ALU.mult))
                done.did(V.tensor_tensor(bi[:, 1:2], bi[:, 1:2], c[:, 3:4], ALU.add))
            done.did(V.tensor_tensor(gbv[:], pv_s[:, 0:1], pv_s[:, 1:2], ALU.mult))
            done.wait(dve)
            dve.sem_inc(pre, 100)

            def pool8(i, chunks):
                for c in chunks:
                    dve.wait_ge(c1_mm, i * 8 + (8 + c + 1))
                    if c == 0:
                        dve.wait_ge(a1_ok, i + 1)
                    V.tensor_reduce(a1[:, c * 64:(c + 1) * 64],
                                    conv_ps[:, c % 2, :].rearrange("p (a k) -> p a k", k=8), AX, ALU.max).then_inc(c1_max, 1)

            def pool4(i, carry):
                for pr in range(4):
                    dve.wait_ge(c2_mm, i * 4 + (pr + 1))
                    if pr == 0:
                        dve.wait_ge(h2_ok, i + 1)
                    V.tensor_reduce(a2[:, pr, :], conv_ps[:, pr % 2, :].rearrange("p (a k) -> p a k", k=4), AX, ALU.max).then_inc(c2_max, 1)
                    sorter.advance(dve, carry)
            sorter.start(dve)
            pool8(0, range(8))
            pool4(0, 0)

            def turn(i, more):
                soft_n = Steps(soft, 2, i)
                dve.wait_ge(e_mm, i + 1)
                V.tensor_reduce(mx[:], e_ps[:].rearrange("p u (r j) -> p (u r) j", j=128), AX, ALU.max, negate=True).then_inc(mx_ok, 1)
                if more:
                    pool8(i + 1, range(4))
                dve.wait_ge(exp_ok, i * 8 + 8)
                soft_n.chain(dve, V.reciprocal(rs[:], sums[:]))
                soft_n.did(V.tensor_tensor(pn[:], p[:], rs[:].rearrange("p (a o) -> p a o", o=1).to_broadcast([128, 8, 128]), ALU.mult))
                if more:
                    pool8(i + 1, range(4, 8))
                dve.wait_ge(pT_mm, i + 1)
                V.tensor_copy(pT[:, 0:4, :], pT_ps[:, 0, :].rearrange("p (a k) -> p a k", k=128)).then_inc(pT_ok, 1)
                dve.wait_ge(c3_mm, i * 2 + 2)
                dve.wait_ge(og_ok, i + 1)
                V.tensor_tensor(h3[:, :, 1:L2 + 1], og[:], h2[:], ALU.add).then_inc(h3_ok, 1)
                soft_n.close()
                if more:
                    pool4(i + 1, 1)
                sorter.advance(dve, AFTER if more else 0)
            for i in range(TURNS):
                turn(i, i < TURNS - 1)

        @block.scalar
        def _(act):
            A = nc.scalar
            act.wait_ge(rec, 2)
            A.activation(sc1[:], sc1[:], ACT.Sqrt).then_inc(pw, 1)
            A.activation(sc2[:], sc2[:], ACT.Sqrt).then_inc(pw, 1)
            act.wait_ge(pre, 120)
            act.sem_inc(a1_ok, 1)
            act.sem_inc(h2_ok, 1)
            act.sem_inc(stored, 32)
            act.sem_inc(h0_ok, 2)

            def relu1(i):
                act.wait_ge(c1_max, i * 8 + 8)
                A.activation(a1r[:, 1:L1 + 1], a1[:], ACT.Relu, bias=bias1[:, 1:2]).then_inc(a1_ok, 1)

            def relu2(i):
                act.wait_ge(c2_max, i * 4 + 4)
                A.activation(h2[:], a2[:], ACT.Relu, bias=bias2[:, 1:2]).then_inc(h2_ok, 1)
            relu1(0)
            relu2(0)

            def turn(i, more):
                act.wait_ge(qk_mm, i * 2 + 2)
                A.activation(q[:], qk_ps[:, 0, :], ACT.Identity, bias=bqk_s[:, 0:1]).then_inc(qk_ok, 1)
                A.activation(k[:], qk_ps[:, 1, :], ACT.Identity, bias=bqk_s[:, 1:2]).then_inc(qk_ok, 1)
                act.wait_ge(v_mm, i + 1)
                A.activation(vT[:], v_ps[:].rearrange("p (a k) -> p a k", k=128), ACT.Copy).then_inc(v_ok, 1)
                act.wait_ge(mx_ok, i + 1)
                for r in range(8):
                    A.activation(p[:, r, :], e_ps[:, r // 4, (r % 4) * 128:(r % 4 + 1) * 128], ACT.Exp,
                                 bias=mx[:, r:r + 1], accum_out=sums[:, r:r + 1]).then_inc(exp_ok, 1)
                if more:
                    relu1(i + 1)
                act.wait_ge(pT_mm, i + 1)
                A.activation(pT[:, 4:8, :], pT_ps[:, 1, :].rearrange("p (a k) -> p a k", k=128), ACT.Copy).then_inc(pT_ok, 1)
                act.wait_ge(o_mm, i + 1)
                A.activation(og[:], o_ps[:].rearrange("p (a k) -> p a k", k=128), ACT.Identity, bias=gbv[:], scale=pv_s[:, 0:1]).then_inc(og_ok, 1)
                if more:
                    act.wait_ge(h3_ok, i + 1)
                    relu2(i + 1)
                act.wait_ge(c3_mm, i * 2 + 4)
                act.wait_ge(stored, i * 32 + 32)
                for u in range(2):
                    A.activation(h0[:, :, u, :], conv_ps[:, u, 0:256].rearrange("p (a k) -> p a k", k=64), ACT.Identity,
                                 bias=bias3[:, 1:2], scale=bias3[:, 0:1]).then_inc(h0_ok, 1)
                act.wait_ge(h0_ok, i * 2 + 4)
                for u in range(2):
                    act.dma_start(ho[:, bass.ds(i, 1), :, u, :], h0[:, :, u, :].rearrange("p (o a) n -> p o a n", o=1)).then_inc(stored, 16)
            turns(act, TURNS, turn)
            act.wait_ge(stored, TURNS * 32 + 32)

        @block.tensor
        def _(pe):
            M = nc.tensor.matmul
            pe.sem_inc(c1_mm, 8)
            pe.wait_ge(pre, 120)
            pe.wait_ge(ident_ok, 3)
            pe.sem_inc(c3_mm, 2)

            def conv1(i):
                pe.wait_ge(x_in, i * 48 + 48)
                for c in range(8):
                    if c >= 2:
                        pe.wait_ge(c1_max, i * 8 + (c - 1))
                    M(conv_ps[:, c % 2, :], w1[:], xin[:, c * 512:(c + 1) * 512], start=True, stop=True).then_inc(c1_mm, 1)

            def conv2(i):
                pe.wait_ge(c1_max, i * 8 + 8)
                pe.wait_ge(a1_ok, i + 2)
                for pr in range(4):
                    if pr >= 2:
                        pe.wait_ge(c2_max, i * 4 + (pr - 1))
                    for t in range(3):
                        mm = M(conv_ps[:, pr % 2, :], w2[:, pr * 3 + t, :], a1r[:, t:t + L1], start=(t == 0), stop=(t == 2))
                    mm.then_inc(c2_mm, 1)
            conv1(0)
            conv2(0)

            def turn(i, more):
                pe.wait_ge(h2_ok, i + 2)
                hh = h2[:].rearrange("p a k -> p (a k)")
                M(qk_ps[:, 0, :], wq_s[:], hh, start=True, stop=True).then_inc(qk_mm, 1)
                M(qk_ps[:, 1, :], wk_s[:], hh, start=True, stop=True).then_inc(qk_mm, 1)
                for pr in range(4):
                    mm = M(v_ps[:, pr * 128:(pr + 1) * 128], h2[:, pr, :], wv_s[:], start=True, stop=True)
                mm.then_inc(v_mm, 1)
                pe.wait_ge(qk_ok, i * 2 + 2)
                for u in range(2):
                    for pr in range(4):
                        s = slice(pr * 128, (pr + 1) * 128)
                        mm = M(e_ps[:, u, s], q[32 * u:32 * u + 8, s], k[32 * u:32 * u + 8, s], start=True, stop=True)
                mm.then_inc(e_mm, 1)
                if more:
                    pe.wait_ge(h0_ok, i * 2 + 2)
                    conv1(i + 1)
                pe.wait_ge(soft, i * 2 + 2)
                for r in range(8):
                    mm = nc.tensor.transpose(pT_ps[:, r // 4, (r % 4) * 128:(r % 4 + 1) * 128], pn[:, r, :], ident[:])
                mm.then_inc(pT_mm, 1)
                pe.wait_ge(pT_ok, i * 2 + 2)
                pe.wait_ge(v_ok, i + 1)
                for u in range(2):
                    for pr in range(4):
                        mm = M(o_ps[64 * u:64 * u + 64, pr * 128:(pr + 1) * 128], vT[:, pr, 64 * u:64 * u + 64],
                               pT[:, u * 4 + pr, :], start=True, stop=True)
                mm.then_inc(o_mm, 1)
                if more:
                    conv2(i + 1)
                    pe.wait_ge(c2_max, i * 4 + 8)
                pe.wait_ge(h3_ok, i + 1)
                for u in range(2):
                    for t in range(4):
                        mm = M(conv_ps[:, u, 0:256], w3[:, u, t, :], h3[:, :, t:t + 127:2],
                               start=(t == 0), stop=(t == 3))
                    mm.then_inc(c3_mm, 1)
            turns(pe, TURNS, turn)


def lay_tokenizer(inp):
    g = lambda n: np.asarray(inp["L0_tok_" + n])
    w1, w2, w3 = g("w1"), g("w2"), g("w3")
    wc1 = np.zeros((96, 128), np.float32)
    for t in range(3):
        for b in range(8):
            wc1[32 * t + 2 * b:32 * t + 2 * b + 2, 16 * b:16 * b + 16] = w1[:, :, t].T
    wc2 = np.zeros((128, 12, 128), np.float32)
    for pr in range(4):
        for t in range(3):
            for u in range(2):
                b = 2 * pr + u
                wc2[16 * b:16 * b + 16, pr * 3 + t, 64 * u:64 * u + 64] = w2[:, :, t].T
    row = lambda n, r, parts: np.ascontiguousarray(np.broadcast_to(np.stack([np.tile(g("g" + n), r), np.tile(g("v" + n), r)]), (parts, 2, 128)))
    col = lambda n, r: np.stack([np.tile(g(a + n), r) for a in ("b", "m", "g", "be", "v")], axis=1)
    wq = np.zeros((128, 64), np.float32); wk = np.zeros((128, 64), np.float32); wv = np.zeros((128, 128), np.float32)
    bqk = np.zeros((64, 2), np.float32)
    for u in range(2):
        wq[64 * u:64 * u + 64, 32 * u:32 * u + 8] = g("wq").T
        wk[64 * u:64 * u + 64, 32 * u:32 * u + 8] = g("wk").T
        wv[64 * u:64 * u + 64, 64 * u:64 * u + 64] = g("wv").T
        bqk[32 * u:32 * u + 8, 0] = g("bq")
        bqk[32 * u:32 * u + 8, 1] = g("bk")
    pv = np.stack([np.broadcast_to(g("gamma"), (128,)), np.tile(g("bv"), 2)], axis=1)
    wc3 = np.zeros((128, 2, 4, 128), np.float32)
    for u in range(2):
        wc3[64 * u:64 * u + 64, u] = np.transpose(w3, (1, 2, 0))
    return dict(tk_wc1=wc1, tk_p1row=row("1", 8, 96), tk_p1col=col("1", 8), tk_wc2=wc2, tk_p2row=row("2", 2, 128),
                tk_p2col=col("2", 2), tk_wq=wq, tk_wk=wk, tk_bqk=bqk, tk_wv=wv, tk_pv=pv, tk_wc3=wc3, tk_p3col=col("3", 1))


D = 64
LN_EPS = 1e-5


def bc(t, shape):
    return t.rearrange("p (a o) -> p a o", o=1).to_broadcast(shape)


class LayerNorm:
    STEPS = 5

    def __init__(self, nc, sb, sem, G, copies=1, name="ln"):
        self.nc, self.G, self.copies = nc, G, copies
        self.x = sb(name + "_x", [128, G, D]); self.sq = sb(name + "_sq", [128, G, D])
        self.mu = sb(name + "_mu", [128, G]); self.var = sb(name + "_var", [128, G]); self.rstd = sb(name + "_rstd", [128, G])
        self.minus_half = sb(name + "_half", [128, G])
        self.out = sb(name + "_out", [128, G, copies, D])
        self.loaded, self.step, self.rs = sem(name + "_loaded"), sem(name + "_step"), sem(name + "_rs")

    def load(self, sp, turn, src):
        self.ready(sp, turn - 1)
        sp.dma_start(self.x[:], src).then_inc(self.loaded, 16)

    def start(self):
        self.nc.vector.memset(self.minus_half[:], -0.5).then_inc(self.step, 1)

    def vector(self, dve, turn, loaded=True):
        self.vector_first(dve, turn, loaded)
        self.vector_second(dve, turn)

    def vector_first(self, dve, turn, loaded=True):
        V, s, G = self.nc.vector, Steps(self.step, self.STEPS, turn), self.G
        wait = lambda n: dve.wait_ge(self.step, turn * self.STEPS + n + 1)
        if loaded:
            dve.wait_ge(self.loaded, turn * 16 + 16)
        s.did(V.tensor_reduce(self.mu[:], self.x[:], AX, ALU.add)); wait(1)
        s.did(V.tensor_scalar(self.mu[:], self.mu[:], 1.0 / D, None, ALU.mult)); wait(2)
        s.did(V.tensor_tensor(self.x[:], self.x[:], bc(self.mu[:], [128, G, D]), ALU.subtract)); wait(3)
        s.did(V.tensor_tensor(self.sq[:], self.x[:], self.x[:], ALU.mult)); wait(4)
        V.tensor_reduce(self.var[:], self.sq[:], AX, ALU.add).then_inc(self.rs, 1)
        dve.wait_ge(self.rs, turn * 3 + 1)
        V.tensor_scalar(self.var[:], self.var[:], 1.0 / D, LN_EPS, ALU.mult, ALU.add).then_inc(self.rs, 1)
        assert s.n == self.STEPS - 1

    def vector_second(self, dve, turn):
        V, G = self.nc.vector, self.G
        dve.wait_ge(self.rs, turn * 3 + 3)
        for c in range(self.copies - 1):
            V.tensor_tensor(self.out[:, :, c, :], self.x[:], bc(self.rstd[:], [128, G, D]), ALU.mult)
        V.tensor_tensor(self.out[:, :, self.copies - 1, :], self.x[:], bc(self.rstd[:], [128, G, D]), ALU.mult).then_inc(self.step, 1)

    def gpsimd(self, pool, turn):
        pool.wait_ge(self.rs, turn * 3 + 2)
        self.nc.gpsimd.tensor_tensor(self.rstd[:], self.var[:], self.minus_half[:], ALU.pow).then_inc(self.rs, 1)

    def ready(self, eng, turn):
        eng.wait_ge(self.step, turn * self.STEPS + self.STEPS + 1)


def make_identity(nc, pool, ident, sem, n=128):
    nc.gpsimd.memset(ident[:], 0.0).then_inc(sem, 1)
    pool.wait_ge(sem, 1)
    nc.gpsimd.affine_select(out=ident[:], in_=ident[:], compare_op=ALU.not_equal, fill=1.0, base=0,
                            pattern=[[-1, n]], channel_multiplier=1).then_inc(sem, 1)


class Split:
    PASSES = ((0, 0), (1, 0), (2, 1))

    @staticmethod
    def weights(nc, dve, go, parts, full, rest):
        V = nc.vector
        go(V.tensor_copy(parts[:, 0], full[:]))
        go(V.tensor_tensor(rest[:], full[:], parts[:, 0], ALU.subtract))
        go(V.tensor_copy(parts[:, 1], rest[:]))
        go(V.tensor_tensor(parts[0:64, 2], rest[0:64], parts[0:64, 1], ALU.subtract))
        go(V.tensor_copy(parts[64:128, 2], parts[64:128, 0]))

    @staticmethod
    def operand(nc, go, parts, full, rest):
        V = nc.vector
        go(V.tensor_tensor(rest[64:128], full[64:128], parts[64:128, 0], ALU.subtract))
        go(V.tensor_copy(parts[64:128, 0], rest[64:128]))
        return V.tensor_tensor(parts[64:128, 1], rest[64:128], parts[64:128, 0], ALU.subtract)


def turns_with_last(eng, n, body):
    body(None, 0, True)
    with eng.Fori(0, n - 2) as k:
        body(k, k + 1, True)
    body(n - 2, n - 1, False)


def linear_attention(nc, h_in, wq, we, h_out):
    B, T, _ = h_in.shape
    G, H = 4, 8
    TURNS = B // G
    with ExitStack() as ctx:
        sb = lambda n, s, d=F32: ctx.enter_context(nc.sbuf_tensor("las_" + n, s, d))
        pb = lambda n, s, d=F32: ctx.enter_context(nc.psum_tensor("lap_" + n, s, d))
        sem = ctx.enter_context(semaphores(nc, "lam_"))
        ln = LayerNorm(nc, sb, sem, G, copies=2)
        w_q = sb("wq", [128, H * 64]); w_e = sb("we", [128, H * 64])
        w_rest = sb("w_rest", [128, H * 64]); q_parts = sb("q_parts", [128, 3, H * 64], BF16); e_parts = sb("e_parts", [128, 3, H * 64], BF16)
        s_parts = sb("s_parts", [128, 2, G * 128], BF16); s_rest = sb("s_rest", [128, G * 128])
        w_st = sem("w_st"); first_ok = sem("first_ok"); split_st = sem("split_st"); split_ok = sem("split_ok")
        ident = sb("ident", [128, 128]); tri = sb("tri", [128, 128])
        res = sb("res", [128, G, D]); new = sb("new", [128, G, D])
        sT = sb("sT", [128, 2, G * 128]); qs = sb("qs", [128, 4, G * 128]); es = sb("es", [128, G, H * 64 + 64])
        om = sb("om", [128, 2, 2, 512])
        sT_ps = pb("sT", [128, 512]); ev_ps = pb("ev", [128, 2, 512]); om_ps = pb("om", [128, 2, 2, 512]); r_ps = pb("r", [128, G, 2 * D])
        w_in = sem("w_in"); const = sem("const"); tri_ok = sem("tri_ok"); zeroed = sem("zeroed"); res_in = sem("res_in"); stored = sem("stored")
        sT_mm = sem("sT_mm"); sT_ok = sem("sT_ok"); ev_mm = sem("ev_mm"); ev_ok = sem("ev_ok")
        om_mm = sem("om_mm"); om_ok = sem("om_ok"); r_mm = sem("r_mm"); new_ok = sem("new_ok")
        hi = h_in.rearrange("b t n -> t b n"); ho = h_out.rearrange("b t n -> t b n")
        block = ctx.enter_context(nc.Block())

        @block.sync
        def _(sp):
            sp.dma_start(w_q[:], wq).then_inc(w_in, 16)
            sp.dma_start(w_e[:], we).then_inc(w_in, 16)
            ln.load(sp, 0, hi[:, 0:G, :])

            def turn(i, more):
                if more:
                    ln.load(sp, i + 1, hi[:, bass.ds(i * G + G, G), :])
                sp.wait_ge(new_ok, i + 1)
                sp.dma_start(res[:], hi[:, bass.ds(i * G, G), :]).then_inc(res_in, 16)
            turns(sp, TURNS, turn)

        @block.gpsimd
        def _(pool):
            make_identity(nc, pool, ident, const)
            nc.gpsimd.memset(tri[:], 1.0).then_inc(tri_ok, 1)
            pool.wait_ge(tri_ok, 1)
            nc.gpsimd.affine_select(out=tri[:], in_=tri[:], compare_op=ALU.is_ge, fill=0.0, base=0,
                                    pattern=[[1, 128]], channel_multiplier=-1).then_inc(tri_ok, 1)
            ln.gpsimd(pool, 0)

            def turn(i, more):
                if more:
                    ln.gpsimd(pool, i + 1)
            turns(pool, TURNS, turn)

        @block.vector
        def _(dve):
            V = nc.vector
            ln.start()
            V.memset(sT[:], 0.0).then_inc(zeroed, 1)
            V.memset(es[:], 0.0).then_inc(zeroed, 1)
            dve.sem_inc(new_ok, 1)
            ln.vector(dve, 0)
            dve.wait_ge(w_in, 32)
            ws = Steps(w_st, None, None)
            Split.weights(nc, dve, lambda ins: ws.chain(dve, ins), q_parts, w_q, w_rest)
            Split.weights(nc, dve, lambda ins: ws.chain(dve, ins), e_parts, w_e, w_rest)
            dve.wait_ge(tri_ok, 2)

            def split(i):
                dve.wait_ge(first_ok, i + 1)
                cut = Steps(split_st, 2, i)
                Split.operand(nc, lambda ins: cut.chain(dve, ins), s_parts, sT[:, 1], s_rest).then_inc(split_ok, 1)
            split(0)

            def turn(i, more):
                if more:
                    dve.wait_ge(sT_mm, i + 1)
                    ln.vector(dve, i + 1)
                for b in range(G):
                    if b >= 2:
                        dve.wait_ge(r_mm, i * G + (b - 1))
                    dve.wait_ge(om_mm, i * G + (b + 1))
                    V.tensor_tensor(om[:, b % 2].rearrange("p u (h t) -> p (u h) t", t=128),
                                    om_ps[:, b % 2].rearrange("p u (h t) -> p (u h) t", t=128),
                                    tri[:].rearrange("p (o t) -> p o t", o=1).to_broadcast([128, 8, 128]), ALU.mult).then_inc(om_ok, 1)
                if more:
                    split(i + 1)
                dve.wait_ge(r_mm, i * G + G)
                dve.wait_ge(res_in, i * 16 + 16)
                dve.wait_ge(stored, i * 16 + 16)
                V.tensor_tensor(new[:], res[:], r_ps[:, :, 0:D], ALU.add).then_inc(new_ok, 1)
            turns(dve, TURNS, turn)

        @block.scalar
        def _(act):
            A = nc.scalar
            act.wait_ge(zeroed, 2)
            act.sem_inc(stored, 16)

            def transposed(i):
                act.wait_ge(sT_mm, i + 1)
                A.activation(sT[64:128, 1, :], sT_ps[64:128, :], ACT.Copy).then_inc(sT_ok, 1)
                act.wait_ge(sT_ok, i * 2 + 1)
                A.activation(s_parts[:, 0], sT_ps[:], ACT.Copy)
                A.activation(s_parts[0:64, 1], sT_ps[0:64], ACT.Copy).then_inc(first_ok, 1)
                A.activation(sT[0:64, 0, :], sT_ps[0:64, :], ACT.Copy).then_inc(sT_ok, 1)
            transposed(0)

            def store(i):
                act.wait_ge(new_ok, i + 2)
                act.dma_start(ho[:, bass.ds(i * G, G), :], new[:]).then_inc(stored, 16)

            def turn(before, i, more):
                for e in range(8):
                    if e == 4 and before is not None:
                        store(before)
                    act.wait_ge(ev_mm, i * 8 + (e + 1))
                    A.activation(qs[:, e, :] if e < 4 else es[:, e - 4, 0:H * 64], ev_ps[:, e % 2, :], ACT.Copy).then_inc(ev_ok, 1)
                if more:
                    transposed(i + 1)
            turns_with_last(act, TURNS, turn)
            store(TURNS - 1)
            act.wait_ge(stored, TURNS * 16 + 16)

        @block.tensor
        def _(pe):
            M = nc.tensor.matmul
            pe.wait_ge(w_in, 32)
            pe.wait_ge(const, 2)
            pe.wait_ge(zeroed, 2)
            pe.wait_ge(w_st, 10)

            def transpose(i):
                ln.ready(pe, i)
                for b in range(G):
                    mm = nc.tensor.transpose(sT_ps[:, b * 128:(b + 1) * 128], ln.out[:, b].rearrange("p c n -> p (c n)"), ident[:])
                mm.then_inc(sT_mm, 1)
            transpose(0)

            def turn(i, more):
                pe.wait_ge(sT_ok, i * 2 + 2)
                pe.wait_ge(split_ok, i + 1)
                for e in range(8):
                    if e >= 2:
                        pe.wait_ge(ev_ok, i * 8 + (e - 1))
                    if e < 4:
                        for n, (w, x) in enumerate(Split.PASSES):
                            mm = M(ev_ps[:, e % 2, :], q_parts[:, w, e * 128:(e + 1) * 128], s_parts[:, x, :], start=(n == 0), stop=(n == 2))
                    else:
                        b = e - 4
                        for n, (w, x) in enumerate(Split.PASSES):
                            mm = M(ev_ps[:, e % 2, :], s_parts[:, x, b * 128:(b + 1) * 128], e_parts[:, w, :], start=(n == 0), stop=(n == 2))
                    mm.then_inc(ev_mm, 1)
                def omega(b):
                    if b >= 2:
                        pe.wait_ge(om_ok, i * G + (b - 1))
                    s = slice(b * 128, (b + 1) * 128)
                    for u in range(2):
                        mm = M(om_ps[:, b % 2, u, :], sT[:, u, s], qs[:, :, s], start=True, stop=True)
                    mm.then_inc(om_mm, 1)

                def retrieve(b):
                    pe.wait_ge(om_ok, i * G + (b + 1))
                    if b == 0:
                        pe.wait_ge(ev_ok, i * 8 + 8)
                        pe.wait_ge(new_ok, i + 1)
                    for u in range(2):
                        for hp in range(4):
                            h = 2 * hp + u
                            mm = M(r_ps[:, b, :], om[:, b % 2, u, hp * 128:(hp + 1) * 128], es[:, b, h * 64:(h + 2) * 64],
                                   start=(u == 0 and hp == 0), stop=(u == 1 and hp == 3))
                    mm.then_inc(r_mm, 1)
                omega(0)
                omega(1)
                retrieve(0)
                omega(2)
                retrieve(1)
                omega(3)
                if more:
                    transpose(i + 1)
                retrieve(2)
                retrieve(3)
            turns(pe, TURNS, turn)


def lay_linear_attention(inp):
    Q, E = np.asarray(inp["L0_attn_Q"]), np.asarray(inp["L0_attn_E"])
    twice = lambda a: np.concatenate([a.reshape(64, 512)] * 2)
    return dict(la_wq=twice(np.transpose(Q, (1, 0, 2))), la_we=twice(np.transpose(E, (2, 0, 1))))


class Gate:
    STEPS = 12

    def __init__(self, nc, sb, sem, G, W):
        self.nc, self.G, self.W = nc, G, W
        self.logits = sb("gt_logits", [128, G, W]); self.top = sb("gt_top", [128, G, 8]); self.at = sb("gt_at", [128, G, 8], U32)
        self.atf = sb("gt_atf", [128, G, 2]); self.w = sb("gt_w", [128, G, 2]); self.e = sb("gt_e", [128, G]); self.pad = sb("gt_pad", [128, 1])
        self.iota = sb("gt_iota", [128, W]); self.one = sb("gt_one", [128, G, W]); self.gates = sb("gt_gates", [128, G, W])
        self.step, self.exp_ok, self.iota_ok = sem("gt_step"), sem("gt_exp"), sem("gt_iota")

    def start(self):
        self.nc.gpsimd.iota(self.iota[:], pattern=[[1, self.W]], base=0, channel_multiplier=0,
                            allow_small_or_imprecise_dtypes=True).then_inc(self.iota_ok, 1)

    def first(self, dve, turn):
        V, G = self.nc.vector, self.G
        base = turn * self.STEPS
        V.memset(self.pad[:], 0.0)
        for g in range(G):
            ins = V.max(self.top[:, g, :], self.logits[:, g, :])
        ins.then_inc(self.step, 1)
        dve.wait_ge(self.step, base + 1)
        V.memset(self.pad[:], 0.0)
        for g in range(G):
            ins = V.max_index(self.at[:, g, :], self.top[:, g, :], self.logits[:, g, :])
        ins.then_inc(self.step, 1)
        V.tensor_tensor(self.e[:], self.top[:, :, 1], self.top[:, :, 0], ALU.subtract).then_inc(self.step, 1)
        dve.wait_ge(self.step, base + 3)
        V.tensor_copy(self.atf[:], self.at[:, :, 0:2]).then_inc(self.step, 1)

    def scalar(self, act, turn):
        act.wait_ge(self.step, turn * self.STEPS + 3)
        self.nc.scalar.activation(self.e[:], self.e[:], ACT.Exp).then_inc(self.exp_ok, 1)

    def second(self, dve, turn):
        V, G, W = self.nc.vector, self.G, self.W
        base, n = turn * self.STEPS, 4

        def did(ins):
            nonlocal n
            n += 1
            ins.then_inc(self.step, 1)
            dve.wait_ge(self.step, base + n)
        dve.wait_ge(self.exp_ok, turn + 1)
        did(V.tensor_scalar(self.w[:, :, 0], self.e[:], 1.0, None, ALU.add))
        did(V.reciprocal(self.w[:, :, 0], self.w[:, :, 0]))
        did(V.tensor_tensor(self.w[:, :, 1], self.w[:, :, 0], self.e[:], ALU.mult))
        wide = [128, G, W]
        iota = self.iota[:].rearrange("p (o w) -> p o w", o=1).to_broadcast(wide)
        did(V.tensor_tensor(self.gates[:], iota, self.atf[:, :, 0:1].to_broadcast(wide), ALU.is_equal))
        did(V.tensor_tensor(self.gates[:], self.gates[:], self.w[:, :, 0:1].to_broadcast(wide), ALU.mult))
        did(V.tensor_tensor(self.one[:], iota, self.atf[:, :, 1:2].to_broadcast(wide), ALU.is_equal))
        did(V.tensor_tensor(self.one[:], self.one[:], self.w[:, :, 1:2].to_broadcast(wide), ALU.mult))
        V.tensor_tensor(self.gates[:], self.gates[:], self.one[:], ALU.add).then_inc(self.step, 1)
        n += 1
        assert n == self.STEPS

    def ready(self, eng, turn):
        eng.wait_ge(self.step, turn * self.STEPS + self.STEPS)


def experts16(nc, h_in, wg, gb, w1, b1, w2, b2, post, h_out):
    B, T, _ = h_in.shape
    G, E = 4, 16
    TURNS = B // G
    with ExitStack() as ctx:
        sb = lambda n, s, d=F32: ctx.enter_context(nc.sbuf_tensor("mos_" + n, s, d))
        pb = lambda n, s, d=F32: ctx.enter_context(nc.psum_tensor("mop_" + n, s, d))
        sem = ctx.enter_context(semaphores(nc, "mom_"))
        ln = LayerNorm(nc, sb, sem, G, copies=2)
        ln2 = LayerNorm(nc, sb, sem, G, name="ln2")
        gt = Gate(nc, sb, sem, G, E)
        wg_s = sb("wg", [128, 128]); gb_s = sb("gb", [128, E]); w1_s = sb("w1", [128, E * 128]); w1_rest = sb("w1_rest", [128, E * 128]); w1_parts = sb("w1_parts", [128, 3, E * 128], BF16); b1_s = sb("b1", [128, E])
        w2_s = sb("w2", [128, E * D + D]); b2_s = sb("b2", [64, G * D]); post_s = sb("post", [128, 2, D])
        ident = sb("ident", [128, 128])
        res = sb("res", [128, G, D]); new = sb("new", [128, G, D])
        sT = sb("sT", [128, G * 128]); s_rest = sb("s_rest", [128, G * 128]); s_next = sb("s_next", [128, 2, G * 128], BF16); s_parts = sb("s_parts", [128, 2, G * 128], BF16)
        first_ok = sem("first_ok"); split_st = sem("split_st"); split_ok = sem("split_ok"); s_ok = sem("s_ok"); w_st = sem("w_st"); hid = sb("hid", [128, 2, G * 128]); part = sb("part", [128, 2, G, D])
        gT = sb("gT", [64, 128])
        acc = sb("acc", [128, G, D])
        sT_ps = pb("sT", [128, 512]); g_ps = pb("g", [128, 512]); hid_ps = pb("hid", [128, 3, 512]); y_ps = pb("y", [128, 3, G, 2 * D])
        w_in = sem("w_in"); const = sem("const"); w2_pad = sem("w2_pad"); res_in = sem("res_in"); stored = sem("stored")
        sT_mm = sem("sT_mm"); sT_ok = sem("sT_ok"); lg_mm = sem("lg_mm"); lg_ok = sem("lg_ok")
        hid_mm = sem("hid_mm"); hid_ok = sem("hid_ok"); y_mm = sem("y_mm"); part_ok = sem("part_ok"); acc_ok = sem("acc_ok")
        gT_mm = sem("gT_mm"); gT_ok = sem("gT_ok"); b2_mm = sem("b2_mm"); fin = sem("fin"); parts_done = sem("parts_done"); new_st = sem("new_st"); new_ok = sem("new_ok")
        hi = h_in.rearrange("b t n -> t b n"); ho = h_out.rearrange("b t n -> t b n")
        loads = [(wg_s[:], wg), (gb_s[:], gb), (w1_s[:], w1), (b1_s[:], b1), (w2_s[:, 0:E * D], w2), (b2_s[:], b2), (post_s[:], post)]
        NB = E + 1
        block = ctx.enter_context(nc.Block())

        @block.sync
        def _(sp):
            for dst, src in loads:
                sp.dma_start(dst, src).then_inc(w_in, 16)
            sp.wait_ge(ln.step, 1)
            sp.dma_start(ln.x[:], hi[:, 0:G, :]).then_inc(ln.loaded, 16)

            def turn(i, more):
                if more:
                    ln.load(sp, i + 1, hi[:, bass.ds(i * G + G, G), :])
                sp.wait_ge(new_ok, i + 1)
                sp.dma_start(res[:], hi[:, bass.ds(i * G, G), :]).then_inc(res_in, 16)
            turns(sp, TURNS, turn)

        @block.gpsimd
        def _(pool):
            make_identity(nc, pool, ident, const)
            gt.start()
            ln.gpsimd(pool, 0)
            pool.sem_inc(acc_ok, 1)

            def turn(before, i, more):
                for e in range(NB):
                    pool.wait_ge(part_ok, i * NB + (e + 1))
                    pool.wait_ge(acc_ok, i * NB + (e + 1))
                    first = acc[:] if e else ln.out[:, :, 0, :]
                    if e == NB - 1:
                        pool.wait_ge(fin, i + 1)
                        nc.gpsimd.tensor_tensor(ln2.x[:], first, part[:, e % 2], ALU.add).then_inc(acc_ok, 1)
                    else:
                        nc.gpsimd.tensor_tensor(acc[:], first, part[:, e % 2], ALU.add).then_inc(acc_ok, 1)
                    if e == 2 and more:
                        ln.gpsimd(pool, i + 1)
                    if e == 6 and before is not None:
                        ln2.gpsimd(pool, before)
            turns_with_last(pool, TURNS, turn)
            ln2.gpsimd(pool, TURNS - 1)

        @block.vector
        def _(dve):
            V = nc.vector
            ln.start()
            ln2.start()
            V.memset(w2_s[:, E * D:], 0.0).then_inc(w2_pad, 1)
            dve.sem_inc(new_ok, 1)
            dve.sem_inc(fin, 1)
            dve.sem_inc(parts_done, 1)
            ln.vector(dve, 0)
            dve.wait_ge(w_in, 16 * len(loads))
            dve.wait_ge(gt.iota_ok, 1)

            ws = Steps(w_st, None, None)
            Split.weights(nc, dve, lambda ins: ws.chain(dve, ins), w1_parts, w1_s, w1_rest)

            def split(i):
                dve.wait_ge(first_ok, i + 1)
                st = Steps(split_st, 2, i)
                Split.operand(nc, lambda ins: st.chain(dve, ins), s_next, sT, s_rest).then_inc(split_ok, 1)
            split(0)

            def turn(before, i, more):
                dve.wait_ge(lg_mm, i + 1)
                V.tensor_tensor(gt.logits[:], sT_ps[:].rearrange("p (g n) -> p g n", g=G)[:, :, 0:E],
                                gb_s[:].rearrange("p (o e) -> p o e", o=1).to_broadcast([128, G, E]), ALU.add).then_inc(lg_ok, 1)
                dve.wait_ge(lg_ok, i + 1)
                gt.first(dve, i)
                gt.second(dve, i)
                gt.ready(dve, i)
                for e in range(NB):
                    dve.wait_ge(acc_ok, i * NB + max(e, 1))
                    if e < E:
                        dve.wait_ge(y_mm, i * E + (e + 1))
                        V.tensor_tensor(part[:, e % 2], y_ps[:, e % 3, :, 0:D], gt.gates[:, :, e:e + 1].to_broadcast([128, G, D]),
                                        ALU.mult).then_inc(part_ok, 1)
                    else:
                        dve.wait_ge(b2_mm, i + 1)
                        V.tensor_copy(part[:, e % 2], g_ps[:, 256:512].rearrange("p (g n) -> p g n", n=D)).then_inc(part_ok, 1)
                    if e == 3 and more:
                        ln.vector_first(dve, i + 1)
                    if e == 4 and more:
                        ln.vector_second(dve, i + 1)
                    if e == 7 and before is not None:
                        ln2.vector_first(dve, before, loaded=False)
                    if e == 8 and before is not None:
                        ln2.vector_second(dve, before)
                    if e == 9 and before is not None:
                        scale(before)
                    if e == 10 and before is not None:
                        residual(before)
                    if e == 11 and more:
                        split(i + 1)
                dve.wait_ge(part_ok, i * NB + NB)
                dve.sem_inc(parts_done, 1)

            def scale(i):
                ln2.ready(dve, i)
                y2 = ln2.out[:, :, 0, :]
                pr = lambda k: post_s[:, k:k + 1, :].to_broadcast([128, G, D])
                V.tensor_tensor(y2, y2, pr(0), ALU.mult).then_inc(fin, 1)
                dve.wait_ge(fin, i + 2)
                V.tensor_tensor(y2, y2, pr(1), ALU.add).then_inc(new_st, 1)

            def residual(i):
                dve.wait_ge(new_st, i + 1)
                dve.wait_ge(res_in, i * 16 + 16)
                dve.wait_ge(stored, i * 16 + 16)
                V.tensor_tensor(new[:], ln2.out[:, :, 0, :], res[:], ALU.add).then_inc(new_ok, 1)
            turns_with_last(dve, TURNS, turn)
            dve.wait_ge(acc_ok, TURNS * NB + 1)
            ln2.vector_first(dve, TURNS - 1, loaded=False)
            ln2.vector_second(dve, TURNS - 1)
            scale(TURNS - 1)
            residual(TURNS - 1)

        @block.scalar
        def _(act):
            A = nc.scalar
            act.sem_inc(stored, 16)
            act.wait_ge(w_in, 16 * len(loads))

            def transposed(i):
                act.wait_ge(sT_mm, i + 1)
                A.activation(sT[:], sT_ps[:], ACT.Copy).then_inc(sT_ok, 1)
                act.wait_ge(sT_ok, i + 1)
                A.activation(s_next[:, 0], sT[:], ACT.Copy)
                A.activation(s_next[0:64, 1], sT[0:64], ACT.Copy).then_inc(first_ok, 1)

            def handed(i):
                act.wait_ge(split_ok, i + 1)
                A.activation(s_parts[:], s_next[:], ACT.Copy).then_inc(s_ok, 1)

            def store(i):
                act.wait_ge(new_ok, i + 2)
                act.dma_start(ho[:, bass.ds(i * G, G), :], new[:]).then_inc(stored, 16)
            transposed(0)
            handed(0)

            def turn(before, i, more):
                for e in range(E):
                    act.wait_ge(hid_mm, i * E + (e + 1))
                    if e >= 2 or before is not None:
                        act.wait_ge(y_mm, i * E + (e - 1))
                    A.activation(hid[:, e % 2, :], hid_ps[:, e % 3, :], ACT.Relu, bias=b1_s[:, e:e + 1]).then_inc(hid_ok, 1)
                    if e == 0:
                        gt.scalar(act, i)
                    if e == 4:
                        act.wait_ge(gT_mm, i + 1)
                        A.activation(gT[:], g_ps[0:64, 64:192], ACT.Copy).then_inc(gT_ok, 1)
                    if e == 9 and more:
                        transposed(i + 1)
                    if e == 11 and before is not None:
                        store(before)
                if more:
                    handed(i + 1)
            turns_with_last(act, TURNS, turn)
            store(TURNS - 1)
            act.wait_ge(stored, TURNS * 16 + 16)

        @block.tensor
        def _(pe):
            M = nc.tensor.matmul
            pe.wait_ge(w_in, 16 * len(loads))
            pe.wait_ge(const, 2)
            pe.wait_ge(w2_pad, 1)
            pe.wait_ge(w_st, 5)

            def transpose(i):
                ln.ready(pe, i)
                if not isinstance(i, int) or i > 0:
                    pe.wait_ge(lg_ok, i)
                for b in range(G):
                    mm = nc.tensor.transpose(sT_ps[:, b * 128:(b + 1) * 128], ln.out[:, b].rearrange("p c n -> p (c n)"), ident[:])
                mm.then_inc(sT_mm, 1)

            def logits(i):
                pe.wait_ge(sT_ok, i + 1)
                for b in range(G):
                    mm = M(sT_ps[:, b * 128:(b + 1) * 128], sT[:, b * 128:(b + 1) * 128], wg_s[:], start=True, stop=True)
                mm.then_inc(lg_mm, 1)
            transpose(0)
            logits(0)

            def turn(i, more):
                def hidden(e):
                    if e >= 3:
                        pe.wait_ge(hid_ok, i * E + (e - 2))
                    if e == 0:
                        pe.wait_ge(s_ok, i + 1)
                    for n, (w, x) in enumerate(Split.PASSES):
                        mm = M(hid_ps[:, e % 3, :], w1_parts[:, w, e * 128:(e + 1) * 128], s_parts[:, x, :], start=(n == 0), stop=(n == 2))
                    mm.then_inc(hid_mm, 1)

                def output(e):
                    if e == 0:
                        pe.wait_ge(parts_done, i + 1)
                    pe.wait_ge(hid_ok, i * E + (e + 1))
                    if e >= 3:
                        pe.wait_ge(part_ok, i * NB + (e - 2))
                    for b in range(G):
                        mm = M(y_ps[:, e % 3, b, :], hid[:, e % 2, b * 128:(b + 1) * 128], w2_s[:, e * D:(e + 2) * D], start=True, stop=True)
                    mm.then_inc(y_mm, 1)
                hidden(0)
                hidden(1)
                for e in range(E):
                    if e == 3:
                        gt.ready(pe, i)
                    output(e)
                    if e + 2 < E:
                        hidden(e + 2)
                    if e == 3:
                        nc.tensor.transpose(g_ps[0:64, 64:192], gt.gates[:].rearrange("p g e -> p (g e)"), ident[:]).then_inc(gT_mm, 1)
                    if e == 6:
                        pe.wait_ge(gT_ok, i + 1)
                        M(g_ps[:, 256:512], gT[:], b2_s[:], start=True, stop=True).then_inc(b2_mm, 1)
                    if e == 8 and more:
                        transpose(i + 1)
                    if e == 10 and more:
                        logits(i + 1)
            turns(pe, TURNS, turn)


def lay_experts16(inp):
    g = lambda n: np.asarray(inp["L0_ffn_" + n])
    E, H, F = g("w1").shape
    w1 = np.tile(np.transpose(g("w1"), (1, 0, 2)).reshape(H, E * F), (2, 1))
    b2 = np.zeros((64, 256), np.float32)
    for b in range(4):
        b2[16 * b:16 * b + 16, 64 * b:64 * b + 64] = g("b2")
    return dict(mo_wg=np.pad(g("gate_w"), ((0, 64), (0, 128 - E))), mo_gb=np.broadcast_to(g("gate_b"), (128, E)),
                mo_w1=w1, mo_b1=g("b1").T, mo_w2=np.transpose(g("w2"), (1, 0, 2)).reshape(F, E * H), mo_b2=b2,
                mo_post=np.broadcast_to(np.stack([g("gamma"), g("beta")]), (128, 2, 64)))


RMS_EPS = 1.1920929e-07
MASKED = -1e30


class Turn:

    def __init__(self, base, loop=None):
        self.base, self.loop, self.parity = base, loop, base % 2

    def at(self, per, n=0):
        fixed = self.base * per + n
        return fixed if self.loop is None else self.loop * (2 * per) + fixed

    def __mul__(self, per):
        return self.at(per)

    def next(self):
        return Turn(self.base + 1, self.loop)


def rope_attention(nc, h_in, wq, wk, wv, wo, norms, cs_head, cs_tok, h_out):
    B, T, _ = h_in.shape
    G, H, U, LAG = 4, 16, 16, 2
    TURNS = B // G
    with ExitStack() as ctx:
        sb = lambda n, s, d=F32: ctx.enter_context(nc.sbuf_tensor("ras_" + n, s, d))
        pb = lambda n, s, d=F32: ctx.enter_context(nc.psum_tensor("rap_" + n, s, d))
        sem = ctx.enter_context(semaphores(nc, "ram_"))
        ln = LayerNorm(nc, sb, sem, G, copies=2)
        wq_s = sb("wq", [128, H * 64]); wk_s = sb("wk", [128, 128]); wv_s = sb("wv", [64, 128]); wo_s = sb("wo", [64, H * 64])
        wq_parts = sb("wq_parts", [128, 3, H * 64], BF16); wvo_parts = sb("wvo_parts", [128, 3, H * 64], BF16); w_rest = sb("w_rest", [128, H * 64])
        s_parts = sb("s_parts", [128, 2, 512], BF16); s_rest = sb("s_rest", [128, 512])
        wvo = sb("wvo", [128, H * 64]); nrm = sb("nrm", [128, 2, 64]); csh = sb("csh", [128, 2, 128]); cst = sb("cst", [128, 2, 64])
        ident = sb("ident", [128, 128]); identb = sb("identb", [128, 128], BF16); mask = sb("mask", [128, 512], BF16)
        sel = sb("sel", [128, 8, 16])
        res = sb("res", [128, G, D]); new = sb("new", [128, G, D])
        sT = sb("sT", [128, 512])
        sq = sb("sq", [128, 2, 512]); raw = sb("raw", [128, 2, 512]); sh = sb("sh", [128, 2, 512]); t1 = sb("t1", [128, 2, 512])
        ssq = sb("ssq", [16, 512]); kc = sb("kc", [128, G, 64]); ks = sb("ks", [128, G, 64]); kr = sb("kr", [128, G, 64])
        kv = sb("kv", [128, G]); minus_half = sb("minus_half", [128, H]); kn = sb("kn", [128, G, 2, 64])
        qr = sb("qr", [128, 2, 8, 512]); rq = sb("rq", [128, 2, G, H]); kz = sb("kz", [128, 2, G, 2, 128]); vwo = sb("vwo", [128, 2, G, H * 64 + 64])
        m4 = sb("m4", [128, 2, 4]); nm = sb("nm", [128, 2, 4]); sm = sb("sm", [128, 2, 4]); rs = sb("rs", [128, 2, 4])
        p = sb("p", [128, 2, 4, 128]); pn = sb("pn", [128, 2, 4, 128]); pT = sb("pT", [128, 2, 4, 128])
        sc_ps = pb("sc", [128, 2, 512]); pT_ps = pb("pT", [128, 2, 512]); y_ps = pb("y", [128, G, 2 * D])
        pj_ps = pb("pj", [128, 512]); ss_ps = pb("ss", [128, 512]); misc = pb("misc", [128, 512])

        w_in = sem("w_in"); const = sem("const"); mk = sem("mk"); sel_ok = sem("sel_ok"); pad_ok = sem("pad_ok"); wvo_mm = sem("wvo_mm"); wvo_ok = sem("wvo_ok")
        res_in = sem("res_in"); stored = sem("stored"); new_ok = sem("new_ok")
        sT_mm = sem("sT_mm"); sT_ok = sem("sT_ok"); first_ok = sem("first_ok"); split_st = sem("split_st"); split_ok = sem("split_ok"); w_st = sem("w_st"); k_mm = sem("k_mm"); pj_mm = sem("pj_mm"); sq_ok = sem("sq_ok")
        rot = sem("rot"); raw_ok = sem("raw_ok"); swapped = sem("swapped"); t1_ok = sem("t1_ok"); qr_ok = sem("qr_ok"); ss_mm = sem("ss_mm"); ss_ok = sem("ss_ok")
        rqT_mm = sem("rqT_mm"); rq_st = sem("rq_st"); rq_ok = sem("rq_ok"); k_st = sem("k_st"); k_pow = sem("k_pow"); kT_mm = sem("kT_mm"); kz_ok = sem("kz_ok")
        vw_mm = sem("vw_mm"); vw_a = sem("vw_a"); vw_v = sem("vw_v")
        sc_mm = sem("sc_mm"); mx_st = sem("mx_st"); exp_ok = sem("exp_ok"); rec_ok = sem("rec_ok"); pn_ok = sem("pn_ok")
        pT_mm = sem("pT_mm"); pT_ok = sem("pT_ok"); pv_mm = sem("pv_mm")
        hi = h_in.rearrange("b t n -> t b n"); ho = h_out.rearrange("b t n -> t b n")
        loads = [(wq_s, wq), (wk_s, wk), (wv_s, wv), (wo_s, wo), (nrm, norms), (csh, cs_head), (cst, cs_tok)]
        KST = 9
        VALUES_FIRST, VALUES_SECOND = {11: 0, 12: 1, 13: 3, 14: 4, 15: 6}, {12: 2, 14: 5, 15: 7}
        swap = [x ^ 1 for x in range(32)]
        four = lambda ap: ap.rearrange("p (g t) -> p g t", g=G)
        over = lambda ap, shape: ap.rearrange("p (o t) -> p o t", o=1).to_broadcast(shape)

        def schedule(eng, turn):
            turn(Turn(-1), False, True)
            turn(Turn(0), True, True)
            with eng.Fori(0, (TURNS - 2) // 2) as k:
                turn(Turn(1, k), True, True)
                turn(Turn(2, k), True, True)
            turn(Turn(TURNS - 1), True, False)

        def lagging(t, n):
            m = n - LAG
            return t.loop is not None or t.base * U + m >= 0, t.parity if m >= 0 else 1 - t.parity, (m % U) // 4, 4 * (m % 4)
        block = ctx.enter_context(nc.Block())

        @block.sync
        def _(sp):
            for dst, src in loads:
                sp.dma_start(dst[:], src).then_inc(w_in, 16)

            def turn(t, units, projections):
                if projections:
                    j = t.next()
                    sp.wait_ge(ln.step, j.at(ln.STEPS, 1))
                    sp.dma_start(ln.x[:], hi[:, bass.ds(j.at(G), G), :]).then_inc(ln.loaded, 16)
                if units:
                    sp.wait_ge(new_ok, t.at(1, 1))
                    sp.dma_start(res[:], hi[:, bass.ds(t.at(G), G), :]).then_inc(res_in, 16)
            schedule(sp, turn)

        @block.gpsimd
        def _(pool):
            P = nc.gpsimd
            make_identity(nc, pool, ident, const)
            P.memset(identb[:], 0.0).then_inc(mk, 1)
            P.memset(mask[:], 0.0).then_inc(mk, 1)
            pool.wait_ge(mk, 2)
            P.affine_select(out=identb[:], in_=identb[:], compare_op=ALU.not_equal, fill=1.0, base=0,
                            pattern=[[-1, 128]], channel_multiplier=1).then_inc(mk, 1)
            P.affine_select(out=mask[:].rearrange("p (g t) -> p g t", g=4), in_=mask[:].rearrange("p (g t) -> p g t", g=4),
                            compare_op=ALU.is_ge, fill=MASKED, base=0, pattern=[[0, 4], [-1, 128]], channel_multiplier=1).then_inc(mk, 1)
            pool.wait_ge(w_in, 16 * len(loads))

            def normalise(t, m):
                pool.wait_ge(rec_ok, t.at(U, m + 1))
                if t.loop is not None or t.base * U + m >= 2:
                    pool.wait_ge(pT_mm, t.at(U, m - 1))
                P.tensor_tensor(pn[:, m % 2], p[:, m % 2], bc(rs[:, m % 2, :], [128, 4, 128]), ALU.mult).then_inc(pn_ok, 1)

            def query_scale(t, b):
                pool.wait_ge(rq_st, t.at(1, 1))
                P.tensor_tensor(rq[:, t.parity, b], rq[:, t.parity, b], minus_half[:, 0:H], ALU.pow).then_inc(rq_ok, 1)

            def turn(t, units, projections):
                j = t.next()
                for n in range(U):
                    if t.loop is not None or t.base * U + n >= 1:
                        normalise(t, n - 1)
                    if projections and n == 0:
                        ln.gpsimd(pool, j)
                    if projections and n == 5:
                        pool.wait_ge(k_st, j.at(KST, 7))
                        P.tensor_tensor(kv[:], kv[:], minus_half[:, 0:G], ALU.pow).then_inc(k_pow, 1)
                    if projections and n in (14, 15):
                        query_scale(j, n - 14)
                    if units and n in (1, 3):
                        query_scale(t, 2 + n // 2)
                    if projections and 4 <= n < 12:
                        blk, s = n - 4, n % 2
                        pool.wait_ge(swapped, j.at(8, blk + 1))
                        P.tensor_tensor(four(sh[:, s, :]), four(sh[:, s, :]), over(csh[:, 1, :], [128, G, 128]), ALU.mult).then_inc(rot, 1)
                        pool.wait_ge(rot, j.at(8, blk + 1))
                        pool.wait_ge(t1_ok, j.at(8, blk + 1))
                        P.tensor_tensor(qr[:, j.parity, blk, :], sh[:, s, :], t1[:, s, :], ALU.add).then_inc(qr_ok, 1)
            schedule(pool, turn)
            normalise(Turn(TURNS), -1)

        @block.vector
        def _(dve):
            V = nc.vector
            ln.start()
            V.memset(sel[:], 0.0).then_inc(sel_ok, 1)
            V.memset(minus_half[:], -0.5).then_inc(sel_ok, 1)
            dve.wait_ge(sel_ok, 2)
            for u in range(2):
                for blk in range(8):
                    ins = V.memset(sel[64 * u:64 * u + 64, blk, 2 * blk + u:2 * blk + u + 1], 1.0)
            ins.then_inc(sel_ok, 1)
            V.memset(kz[:], 0.0).then_inc(pad_ok, 1)
            V.memset(vwo[:, :, :, H * 64:], 0.0).then_inc(pad_ok, 1)
            dve.wait_ge(w_in, 16 * len(loads))
            V.scalar_tensor_tensor(nrm[:, 0, :], nrm[:, 0, :], 0.125, nrm[:, 1, :], ALU.mult, ALU.mult).then_inc(pad_ok, 1)
            dve.sem_inc(new_ok, 1)
            dve.wait_ge(pad_ok, 3)
            ws = Steps(w_st, None, None)
            Split.weights(nc, dve, lambda ins: ws.chain(dve, ins), wq_parts, wq_s, w_rest)
            dve.wait_ge(wvo_ok, 2)
            Split.weights(nc, dve, lambda ins: ws.chain(dve, ins), wvo_parts, wvo, w_rest)

            def reciprocals(t, m):
                dve.wait_ge(exp_ok, t.at(U, m + 1))
                V.reciprocal(rs[:, m % 2, :], sm[:, m % 2, :]).then_inc(rec_ok, 1)

            def probabilities(t, m):
                dve.wait_ge(pT_mm, t.at(U, m + 1))
                if t.loop is not None or t.base * U + m >= 2:
                    dve.wait_ge(pv_mm, t.at(U, m - 1))
                V.tensor_copy(pT[:, m % 2], pT_ps[:, m % 2, :].rearrange("p (h t) -> p h t", t=128)).then_inc(pT_ok, 1)

            def sums(t):
                dve.wait_ge(pv_mm, t.at(U))
                dve.wait_ge(res_in, t.at(16))
                dve.wait_ge(stored, t.at(16))
                V.tensor_tensor(new[:], res[:], y_ps[:, :, 0:D], ALU.add).then_inc(new_ok, 1)

            def turn(t, units, projections):
                j = t.next()
                c = t.parity
                for n in range(U):
                    s = n % 2
                    some = t.loop is not None or t.base > 0
                    if n == LAG and some:
                        sums(t)
                    if projections and 4 <= n < 12:
                        blk, o = n - 4, n % 2
                        dve.wait_ge(raw_ok, j.at(8, blk + 1))
                        if blk >= 2:
                            dve.wait_ge(qr_ok, j.at(8, blk - 1))
                        V.tensor_tensor(four(t1[:, o, :]), four(raw[:, o, :]), over(csh[:, 0, :], [128, G, 128]), ALU.mult).then_inc(t1_ok, 1)
                        V.stream_shuffle(sh[:, o, :], raw[:, o, :], swap).then_inc(swapped, 1)
                    if lagging(t, n)[0]:
                        probabilities(t, n - LAG)
                    if some or (t.base == 0 and n >= 1):
                        reciprocals(t, n - 1)
                    if units:
                        dve.wait_ge(sc_mm, t.at(U, n + 1))
                        V.tensor_reduce(m4[:, s, :], sc_ps[:, s].rearrange("p (h t) -> p h t", t=128), AX, ALU.max).then_inc(mx_st, 1)
                        dve.wait_ge(mx_st, t.at(2 * U, 2 * n + 1))
                        b, h0 = n // 4, 4 * (n % 4)
                        if h0 == 0:
                            dve.wait_ge(rq_ok, t.at(G, b + 1))
                        V.scalar_tensor_tensor(nm[:, s, :], m4[:, s, :], -1.0, rq[:, c, b, h0:h0 + 4], ALU.mult, ALU.mult).then_inc(mx_st, 1)
                    if projections:
                        if n == 11:
                            dve.wait_ge(ss_mm, j.at(8, 8))
                            V.tensor_copy(ssq[:], ss_ps[0:16]).then_inc(ss_ok, 1)
                        if n in VALUES_SECOND:
                            k = VALUES_SECOND[n]
                            dve.wait_ge(vw_mm, j.at(8, k + 1))
                            V.tensor_copy(vwo[:, j.parity, k // 2, (k % 2) * 512:(k % 2 + 1) * 512], pj_ps[:]).then_inc(vw_v, 1)
                        if n == 0:
                            ln.vector_first(dve, j)
                        if n == 1:
                            ln.vector_second(dve, j)
                        if n == 2:
                            dve.wait_ge(first_ok, j.at(1, 1))
                            cut = Steps(split_st, 2, j)
                            Split.operand(nc, lambda ins: cut.chain(dve, ins), s_parts, sT, s_rest).then_inc(split_ok, 1)
                        if n == 4:
                            st = Steps(k_st, KST, j)
                            dve.wait_ge(k_mm, j.at(1, 1))
                            kp = misc[:].rearrange("p (g n) -> p g n", g=G)[:, :, 0:64]
                            st.did(V.tensor_tensor(kc[:], kp, over(cst[:, 0, :], [128, G, 64]), ALU.mult))
                            st.chain(dve, V.tensor_tensor(ks[:], kp, over(cst[:, 1, :], [128, G, 64]), ALU.mult))
                            pair = lambda x, o: x[:, :, o:64:2]
                            st.did(V.tensor_tensor(pair(kr, 0), pair(kc, 0), pair(ks, 1), ALU.subtract))
                            st.chain(dve, V.tensor_tensor(pair(kr, 1), pair(ks, 0), pair(kc, 1), ALU.add))
                            st.chain(dve, V.tensor_tensor(kc[:], kr[:], kr[:], ALU.mult))
                            st.chain(dve, V.tensor_reduce(kv[:], kc[:], AX, ALU.add))
                            st.did(V.tensor_scalar(kv[:], kv[:], 1.0 / 64, RMS_EPS, ALU.mult, ALU.add))
                        if n == 6:
                            dve.wait_ge(k_pow, j.at(1, 1))
                            st.chain(dve, V.tensor_tensor(kr[:], kr[:], bc(kv[:], [128, G, 64]), ALU.mult))
                            V.tensor_tensor(kn[:, :, 0, :], kr[:], over(nrm[:, 0, :], [128, G, 64]), ALU.mult)
                            st.did(V.tensor_tensor(kn[:, :, 1, :], kr[:], over(nrm[:, 0, :], [128, G, 64]), ALU.mult))
                            st.close()
                        if n == 13:
                            dve.wait_ge(rqT_mm, j.at(1, 1))
                            rqv = rq[:, j.parity].rearrange("p g h -> p (g h)")
                            V.tensor_scalar(rqv, ss_ps[:, 0:64], 1.0 / 64, RMS_EPS, ALU.mult, ALU.add).then_inc(rq_st, 1)
            schedule(dve, turn)
            end = Turn(TURNS)
            probabilities(end, -2)
            reciprocals(end, -1)
            probabilities(end, -1)
            sums(end)

        @block.scalar
        def _(act):
            A = nc.scalar
            act.sem_inc(stored, 16)
            act.wait_ge(pad_ok, 3)
            for half in range(2):
                act.wait_ge(wvo_mm, half + 1)
                A.activation(wvo[:, half * 512:(half + 1) * 512], pj_ps[:], ACT.Copy).then_inc(wvo_ok, 1)

            def store(t):
                act.wait_ge(new_ok, t.at(1, 1))
                act.dma_start(ho[:, bass.ds(t.at(G, -G), G), :], new[:]).then_inc(stored, 16)

            def turn(t, units, projections):
                j = t.next()

                for n in range(U):
                    s, b, h0 = n % 2, n // 4, 4 * (n % 4)
                    if projections:
                        if n == 2:
                            act.wait_ge(sT_mm, j.at(1, 1))
                            A.activation(sT[:], misc[:], ACT.Copy).then_inc(sT_ok, 1)
                            act.wait_ge(sT_ok, j.at(1, 1))
                            A.activation(s_parts[:, 0], sT[:], ACT.Copy)
                            A.activation(s_parts[0:64, 1], sT[0:64], ACT.Copy).then_inc(first_ok, 1)
                        if 3 <= n < 11:
                            blk, o = n - 3, (n - 3) % 2
                            act.wait_ge(pj_mm, j.at(8, blk + 1))
                            if blk >= 2:
                                act.wait_ge(ss_mm, j.at(8, blk - 1))
                                act.wait_ge(swapped, j.at(8, blk - 1))
                            A.activation(raw[:, o, :], pj_ps[:], ACT.Copy).then_inc(raw_ok, 1)
                            A.activation(sq[:, o, :], pj_ps[:], ACT.Square).then_inc(sq_ok, 1)
                        if n in VALUES_FIRST:
                            c = VALUES_FIRST[n]
                            act.wait_ge(vw_mm, j.at(8, c + 1))
                            A.activation(vwo[:, j.parity, c // 2, (c % 2) * 512:(c % 2 + 1) * 512], pj_ps[:], ACT.Copy).then_inc(vw_a, 1)
                    if units:
                        act.wait_ge(mx_st, t.at(2 * U, 2 * n + 2))
                        if t.loop is not None or t.base * U + n >= 2:
                            act.wait_ge(pn_ok, t.at(U, n - 1))
                        for h in range(4):
                            ins = A.activation(p[:, s, h, :], sc_ps[:, s, h * 128:(h + 1) * 128], ACT.Exp,
                                               bias=nm[:, s, h:h + 1], scale=rq[:, t.parity, b, h0 + h:h0 + h + 1],
                                               accum_out=sm[:, s, h:h + 1])
                        ins.then_inc(exp_ok, 1)
                    if projections:
                        if n == 13:
                            act.wait_ge(kT_mm, j.at(1, 1))
                            for u in range(2):
                                A.activation(kz[64 * u:64 * u + 64, j.parity, :, u, :], misc[64 * u:64 * u + 64, :].rearrange("p (g s) -> p g s", g=G),
                                             ACT.Copy).then_inc(kz_ok, 1)
                    if n == LAG and (t.loop is not None or t.base > 0):
                        store(t)
            schedule(act, turn)
            store(Turn(TURNS))
            act.wait_ge(stored, TURNS * 16 + 16)

        @block.tensor
        def _(pe):
            M, X = nc.tensor.matmul, nc.tensor.transpose
            pe.wait_ge(w_in, 16 * len(loads))
            pe.wait_ge(const, 2)
            pe.wait_ge(mk, 4)
            pe.wait_ge(sel_ok, 3)
            pe.wait_ge(pad_ok, 3)
            for half in range(2):
                if half:
                    pe.wait_ge(wvo_ok, 1)
                M(pj_ps[:], wv_s[:], wo_s[:, half * 512:(half + 1) * 512], start=True, stop=True).then_inc(wvo_mm, 1)
            pe.wait_ge(wvo_ok, 2)
            pe.wait_ge(w_st, 10)

            def product(out, weights, columns, operand, tokens, operand_stationary):
                for n, (w, x) in enumerate(Split.PASSES):
                    pair = weights[:, w, columns], operand[:, x, tokens]
                    mm = M(out, *(pair[::-1] if operand_stationary else pair), start=(n == 0), stop=(n == len(Split.PASSES) - 1))
                return mm

            def transpose_probabilities(t, n):
                m = n - LAG
                pe.wait_ge(pn_ok, t.at(U, m + 1))
                for h in range(4):
                    mm = X(pT_ps[:, m % 2, h * 128:(h + 1) * 128], pn[:, m % 2, h, :], ident[:])
                mm.then_inc(pT_mm, 1)

            def attend(t, n):
                m = n - LAG
                _, c, b, h0 = lagging(t, n)
                pe.wait_ge(pT_ok, t.at(U, m + 1))
                if m == 0:
                    pe.wait_ge(new_ok, t.at(1, 1))
                for hh in range(h0, h0 + 4):
                    mm = M(y_ps[:, b, :], pT[:, m % 2, hh - h0, :], vwo[:, c, b, hh * 64:(hh + 2) * 64], start=(hh == 0), stop=(hh == 15))
                mm.then_inc(pv_mm, 1)

            def turn(t, units, projections):
                j = t.next()

                def scores(n):
                    s, b, c = n % 2, n // 4, t.parity
                    if t.loop is not None or t.base * U + n >= 2:
                        pe.wait_ge(exp_ok, t.at(U, n - 1))
                    M(sc_ps[:, s, :], identb[:], mask[:], start=True, stop=False)
                    for k in range(2):
                        mm = M(sc_ps[:, s, k * 256:(k + 1) * 256], qr[:, c, 2 * (n % 4) + k, b * 128:(b + 1) * 128],
                               kz[:, c, b].rearrange("p u s -> p (u s)"), start=False, stop=(k == 1))
                    mm.then_inc(sc_mm, 1)

                def proj(blk):
                    if blk >= 1:
                        pe.wait_ge(sq_ok, j.at(8, blk))
                    else:
                        pe.wait_ge(split_ok, j.at(1, 1))
                    product(pj_ps[:], wq_parts, slice(blk * 128, (blk + 1) * 128), s_parts, slice(0, 512), False).then_inc(pj_mm, 1)

                def sumsq(blk):
                    pe.wait_ge(sq_ok, j.at(8, blk + 1))
                    M(ss_ps[0:16, :], sel[:, blk, :], sq[:, blk % 2, :], start=(blk == 0), stop=(blk == 7)).then_inc(ss_mm, 1)

                def values(c):
                    if c == 0:
                        pe.wait_ge(sq_ok, j.at(8, 8))
                    elif c - 1 in VALUES_FIRST.values():
                        pe.wait_ge(vw_a, j.at(5, 1 + sorted(VALUES_FIRST.values()).index(c - 1)))
                    else:
                        pe.wait_ge(vw_v, j.at(3, 1 + sorted(VALUES_SECOND.values()).index(c - 1)))
                    b = c // 2
                    product(pj_ps[:], wvo_parts, slice((c % 2) * 512, (c % 2 + 1) * 512), s_parts, slice(b * 128, (b + 1) * 128), True).then_inc(vw_mm, 1)

                def projections_first(n):
                    if n == 2:
                        ln.ready(pe, j)
                        for b in range(G):
                            mm = X(misc[:, b * 128:(b + 1) * 128], ln.out[:, b].rearrange("p c n -> p (c n)"), ident[:])
                        mm.then_inc(sT_mm, 1)
                    if n == 3:
                        pe.wait_ge(sT_ok, j.at(1, 1))
                        for b in range(G):
                            mm = M(misc[:, b * 128:(b + 1) * 128], sT[:, b * 128:(b + 1) * 128], wk_s[:], start=True, stop=True)
                        mm.then_inc(k_mm, 1)
                    if 4 <= n < 11:
                        proj(n - 3)
                    if n in VALUES_FIRST:
                        values(VALUES_FIRST[n])

                def projections_second(n):
                    if 3 <= n < 11:
                        sumsq(n - 3)
                    if n == 12:
                        pe.wait_ge(ss_ok, j.at(1, 1))
                    if n in VALUES_SECOND:
                        values(VALUES_SECOND[n])
                    if n == 12:
                        for b in range(G):
                            mm = X(ss_ps[:, b * 16:(b + 1) * 16], ssq[:, b * 128:(b + 1) * 128], ident[0:16, 0:16])
                        mm.then_inc(rqT_mm, 1)
                    if n == 13:
                        pe.wait_ge(k_st, j.at(KST, KST))
                        for b in range(G):
                            mm = X(misc[:, b * 128:(b + 1) * 128], kn[:, b].rearrange("p c n -> p (c n)"), ident[:])
                        mm.then_inc(kT_mm, 1)
                if units:
                    pe.wait_ge(kz_ok, t.at(2, 2))
                    pe.wait_ge(qr_ok, t.at(8, 8))
                    pe.wait_ge(rq_st, t.at(1, 1))
                for n in range(U):
                    if projections:
                        projections_first(n)
                    if lagging(t, n)[0]:
                        transpose_probabilities(t, n)
                    if projections and n == 3:
                        proj(0)
                    if units:
                        scores(n)
                    if projections:
                        projections_second(n)
                    if lagging(t, n)[0]:
                        attend(t, n)
            schedule(pe, turn)
            for n in range(LAG):
                transpose_probabilities(Turn(TURNS), n)
                attend(Turn(TURNS), n)


def lay_rope_attention(inp):
    g = lambda n: np.asarray(inp["L1_attn_" + n])
    wq, wkv, wo = g("wq"), g("wkv"), g("wo")
    T, d = 128, 64
    freqs = (10000.0 ** (-2.0 * np.arange(d // 2, dtype=np.float32) / d)).astype(np.float32)
    theta = np.arange(T, dtype=np.float32)[:, None] * freqs[None, :]
    cos, sin = np.repeat(np.cos(theta), 2, axis=1), np.repeat(np.sin(theta), 2, axis=1)
    signed = sin * np.tile(np.array([-1.0, 1.0], np.float32), 32)
    csh = np.stack([np.tile(cos.T, (2, 1)), np.tile(signed.T, (2, 1))], axis=1).astype(np.float32)
    cst = np.stack([cos, sin], axis=1).astype(np.float32)
    wv = wkv[64:128]
    return dict(ra_wq=np.concatenate([wq.T, wq.T]), ra_wk=np.pad(wkv[0:64].T, ((0, 64), (0, 64))), ra_wv=np.concatenate([wv, wv], axis=1),
                ra_wo=np.transpose(wo.reshape(64, 16, 64), (2, 1, 0)).reshape(64, 1024),
                ra_norms=np.broadcast_to(np.stack([g("q_norm_w"), g("k_norm_w")]), (128, 2, 64)), ra_csh=csh, ra_cst=cst)


NODE_BITS = 14
SELF_BIT = 14
DST_SHIFT = 15
KEY_BIT = 29
LIVE_BIT = 20


HALO = 128


def exchange_steps(bits, cols, whole):
    out = []
    for k in (range(1, bits + 1) if whole else [bits]):
        if whole:
            out.append(("flip", k - 1))
        if k > cols:
            change = "cross" if whole and k - cols <= 5 else "turn"
            out.append((change, None))
            out += [("swap", 1 << (j - cols)) for j in range(k - 1, cols - 1, -1)]
            out.append((change, None))
        out += [("swap", 1 << j) for j in range(min(k, cols) - 1, -1, -1)]
    return out


class KeySort:

    def __init__(self, nc, edges, sb, sem):
        self.nc, self.edges = nc, edges
        self.tiles = [sb("big0", [128, 2048]), sb("big1", [128, 2048])]
        self.pid = sb("pid", [128, 1], I32); self.bit = sb("bit", [128, 8], I32)
        self.sgn = sb("sgn", [128, 8]); self.flips = sb("flips", [128, 7])
        self.loaded, self.pid_ok = sem("loaded"), sem("pid_ok")
        self.done = Steps(sem("done"), None, None)
        self.steps = exchange_steps(18, 11, True)
        self.next = self.at = 0

    def load(self, sp):
        for tile, row in ((0, 1), (1, 0)):
            sp.dma_start(self.tiles[tile][:].bitcast(I32), self.edges[row, :].rearrange("(p c) -> p c", p=128)).then_inc(self.loaded, 16)

    def gpsimd(self):
        self.nc.gpsimd.iota(self.pid[:], pattern=[[0, 1]], base=0, channel_multiplier=1).then_inc(self.pid_ok, 1)

    def start(self, dve):
        V, go = self.nc.vector, lambda ins: self.done.chain(dve, ins)
        dve.wait_ge(self.pid_ok, 1)
        for b in range(8):
            go(V.tensor_scalar(self.bit[:, b:b + 1], self.pid[:], b, 1, ALU.logical_shift_right, ALU.bitwise_and))
        go(V.tensor_copy(self.sgn[:], self.bit[:]))
        go(V.tensor_scalar(self.sgn[:], self.sgn[:], -2.0, 1.0, ALU.mult, ALU.add))
        go(V.tensor_tensor(self.flips[:], self.sgn[:, 0:7], self.sgn[:, 1:8], ALU.mult))
        dve.wait_ge(self.loaded, 32)
        dst, src = (t[:].bitcast(I32) for t in self.tiles)
        go(V.tensor_scalar(dst, dst, DST_SHIFT, (1 << KEY_BIT) | (1 << SELF_BIT), ALU.logical_shift_left, ALU.bitwise_or))
        go(V.tensor_tensor(dst, dst, src, ALU.bitwise_or))

    def exchange(self, dve, kind, arg, t, d):
        V, s, go = self.nc.vector, self.done, lambda ins: self.done.chain(dve, ins)
        if kind == "flip":
            if arg == 0:
                v = t[:].rearrange("p (a y b) -> p a y b", y=2, b=2)
                go(V.tensor_scalar(v[:, :, 1, :], v[:, :, 1, :], -1.0, None, ALU.mult))
            elif arg < 10:
                v = t[:].rearrange("p (a y b) -> p a y b", y=4, b=1 << arg)
                s.did(V.tensor_scalar(v[:, :, 1, :], v[:, :, 1, :], -1.0, None, ALU.mult))
                go(V.tensor_scalar(v[:, :, 2, :], v[:, :, 2, :], -1.0, None, ALU.mult))
            elif arg == 10:
                s.did(V.tensor_scalar(t[:, 0:1024], t[:, 0:1024], self.sgn[:, 0:1], None, ALU.mult))
                go(V.tensor_scalar(t[:, 1024:2048], t[:, 1024:2048], self.sgn[:, 0:1], -1.0, ALU.mult, ALU.mult))
            else:
                go(V.tensor_scalar(t[:], t[:], self.flips[:, arg - 11:arg - 10], None, ALU.mult))
        elif kind == "cross":
            go(V.transpose(d[:], t[:]))
        else:
            a = t[:].rearrange("p (a y b) -> p a y b", y=2, b=arg)
            z = d[:].rearrange("p (a y b) -> p a y b", y=2, b=arg)
            s.did(V.tensor_tensor(z[:, :, 0, :], a[:, :, 0, :], a[:, :, 1, :], ALU.min))
            go(V.tensor_tensor(z[:, :, 1, :], a[:, :, 0, :], a[:, :, 1, :], ALU.max))

    def advance(self, dve, count):
        for kind, arg in self.steps[self.next:self.next + count]:
            if kind == "turn":
                return
            self.exchange(dve, kind, arg, self.tiles[self.at], self.tiles[1 - self.at])
            self.next += 1
            if kind != "flip":
                self.at = 1 - self.at


def sort_edges(nc, sorter, edges, srt, src_out, start_out, lead_out, route):
    E = edges.shape[1]
    NODES = 1 << NODE_BITS
    TOTAL = E + NODES
    C = TOTAL // 128
    CH = C + HALO
    with ExitStack() as ctx:
        sb = lambda n, s, d=F32: ctx.enter_context(nc.sbuf_tensor("sos_" + n, s, d))
        pb = lambda n, s, d=F32: ctx.enter_context(nc.psum_tensor("sop_" + n, s, d))
        sem = ctx.enter_context(semaphores(nc, "som_"))
        big = sorter.tiles
        small = [sb("small0", [128, 128]), sb("small1", [128, 128])]
        ident = sb("ident", [128, 128])
        own = sb("own", [128, 128], I32); tail = sb("tail", [128, 128])
        keys = sb("keys", [128, CH + 1], I32); tmp = sb("tmp", [128, CH], I32); tmp2 = sb("tmp2", [128, CH], I32)
        dist = sb("dist", [128, CH], I32)
        posn = sb("posn", [128, CH], I32)
        fl = sb("fl", [128, C]); fl2 = sb("fl2", [128, C]); lead = sb("lead", [128, 1])
        stop = sb("stop", [1, HALO + 1], I32)
        ps = pb("ps", [128, 4, 512])
        ident_ok = sem("ident_ok"); consts = sem("consts")
        turn_src = sem("turn_src"); turn_mm = sem("turn_mm"); turn_a = sem("turn_a")
        a_out = sem("a_out"); tail_in = sem("tail_in"); lo_ok = sem("lo_ok"); lo_out = sem("lo_out"); l_in = sem("l_in")
        fin_ok = sem("fin_ok"); s_out = sem("s_out"); k_in = sem("k_in"); o_ok = sem("o_ok"); outs = sem("outs")
        srt_f = srt.bitcast(F32)
        rows = lambda ap, n: ap.rearrange("(p c) -> p c", p=n)
        MERGE = exchange_steps(18, 11, False)
        MERGE_TAIL = exchange_steps(14, 7, False)
        runs = [(sorter.steps[sorter.next:], big, 16, sorter.at), (MERGE, big, 16, 0), (MERGE_TAIL, small, 1, 0)]
        ends_in = [(at + sum(1 for kind, _ in steps if kind != "flip")) % 2 for steps, _, _, at in runs]
        block = ctx.enter_context(nc.Block())

        def each_turn():
            n = 0
            for steps, tiles, nb, at in runs:
                for kind, _ in steps:
                    if kind == "turn":
                        yield n, tiles[at], tiles[1 - at], nb
                        n += 1
                    if kind != "flip":
                        at = 1 - at

        @block.sync
        def _(sp):
            sp.wait_ge(fin_ok, 1)
            sp.dma_start(rows(srt_f[0:E], 128), big[ends_in[0]][:]).then_inc(a_out, 16)
            sp.wait_ge(a_out, 16)
            sp.dma_start(tail[:], rows(srt_f[E - NODES:E], 128)).then_inc(tail_in, 16)
            sp.wait_ge(lo_ok, 2)
            sp.dma_start(rows(srt_f[E - NODES:E], 128), small[1][:]).then_inc(lo_out, 16)
            sp.wait_ge(lo_out, 16)
            sp.dma_start(big[0][:], rows(srt_f[0:E], 128)).then_inc(l_in, 16)
            sp.wait_ge(fin_ok, 2)
            sp.dma_start(rows(srt_f[0:E], 128), big[ends_in[1]][:]).then_inc(s_out, 16)
            sp.wait_ge(fin_ok, 3)
            sp.dma_start(rows(srt_f[E:TOTAL], 128), small[ends_in[2]][:]).then_inc(s_out, 16)
            sp.wait_ge(consts, 2)
            sp.dma_start(rows(srt[TOTAL:TOTAL + HALO + 1], 1), stop[:]).then_inc(s_out, 16)
            sp.wait_ge(s_out, 48)
            sp.dma_start(keys[0:127, :], bass.AP(srt.tensor, srt.offset, [[C, 127], [1, CH + 1]])).then_inc(k_in, 16)
            sp.dma_start(keys[127:128, :], rows(srt[127 * C:127 * C + CH + 1], 1)).then_inc(k_in, 16)
            sp.wait_ge(o_ok, 1)
            sp.dma_start(src_out.bitcast(I32), tmp2[:, 0:C]).then_inc(outs, 16)
            sp.wait_ge(o_ok, 2)
            sp.dma_start(start_out, fl[:]).then_inc(outs, 16)
            sp.wait_ge(o_ok, 3)
            sp.dma_start(lead_out, lead[:]).then_inc(outs, 16)
            sp.wait_ge(outs, 48)

        @block.gpsimd
        def _(pool):
            P = nc.gpsimd
            make_identity(nc, pool, ident, ident_ok)
            P.iota(own[:], pattern=[[-1, 128]], base=NODES - 1, channel_multiplier=-128).then_inc(consts, 1)
            P.memset(stop[:, 1:], (1 << KEY_BIT) | (1 << SELF_BIT))
            P.memset(stop[:, 0:1], 1 << KEY_BIT).then_inc(consts, 1)
            P.iota(posn[:], pattern=[[1, CH]], base=0, channel_multiplier=C).then_inc(consts, 1)

        @block.tensor
        def _(pe):
            pe.wait_ge(ident_ok, 2)
            for n, src, dst, nb in each_turn():
                pe.wait_ge(turn_src, n + 1)
                for c in range(nb):
                    mm = nc.tensor.transpose(ps[:, c // 4, (c % 4) * 128:(c % 4 + 1) * 128], src[:, c * 128:(c + 1) * 128], ident[:])
                mm.then_inc(turn_mm, 1)

        @block.scalar
        def _(act):
            for n, src, dst, nb in each_turn():
                act.wait_ge(turn_mm, n + 1)
                if nb == 1:
                    nc.scalar.activation(dst[:], ps[:, 0, 0:128], ACT.Copy).then_inc(turn_a, 1)
                else:
                    nc.scalar.activation(dst[:, 0:1024], ps[:, 0:2, :].rearrange("p a k -> p (a k)"), ACT.Copy).then_inc(turn_a, 1)

        @block.vector
        def _(dve):
            V = nc.vector
            s = sorter.done
            go = lambda ins: s.chain(dve, ins)
            dve.wait_ge(consts, 3)
            turn_no = 0
            for r, (steps, tiles, nb, at) in enumerate(runs):
                if r == 1:
                    go(V.tensor_scalar(tmp[:, 0:128], own[:], DST_SHIFT, 1 << KEY_BIT, ALU.logical_shift_left, ALU.bitwise_or))
                    go(V.tensor_tensor(own[:], own[:], tmp[:, 0:128], ALU.bitwise_or))
                    dve.wait_ge(tail_in, 16)
                    V.tensor_tensor(small[0][:], tail[:], own[:].bitcast(F32), ALU.max).then_inc(lo_ok, 1)
                    V.tensor_tensor(small[1][:], tail[:], own[:].bitcast(F32), ALU.min).then_inc(lo_ok, 1)
                    dve.wait_ge(lo_ok, 2)
                    dve.wait_ge(l_in, 16)
                for kind, arg in steps:
                    t, d = tiles[at], tiles[1 - at]
                    if kind == "turn":
                        dve.sem_inc(turn_src, 1)
                        turn_no += 1
                        if nb > 1:
                            dve.wait_ge(turn_mm, turn_no)
                            go(V.tensor_copy(d[:, 1024:2048], ps[:, 2:4, :].rearrange("p a k -> p (a k)")))
                        dve.wait_ge(turn_a, turn_no)
                    else:
                        sorter.exchange(dve, kind, arg, t, d)
                    if kind != "flip":
                        at = 1 - at
                assert at == ends_in[r]
                dve.sem_inc(fin_ok, 1)
            dve.wait_ge(k_in, 32)
            V.tensor_scalar(tmp2[:, 0:C], keys[:, 0:C], NODES - 1, None, ALU.bitwise_and).then_inc(o_ok, 1)
            go(V.tensor_scalar(tmp[:], keys[:, 0:CH], SELF_BIT, 1, ALU.logical_shift_right, ALU.bitwise_and))
            go(V.tensor_scalar(tmp[:], tmp[:], 1, None, ALU.bitwise_xor))
            V.tensor_copy(fl[:], tmp[:, 0:C]).then_inc(o_ok, 1)
            dve.wait_ge(o_ok, 2)
            go(V.tensor_tensor_scan(fl2[:], fl[:], fl[:], 0.0, ALU.max, ALU.max))
            go(V.tensor_reduce(lead[:], fl2[:], AX, ALU.add))
            V.tensor_scalar(lead[:], lead[:], -1.0, float(C), ALU.mult, ALU.add).then_inc(o_ok, 1)
            go(V.tensor_scalar(tmp[:], keys[:, 1:CH + 1], SELF_BIT, 1, ALU.logical_shift_right, ALU.bitwise_and))
            go(V.tensor_scalar(dist[:], keys[:, 0:CH], DST_SHIFT, NODES - 1, ALU.logical_shift_right, ALU.bitwise_and))
            go(V.tensor_tensor(dist[:], posn[:], dist[:], ALU.subtract))
            go(V.tensor_scalar(dist[:], dist[:], float(1 << LIVE_BIT), None, ALU.add))
            go(V.tensor_scalar(tmp[:], tmp[:], -1.0, None, ALU.add))
            go(V.tensor_tensor(route[:], dist[:], tmp[:], ALU.bitwise_and))


LOWEST = -3.0e38
ROW = 24


def node_table(nc, h_in, wg, att, table, sT_out):
    B, T, _ = h_in.shape
    G = 8
    TURNS = B // G
    with ExitStack() as ctx:
        sb = lambda n, s, d=F32: ctx.enter_context(nc.sbuf_tensor("nts_" + n, s, d))
        pb = lambda n, s, d=F32: ctx.enter_context(nc.psum_tensor("ntp_" + n, s, d))
        sem = ctx.enter_context(semaphores(nc, "ntm_"))
        ln = LayerNorm(nc, sb, sem, G, copies=2)
        w = sb("w", [128, 128]); a = sb("a", [128, 2, 16]); prod = sb("prod", [128, 2, 16])
        ident = sb("ident", [128, 128]); sT = sb("sT", [128, 2, 512]); t = sb("t", [128, G, ROW])
        sT_ps = pb("sT", [128, 2, 512]); t_ps = pb("t", [128, G, 128])
        w_in = sem("w_in"); const = sem("const"); w_ok = sem("w_ok"); sT_mm = sem("sT_mm"); sT_ok = sem("sT_ok"); t_mm = sem("t_mm"); t_ok = sem("t_ok")
        out_s = sem("out_s"); out_t = sem("out_t")
        hi = h_in.rearrange("b t n -> t b n"); to = table.rearrange("(b t) n -> t b n", t=T)
        block = ctx.enter_context(nc.Block())

        @block.sync
        def _(sp):
            sp.wait_ge(w_ok, 1)
            sp.dma_start(w[:, 0:16], wg).then_inc(w_in, 16)
            sp.dma_start(a[:], att).then_inc(w_in, 16)
            sp.wait_ge(ln.step, 1)
            sp.dma_start(ln.x[:], hi[:, 0:G, :]).then_inc(ln.loaded, 16)

            def turn(i, more):
                if more:
                    ln.load(sp, i + 1, hi[:, bass.ds(i * G + G, G), :])
                sp.wait_ge(sT_ok, i + 2)
                sp.dma_start(sT_out[:, bass.ds(i * 1024, 1024)], sT[:].rearrange("p a n -> p (a n)")).then_inc(out_s, 16)
                sp.wait_ge(t_ok, i + 2)
                sp.dma_start(to[:, bass.ds(i * G, G), :], t[:]).then_inc(out_t, 16)
            turns(sp, TURNS, turn)
            sp.wait_ge(out_s, TURNS * 16 + 16)
            sp.wait_ge(out_t, TURNS * 16 + 16)

        @block.gpsimd
        def _(pool):
            make_identity(nc, pool, ident, const)
            ln.gpsimd(pool, 0)

            def turn(i, more):
                if more:
                    ln.gpsimd(pool, i + 1)
            turns(pool, TURNS, turn)

        @block.vector
        def _(dve):
            V = nc.vector
            ln.start()
            V.memset(w[:], 0.0).then_inc(w_ok, 1)
            dve.wait_ge(w_in, 32)
            V.tensor_tensor(prod[:], a[:], w[:, 0:16].rearrange("p (o e) -> p o e", o=1).to_broadcast([128, 2, 16]), ALU.mult).then_inc(w_ok, 1)
            dve.wait_ge(w_ok, 2)
            V.tensor_reduce(w[:, 16:24].rearrange("p (a h) -> p a h", a=2), prod[:].rearrange("p a (h e) -> p a h e", e=4), AX, ALU.add).then_inc(w_ok, 1)
            ln.vector(dve, 0)
            dve.sem_inc(t_ok, 1)

            def turn(i, more):
                if more:
                    ln.vector_first(dve, i + 1)
                    dve.wait_ge(sT_mm, i + 1)
                    ln.vector_second(dve, i + 1)
                dve.wait_ge(t_mm, i + 1)
                dve.wait_ge(out_t, i * 16 + 16)
                V.tensor_copy(t[:], t_ps[:, :, 0:ROW]).then_inc(t_ok, 1)
            turns(dve, TURNS, turn)

        @block.scalar
        def _(act):
            act.sem_inc(out_s, 16)
            act.sem_inc(out_t, 16)
            act.sem_inc(sT_ok, 1)

            def turn(i, more):
                act.wait_ge(sT_mm, i + 1)
                act.wait_ge(out_s, i * 16 + 16)
                act.wait_ge(t_ok, i + 1)
                nc.scalar.activation(sT[:], sT_ps[:], ACT.Copy).then_inc(sT_ok, 1)
            turns(act, TURNS, turn)

        @block.tensor
        def _(pe):
            pe.wait_ge(const, 2)
            pe.wait_ge(w_ok, 3)

            def turn(i, more):
                ln.ready(pe, i)
                for b in range(G):
                    mm = nc.tensor.transpose(sT_ps[:, b // 4, (b % 4) * 128:(b % 4 + 1) * 128], ln.out[:, b].rearrange("p c n -> p (c n)"), ident[:])
                mm.then_inc(sT_mm, 1)
                pe.wait_ge(sT_ok, i + 2)
                pe.wait_ge(t_ok, i + 1)
                for b in range(G):
                    mm = nc.tensor.matmul(t_ps[:, b, :], sT[:, b // 4, (b % 4) * 128:(b % 4 + 1) * 128], w[:], start=True, stop=True)
                mm.then_inc(t_mm, 1)
            turns(pe, TURNS, turn)


def edge_softmax(nc, table, src, start, lead_in, route, comp, srt, seg, post, iota_in, gates_out):
    C = src.shape[1]
    N = 34
    TURNS = C // (2 * N)
    F = 24
    B = 128
    MOVES = [(0, 1), (2, 3), (4, 5), (6,), (7, 8), (9, 10), (11, 12), (13, 14), (15, 16), (17, 18)]
    ANEW = 3 * 4
    with ExitStack() as ctx:
        sb = lambda n, s, d=F32: ctx.enter_context(nc.sbuf_tensor("ess_" + n, s, d))
        pb = lambda n, s, d=F32: ctx.enter_context(nc.psum_tensor("esp_" + n, s, d))
        sem = ctx.enter_context(semaphores(nc, "esm_"))
        idx = sb("idx", [128, 2, N], U32); st = sb("st", [128, 2, N])
        keep = sb("keep", [128, N]); neg = sb("neg", [128, N])
        g = sb("g", [128, 2, N, ROW])
        adm = sb("adm", [128, N, 4]); ad = sb("ad", [128, 2, N, 4]); e = sb("e", [128, N, 4]); el = sb("el", [128, N, 4])
        mx = sb("mx", [128, 2, N + 1, 4]); x = sb("x", [128, 2, N, 4]); xe = sb("xe", [128, 2, N, 4])
        v = sb("v", [128, N, 16]); r = sb("r", [128, 2, N, F])
        fidx = sb("fidx", [128, 1], I32); frow = sb("frow", [128, ROW]); dummy = sb("dummy", [128, 1]); dummy2 = sb("dummy2", [128, 1]); poked = sem("poked")
        ident = sb("ident", [128, 128])
        tot = sb("tot", [128, 3, 20]); tt = sb("tt", [20, 3, 128]); cm = sb("cm", [20, B + 1]); cs = sb("cs", [20, B + 1])
        ca = sb("ca", [20, 128]); cb = sb("cb", [20, 128]); ct = sb("ct", [128, 40])
        lead = sb("lead", [128, 1]); rowbase = sb("rowbase", [128, 1], I32); at = sb("at", [128, 1]); lead_at = sb("lead_at", [128, 1], U32)
        some = sb("some", [128, 1]); none = sb("none", [128, 1]); own = sb("own", [128, F]); joined = sb("joined", [128, F]); w2 = sb("w2", [128, 2, 4])
        endi = sb("endi", [128, B], I32); node = sb("node", [128, B], I32); tmp = sb("tmp", [128, C + HALO], I32); place = sb("place", [128, C]); square_ps = pb("square", [128, 5, 512])
        c_ok = sem("c_ok"); c_out = sem("c_out"); c_in = sem("c_in"); cT_mm = sem("cT_mm"); end_ok = sem("end_ok"); q = sb("q", [128, B, F]); sq = sb("sq", [128, B, 16])
        m2 = sb("m2", [128, B, 4]); mu = sb("mu", [128, B]); var = sb("var", [128, B])
        post_s = sb("post", [128, 3, 16]); sc = sb("sc", [128, B, 4])
        down = sb("down", [128, 4]); one = sb("one", [128, 2, B, 4]); top = sb("top", [128, 2, B]); gate = sb("gate", [128, 2, B]); es = sb("es", [128, B]); gates = sb("gates", [128, B, 4])
        te_st = sem("te_st"); te_e = sem("te_e")
        tot_ps = pb("tot", [20, 3, 128]); ct_ps = pb("ct", [128, 2, 20])
        idx_in = [sem("idx_in0"), sem("idx_in1")]; g_in = [sem("g_in0"), sem("g_in1")]; done = sem("done"); st_ = sem("st"); ex = sem("ex"); x_ok = sem("x_ok")
        tail_ok = sem("tail_ok"); put = [sem("put0"), sem("put1")]; first = sem("first"); first_in = sem("first_in"); f_ok = sem("f_ok")
        free = [sem("free0"), sem("free1")]; fin2 = sem("fin2"); dmy = sb("dmy", [128, 1])
        const = sem("const"); fin = sem("fin"); tot_ok = sem("tot_ok"); tot_mm = sem("tot_mm"); cexp = sem("cexp"); ct_src = sem("ct_src"); ct_mm = sem("ct_mm"); ct_ok = sem("ct_ok"); own_in = sem("own_in"); join_ok = sem("join_ok"); join_out = sem("join_out")
        q_in = sem("q_in"); lead_ok = sem("lead_ok"); w12_ok = sem("w12_ok"); w12_e = sem("w12_e"); sq_s = sem("sq_s"); sq_e = sem("sq_e"); sc_ok = sem("sc_ok"); p_in = sem("p_in"); out = sem("out")
        seg_v = seg.rearrange("(p c) f -> p (c f)", p=128)
        CHAIN = 12
        block = ctx.enter_context(nc.Block())

        @block.sync
        def _(sp):
            sp.dma_start(post_s[:], post).then_inc(p_in, 16)
            sp.dma_start(lead[:], lead_in).then_inc(p_in, 16)
            sp.dma_start(down[:], iota_in).then_inc(p_in, 16)
            sp.dma_start(fidx[:], srt[0:128 * C].rearrange("(p c) -> p c", p=128)[:, 0:1], allow_slow_non_contiguous=True).then_inc(first, 16)

            def load(i, c):
                s = bass.ds(i * (2 * N) + c * N, N)
                sp.dma_start(idx[:, c, :], src[:, s]).then_inc(idx_in[c], 16)
                sp.dma_start(st[:, c, :], start[:, s]).then_inc(idx_in[c], 16)
            for c in range(2):
                load(0, c)

            def turn(i, more):
                for c in range(2):
                    sp.wait_ge(tail_ok, i * 2 + (c + 3))
                    sp.dma_start(seg_v[:, bass.ds(i * (2 * N * F) + c * N * F, N * F)], r[:, c].rearrange("p n f -> p (n f)")).then_inc(put[c], 16)
                    if more:
                        load(i + 1, c)
            with sp.Fori(0, ANEW) as i:
                turn(i, True)
            sp.wait_ge(c_ok, 1)
            sp.dma_start(comp.rearrange("(p c) -> p c", p=128), place[:]).then_inc(c_out, 16)
            sp.wait_ge(c_out, 16)
            sp.dma_start(place[:].rearrange("p (a k) -> p a k", k=128), comp.rearrange("(a p k) -> p a k", p=128, k=128)).then_inc(c_in, 16)
            with sp.Fori(ANEW, TURNS - 1) as i:
                turn(i, True)
            turn(TURNS - 1, False)
            for c in range(2):
                sp.wait_ge(put[c], TURNS * 16 + 16)
            sp.sem_inc(fin, 1)
            sp.wait_ge(sc_ok, 1)
            sp.dma_start(gates_out, gates[:]).then_inc(out, 16)
            sp.wait_ge(out, 16)

        @block.gpsimd
        def _(pool):
            P = nc.gpsimd
            make_identity(nc, pool, ident, const)
            P.memset(dummy[:], 0.0).then_inc(const, 1)
            P.iota(node[:], pattern=[[128, B]], base=0, channel_multiplier=1).then_inc(const, 1)
            P.iota(rowbase[:], pattern=[[0, 1]], base=0, channel_multiplier=C).then_inc(const, 1)
            pool.wait_ge(const, 5)
            pool.wait_ge(f_ok, 1)
            P.indirect_dma_start(frow[:], None, table, bass.IndirectOffsetOnAxis(ap=fidx[:].bitcast(U32), axis=0)).then_inc(first_in, 16)

            pool.sem_inc(poked, 1)

            def turn(i, more):
                for c in range(2):
                    pool.wait_ge(idx_in[c], i * 32 + 32)
                    pool.wait_ge(free[c], i + 1)
                    pool.wait_ge(poked, i * 2 + (c + 1))
                    P.tensor_tensor(dummy2[:], dummy[:], dummy[:], ALU.add).then_inc(poked, 1)
                    for k in range(N):
                        P.indirect_dma_start(g[:, c, k, :], None, table, bass.IndirectOffsetOnAxis(ap=idx[:, c, k:k + 1], axis=0)).then_inc(g_in[c], 16)
            turns(pool, TURNS, turn)
            pool.wait_ge(fin, 1)
            pool.wait_ge(lead_ok, 1)
            P.indirect_dma_start(own[:], None, seg, bass.IndirectOffsetOnAxis(ap=lead_at[:], axis=0)).then_inc(own_in, 16)
            pool.wait_ge(join_ok, 1)
            P.indirect_dma_start(seg, bass.IndirectOffsetOnAxis(ap=lead_at[:], axis=0), joined[:], None).then_inc(join_out, 16)
            pool.wait_ge(join_out, 16)
            pool.wait_ge(end_ok, 1)
            for b in range(B):
                P.indirect_dma_start(q[:, b, :], None, seg, bass.IndirectOffsetOnAxis(ap=endi[:, b:b + 1].bitcast(U32), axis=0)).then_inc(q_in, 16)

        @block.scalar
        def _(act):
            A = nc.scalar
            act.sem_inc(put[0], 16)
            act.sem_inc(put[1], 16)
            act.sem_inc(tail_ok, 2)

            def turn(i, more):
                for c in range(2):
                    act.wait_ge(ex, i * 2 + (c + 1))
                    A.activation(xe[:], x[:], ACT.Exp).then_inc(x_ok, 1)
                    act.wait_ge(put[c], i * 16 + 16)
                    act.wait_ge(done, i * 2 + (c + 1))
                    A.activation(r[:, c, :, 20:24], mx[:, c, 1:N + 1, :], ACT.Copy).then_inc(tail_ok, 1)
            turns(act, TURNS, turn)
            act.wait_ge(cexp, 1)
            A.activation(ca[:], ca[:], ACT.Exp).then_inc(cexp, 1)
            A.activation(cb[:], cb[:], ACT.Exp).then_inc(cexp, 1)
            act.wait_ge(w12_ok, 1)
            A.activation(w2[:], w2[:], ACT.Exp).then_inc(w12_e, 1)
            act.wait_ge(sq_s, 1)
            A.activation(var[:], var[:], ACT.Sqrt).then_inc(sq_e, 1)
            act.wait_ge(te_st, 1)
            A.activation(es[:], es[:], ACT.Exp).then_inc(te_e, 1)

        @block.tensor
        def _(pe):
            pe.wait_ge(const, 2)
            pe.wait_ge(c_in, 16)
            for c in range(C // 128):
                mm = nc.tensor.transpose(square_ps[:, c // 4, (c % 4) * 128:(c % 4 + 1) * 128], place[:, c * 128:(c + 1) * 128], ident[:])
            mm.then_inc(cT_mm, 1)
            pe.wait_ge(tot_ok, 1)
            for k in range(3):
                mm = nc.tensor.transpose(tot_ps[:, k, :], tot[:, k, :], ident[:])
            mm.then_inc(tot_mm, 1)
            pe.wait_ge(ct_src, 1)
            nc.tensor.transpose(ct_ps[:, 0, :], cs[:, 0:128], ident[0:20, 0:20])
            nc.tensor.transpose(ct_ps[:, 1, :], cm[:, 0:128], ident[0:20, 0:20]).then_inc(ct_mm, 1)

        @block.vector
        def _(dve):
            V = nc.vector
            steps = Steps(fin2, None, None)
            go = lambda ins: steps.chain(dve, ins)
            dve.wait_ge(first, 16)
            V.tensor_scalar(fidx[:], fidx[:], DST_SHIFT, (1 << NODE_BITS) - 1, ALU.logical_shift_right, ALU.bitwise_and).then_inc(f_ok, 1)
            dve.wait_ge(p_in, 48)
            dve.wait_ge(const, 5)
            go(V.tensor_scalar(some[:], lead[:], 1.0, None, ALU.min))
            go(V.tensor_scalar(none[:], some[:], -LOWEST, LOWEST, ALU.mult, ALU.add))
            go(V.tensor_copy(at[:], rowbase[:]))
            go(V.tensor_tensor(at[:], at[:], lead[:], ALU.add))
            go(V.tensor_tensor(at[:], at[:], some[:], ALU.subtract))
            V.tensor_copy(lead_at[:], at[:]).then_inc(lead_ok, 1)
            go(V.memset(mx[:, 1, N, :], LOWEST))
            go(V.memset(r[:, 1, N - 1, 0:20], 0.0))
            dve.wait_ge(first_in, 16)
            go(V.tensor_copy(ad[:, 1, N - 1, :], frow[:, 20:24]))
            dve.sem_inc(free[0], 1)
            dve.sem_inc(free[1], 1)

            def turn(i, more):
                for c in range(2):
                    o = 1 - c
                    s = Steps(st_, 2 * CHAIN, i)
                    s.n = c * CHAIN
                    dve.wait_ge(idx_in[c], i * 32 + 32)
                    s.did(V.tensor_scalar(keep[:], st[:, c, :], -1.0, 1.0, ALU.mult, ALU.add))
                    s.did(V.tensor_scalar(neg[:], st[:, c, :], LOWEST, None, ALU.mult))
                    dve.wait_ge(g_in[c], i * (16 * N) + 16 * N)
                    s.chain(dve, V.tensor_tensor(adm[:], g[:, c, :, 20:24], bc(st[:, c, :], [128, N, 4]), ALU.mult))
                    for h in range(4):
                        ins = V.tensor_tensor_scan(ad[:, c, :, h], keep[:], adm[:, :, h], ad[:, o, N - 1, h:h + 1], ALU.mult, ALU.add)
                    s.chain(dve, ins)
                    s.chain(dve, V.tensor_tensor(e[:], g[:, c, :, 16:20], ad[:, c], ALU.add))
                    s.chain(dve, V.scalar_tensor_tensor(el[:], e[:], 0.2, e[:], ALU.mult, ALU.max))
                    dve.wait_ge(tail_ok, i * 2 + (c + 1))
                    s.chain(dve, V.tensor_copy(mx[:, c, 0, :], mx[:, o, N, :]))
                    for h in range(4):
                        ins = V.tensor_tensor_scan(mx[:, c, 1:N + 1, h], neg[:], el[:, :, h], mx[:, o, N, h:h + 1], ALU.add, ALU.max)
                    s.chain(dve, ins)
                    s.did(V.tensor_tensor(x[:, 1], el[:], mx[:, c, 1:N + 1, :], ALU.subtract))
                    s.chain(dve, V.tensor_tensor(x[:, 0], mx[:, c, 0:N, :], mx[:, c, 1:N + 1, :], ALU.subtract))
                    V.tensor_scalar(x[:, 0], x[:, 0], 0.0, None, ALU.min).then_inc(ex, 1)
                    dve.wait_ge(x_ok, i * 2 + (c + 1))
                    s.did(V.tensor_tensor(xe[:, 0], xe[:, 0], bc(keep[:], [128, N, 4]), ALU.mult))
                    s.chain(dve, V.tensor_tensor(v[:].rearrange("p n (h k) -> p n h k", k=4), g[:, c, :, 0:16].rearrange("p n (h k) -> p n h k", k=4),
                                                 xe[:, 1].rearrange("p n (h o) -> p n h o", o=1).to_broadcast([128, N, 4, 4]), ALU.mult))
                    dve.sem_inc(free[c], 1)
                    dve.wait_ge(put[c], i * 16 + 16)
                    for f in range(20):
                        h = f // 4 if f < 16 else f - 16
                        ins = V.tensor_tensor_scan(r[:, c, :, f], xe[:, 0, :, h], v[:, :, f] if f < 16 else xe[:, 1, :, h],
                                                   r[:, o, N - 1, f:f + 1], ALU.mult, ALU.add)
                    ins.then_inc(done, 1)
                    dve.wait_ge(done, i * 2 + (c + 1))
                    assert s.n == (c + 1) * CHAIN, s.n

            def pull(j):
                shift, n = (1 << j, C + HALO) if j < 7 else (1 << (j - 7), C)
                a = route
                go(V.tensor_scalar(tmp[:, 0:n], a[:, 0:n], 31 - j, 31, ALU.logical_shift_left, ALU.arith_shift_right))
                go(V.tensor_tensor(tmp[:, 0:n], tmp[:, 0:n], a[:, 0:n], ALU.bitwise_and))
                go(V.tensor_tensor(a[:, 0:n], a[:, 0:n], tmp[:, 0:n], ALU.bitwise_xor))
                go(V.tensor_tensor(a[:, 0:n - shift], a[:, 0:n - shift], tmp[:, shift:n], ALU.bitwise_or))
            for step, bits in enumerate(MOVES):
                with dve.Fori(3 * step, 3 * step + 3) as i:
                    turn(i, True)
                if bits[0] == 7:
                    dve.wait_ge(cT_mm, 1)
                    go(V.tensor_copy(route[:, 0:C], square_ps[:].rearrange("p a k -> p (a k)")[:, 0:C]))
                for j in bits:
                    pull(j)
                if bits[-1] == 6:
                    V.tensor_copy(place[:], route[:, 0:C]).then_inc(c_ok, 1)
            go(V.tensor_scalar(endi[:], route[:, 0:B], (1 << LIVE_BIT) - 1, None, ALU.bitwise_and))
            V.tensor_tensor(endi[:], endi[:], node[:], ALU.add).then_inc(end_ok, 1)
            with dve.Fori(3 * len(MOVES), TURNS) as i:
                turn(i, True)
            dve.wait_ge(tail_ok, TURNS * 2 + 2)
            go(V.tensor_copy(tot[:, 0, :], r[:, 1, N - 1, 0:20]))
            go(V.tensor_copy(tot[:, 1, 0:16].rearrange("p (h k) -> p h k", k=4), bc(mx[:, 1, N, :], [128, 4, 4])))
            go(V.tensor_copy(tot[:, 1, 16:20], mx[:, 1, N, :]))
            go(V.tensor_scalar(dmy[:], lead[:], float(C), None, ALU.is_lt))
            V.tensor_copy(tot[:, 2, :], dmy[:].to_broadcast([128, 20])).then_inc(tot_ok, 1)
            dve.wait_ge(tot_mm, 1)
            go(V.tensor_copy(tt[:], tot_ps[:]))
            go(V.memset(cm[:, 0:1], LOWEST))
            go(V.memset(cs[:, 0:1], 0.0))
            go(V.tensor_scalar(cb[:], tt[:, 2, :], LOWEST, None, ALU.mult))
            go(V.tensor_tensor_scan(cm[:, 1:], cb[:], tt[:, 1, :], LOWEST, ALU.add, ALU.max))
            go(V.tensor_tensor(ca[:], cm[:, 0:B], cm[:, 1:], ALU.subtract))
            go(V.tensor_scalar(ca[:], ca[:], 0.0, None, ALU.min))
            V.tensor_tensor(cb[:], tt[:, 1, :], cm[:, 1:], ALU.subtract).then_inc(cexp, 1)
            dve.wait_ge(cexp, 3)
            go(V.tensor_scalar(tt[:, 2, :], tt[:, 2, :], -1.0, 1.0, ALU.mult, ALU.add))
            go(V.tensor_tensor(ca[:], ca[:], tt[:, 2, :], ALU.mult))
            go(V.tensor_tensor(cb[:], cb[:], tt[:, 0, :], ALU.mult))
            V.tensor_tensor_scan(cs[:, 1:], ca[:], cb[:], 0.0, ALU.mult, ALU.add).then_inc(ct_src, 1)
            dve.wait_ge(ct_mm, 1)
            go(V.tensor_copy(ct[:].rearrange("p (a f) -> p a f", a=2), ct_ps[:]))
            go(V.tensor_scalar(ct[:, 0:20], ct[:, 0:20], some[:], None, ALU.mult))
            go(V.tensor_scalar(ct[:, 36:40], ct[:, 36:40], some[:], none[:], ALU.mult, ALU.add))
            dve.wait_ge(own_in, 16)
            go(V.tensor_tensor(joined[:, 20:24], own[:, 20:24], ct[:, 36:40], ALU.max))
            go(V.tensor_tensor(w2[:, 0], own[:, 20:24], joined[:, 20:24], ALU.subtract))
            V.tensor_tensor(w2[:, 1], ct[:, 36:40], joined[:, 20:24], ALU.subtract).then_inc(w12_ok, 1)
            dve.wait_ge(w12_e, 1)
            for t, k in ((own, 0), (ct, 1)):
                go(V.tensor_tensor(t[:, 0:16].rearrange("p (h k) -> p h k", k=4), t[:, 0:16].rearrange("p (h k) -> p h k", k=4), bc(w2[:, k], [128, 4, 4]), ALU.mult))
                go(V.tensor_tensor(t[:, 16:20], t[:, 16:20], w2[:, k], ALU.mult))
            V.tensor_tensor(joined[:, 0:20], own[:, 0:20], ct[:, 0:20], ALU.add).then_inc(join_ok, 1)
            dve.wait_ge(q_in, 16 * B)
            quad = lambda t: t.rearrange("p b (h k) -> p b h k", k=4)
            wide = lambda t: t.rearrange("p b (h o) -> p b h o", o=1).to_broadcast([128, B, 4, 4])
            go(V.tensor_scalar(m2[:], q[:, :, 16:20], 1e-16, None, ALU.add))
            go(V.reciprocal(m2[:], m2[:]))
            a = q[:, :, 0:16]
            go(V.tensor_tensor(quad(a), quad(a), wide(m2[:]), ALU.mult))
            over = lambda k: post_s[:, k:k + 1, :].to_broadcast([128, B, 16])
            go(V.tensor_tensor(a, a, over(0), ALU.add))
            go(V.tensor_reduce(mu[:], a, AX, ALU.add))
            go(V.tensor_scalar(mu[:], mu[:], 1.0 / 16, None, ALU.mult))
            go(V.tensor_tensor(a, a, bc(mu[:], [128, B, 16]), ALU.subtract))
            go(V.tensor_tensor(sq[:], a, a, ALU.mult))
            go(V.tensor_reduce(var[:], sq[:], AX, ALU.add))
            go(V.tensor_scalar(var[:], var[:], 1.0 / 16, LN_EPS, ALU.mult, ALU.add))
            V.reciprocal(var[:], var[:]).then_inc(sq_s, 1)
            dve.wait_ge(sq_e, 1)
            go(V.tensor_tensor(a, a, bc(var[:], [128, B, 16]), ALU.mult))
            go(V.tensor_tensor(a, a, over(1), ALU.mult))
            go(V.tensor_tensor(a, a, over(2), ALU.add))
            go(V.tensor_reduce(sc[:], a.rearrange("p b (h k) -> p b k h", k=4), AX, ALU.add))
            go(V.tensor_scalar(sc[:], sc[:], 0.25, None, ALU.mult))
            places = down[:].rearrange("p (o k) -> p o k", o=1).to_broadcast([128, B, 4])
            for k in range(2):
                hot = one[:, k]
                go(V.tensor_reduce(top[:, k], sc[:], AX, ALU.max))
                go(V.tensor_tensor(hot, sc[:], bc(top[:, k], [128, B, 4]), ALU.is_equal))
                go(V.tensor_tensor(hot, hot, places, ALU.mult))
                go(V.tensor_reduce(mu[:], hot, AX, ALU.max))
                go(V.tensor_tensor(hot, places, bc(mu[:], [128, B, 4]), ALU.is_equal))
                if k == 0:
                    go(V.scalar_tensor_tensor(sc[:], hot, LOWEST, sc[:], ALU.mult, ALU.add))
            V.tensor_tensor(es[:], top[:, 1], top[:, 0], ALU.subtract).then_inc(te_st, 1)
            dve.wait_ge(te_e, 1)
            go(V.tensor_scalar(gate[:, 0], es[:], 1.0, None, ALU.add))
            go(V.reciprocal(gate[:, 0], gate[:, 0]))
            go(V.tensor_tensor(gate[:, 1], gate[:, 0], es[:], ALU.mult))
            for k in range(2):
                go(V.tensor_tensor(one[:, k], one[:, k], bc(gate[:, k], [128, B, 4]), ALU.mult))
            V.tensor_tensor(gates[:], one[:, 0], one[:, 1], ALU.add).then_inc(sc_ok, 1)


def experts4(nc, h_in, sT_in, gates_in, w1, b1, w2, b2, h_out):
    B, T, _ = h_in.shape
    G, E = 4, 4
    TURNS = B // (2 * G)
    with ExitStack() as ctx:
        sb = lambda n, s, d=F32: ctx.enter_context(nc.sbuf_tensor("mgs_" + n, s, d))
        pb = lambda n, s, d=F32: ctx.enter_context(nc.psum_tensor("mgp_" + n, s, d))
        sem = ctx.enter_context(semaphores(nc, "mgm_"))
        w1_s = sb("w1", [128, E * 128]); b1_s = sb("b1", [128, E]); w2_s = sb("w2", [128, E * D + D]); b2_s = sb("b2", [128, E, D])
        sT = sb("sT", [128, 2, 512]); res = sb("res", [128, 2, G, D]); acc = sb("acc", [128, 2, G, D]); part = sb("part", [128, 2, G, D])
        gates = sb("gates", [128, 2, G, 4]); hid = sb("hid", [128, 2, 512])
        hid_ps = pb("hid", [128, 2, 512]); y_ps = pb("y", [128, 4, G, 2 * D])
        w_in = sem("w_in"); pad = sem("pad"); in_ = [sem("in0"), sem("in1")]; s_in = [sem("s_in0"), sem("s_in1")]; hid_mm = sem("hid_mm"); hid_ok = sem("hid_ok")
        y_mm = sem("y_mm"); gated = sem("gated"); sum_ok = sem("sum_ok"); put = [sem("put0"), sem("put1")]
        hi = h_in.rearrange("b t n -> t b n"); ho = h_out.rearrange("b t n -> t b n")
        loads = [(w1_s[:], w1), (b1_s[:], b1), (w2_s[:, 0:E * D], w2), (b2_s[:], b2)]
        P = 2 * E
        block = ctx.enter_context(nc.Block())

        @block.sync
        def _(sp):
            for dst, src in loads:
                sp.dma_start(dst, src).then_inc(w_in, 16)

            def load_s(i, c):
                sp.dma_start(sT[:, c, :], sT_in[:, bass.ds(i * 1024 + c * 512, 512)]).then_inc(s_in[c], 16)

            def load(i, c):
                b = bass.ds(i * 2 * G + c * G, G)
                sp.dma_start(res[:, c], hi[:, b, :]).then_inc(in_[c], 16)
                sp.dma_start(gates[:, c], gates_in[:, b, :]).then_inc(in_[c], 16)
            for c in range(2):
                load_s(0, c)
                load(0, c)

            def turn(i, more):
                for c in range(2):
                    if more:
                        sp.wait_ge(hid_mm, i * P + (c * E + E))
                        load_s(i + 1, c)
                    sp.wait_ge(sum_ok, i * P + (P + c * E + E))
                    sp.dma_start(ho[:, bass.ds(i * 2 * G + c * G, G), :], acc[:, c]).then_inc(put[c], 16)
                    if more:
                        load(i + 1, c)
            turns(sp, TURNS, turn)
            for c in range(2):
                sp.wait_ge(put[c], TURNS * 16 + 16)

        @block.gpsimd
        def _(pool):
            def turn(i, more):
                for n in range(P):
                    c, e = n // E, n % E
                    pool.wait_ge(gated, i * P + (n + 1))
                    pool.wait_ge(sum_ok, i * P + (P + n))
                    if e == 0:
                        pool.wait_ge(put[c], i * 16 + 16)
                    nc.gpsimd.tensor_tensor(acc[:, c], part[:, n % 2], acc[:, c] if e else res[:, c], ALU.add).then_inc(sum_ok, 1)
            turns(pool, TURNS, turn)

        @block.vector
        def _(dve):
            V = nc.vector
            V.memset(w2_s[:, E * D:], 0.0).then_inc(pad, 1)
            dve.wait_ge(w_in, 16 * len(loads))
            dve.sem_inc(sum_ok, P)

            def turn(i, more):
                for n in range(P):
                    c, e = n // E, n % E
                    if e == 0:
                        dve.wait_ge(in_[c], i * 32 + 32)
                    dve.wait_ge(y_mm, i * P + (n + 1))
                    dve.wait_ge(sum_ok, i * P + (P + n - 1))
                    V.tensor_tensor(part[:, n % 2], y_ps[:, e, :, 0:D], b2_s[:, e:e + 1, :].to_broadcast([128, G, D]), ALU.add).then_inc(pad, 1)
                    dve.wait_ge(pad, i * P + (n + 2))
                    V.tensor_tensor(part[:, n % 2], part[:, n % 2], gates[:, c, :, e:e + 1].to_broadcast([128, G, D]), ALU.mult).then_inc(gated, 1)
            turns(dve, TURNS, turn)

        @block.scalar
        def _(act):
            A = nc.scalar
            for c in range(2):
                act.sem_inc(put[c], 16)
            act.wait_ge(w_in, 16 * len(loads))

            def turn(i, more):
                for n in range(P):
                    c, e = n // E, n % E
                    act.wait_ge(hid_mm, i * P + (n + 1))
                    if n >= 2:
                        act.wait_ge(y_mm, i * P + (n - 1))
                    A.activation(hid[:, n % 2, :], hid_ps[:, n % 2, :], ACT.Gelu, bias=b1_s[:, e:e + 1]).then_inc(hid_ok, 1)
            turns(act, TURNS, turn)

        @block.tensor
        def _(pe):
            M = nc.tensor.matmul
            pe.wait_ge(w_in, 16 * len(loads))
            pe.wait_ge(pad, 1)

            def hidden(i, n):
                c, e = n // E, n % E
                if e == 0:
                    pe.wait_ge(s_in[c], i * 16 + 16)
                M(hid_ps[:, n % 2, :], w1_s[:, e * 128:(e + 1) * 128], sT[:, c, :], start=True, stop=True).then_inc(hid_mm, 1)

            def output(i, n):
                pe.wait_ge(hid_ok, i * P + (n + 1))
                pe.wait_ge(sum_ok, i * P + (P + n + 1 - E))
                for b in range(G):
                    mm = M(y_ps[:, n % E, b, :], hid[:, n % 2, b * 128:(b + 1) * 128], w2_s[:, (n % E) * D:(n % E + 2) * D], start=True, stop=True)
                mm.then_inc(y_mm, 1)
            hidden(0, 0)
            hidden(0, 1)

            def turn(i, more):
                for n in range(P):
                    output(i, n)
                    if n + 2 < P:
                        hidden(i, n + 2)
                    elif more:
                        hidden(i + 1, n + 2 - P)
            turns(pe, TURNS, turn)


def lay_gat(inp):
    g = lambda n: np.asarray(inp["L1_ffn_" + n])
    z = lambda a: np.concatenate([a, np.zeros_like(a)])
    att = np.stack([g("att_src").reshape(16), g("att_dst").reshape(16)])
    return dict(ga_wg=z(g("W_gat")), ga_att=np.broadcast_to(att, (128, 2, 16)),
                ga_post=np.broadcast_to(np.stack([g("b_gat"), g("ln_gamma"), g("ln_beta")]), (128, 3, 16)),
                ga_w1=z(np.transpose(g("W1"), (1, 0, 2)).reshape(64, 512)), ga_b1=g("b1").T,
                ga_w2=np.transpose(g("W2"), (1, 0, 2)).reshape(128, 256), ga_b2=np.broadcast_to(g("b2"), (128, 4, 64)),
                ga_down=np.broadcast_to(np.arange(4, 0, -1, dtype=np.float32), (128, 4)), ga_edges=g("edge_index"))


def tower(nc, a, out):
    B, N = 128, 128 * 128
    keys = a["ga_edges"].shape[1] + N
    C = keys // 128
    scratch = lambda name, shape, d=F32: nc.dram_tensor(name, shape, d, kind="Internal").ap()
    h = [scratch("h%d_scratch" % k, (B, 128, D)) for k in range(4)]
    srt = scratch("sorted_scratch", (keys + 129,), I32)
    comp = scratch("compact_scratch", (keys,))
    src = scratch("source_scratch", (128, C), U32)
    start = scratch("start_scratch", (128, C))
    lead = scratch("lead_scratch", (128, 1))
    table = scratch("table_scratch", (N, ROW))
    sT = scratch("sT_scratch", (128, N))
    seg = scratch("segment_scratch", (keys, 24))
    gates = scratch("gates_scratch", (128, B, 4))
    with nc.sbuf_tensor("route", [128, C + HALO], I32) as route:
        with ExitStack() as ctx:
            sorter = KeySort(nc, a["ga_edges"], lambda n, s, d=F32: ctx.enter_context(nc.sbuf_tensor("sort_" + n, s, d)),
                             ctx.enter_context(semaphores(nc, "sort_")))
            tokenizer(nc, sorter, a["x"], *[a["tk_" + n] for n in ("wc1", "p1row", "p1col", "wc2", "p2row", "p2col", "wq", "wk", "bqk", "wv", "pv", "wc3", "p3col")], h[0])
            sort_edges(nc, sorter, a["ga_edges"], srt, src, start, lead, route)
        linear_attention(nc, h[0], a["la_wq"], a["la_we"], h[1])
        experts16(nc, h[1], *[a["mo_" + n] for n in ("wg", "gb", "w1", "b1", "w2", "b2", "post")], h[2])
        rope_attention(nc, h[2], *[a["ra_" + n] for n in ("wq", "wk", "wv", "wo", "norms", "csh", "cst")], h[3])
        node_table(nc, h[3], a["ga_wg"], a["ga_att"], table, sT)
        edge_softmax(nc, table, src, start, lead, route, comp, srt, seg, a["ga_post"], a["ga_down"], gates)
    experts4(nc, h[3], sT, gates, a["ga_w1"], a["ga_b1"], a["ga_w2"], a["ga_b2"], out)


def kernel(**inputs):
    import numpy as _np
    import concourse.bacc as _bacc
    from concourse import mybir as _mybir
    from concourse.bass_utils import run_bass_kernel_spmd as _run

    laid = dict(x=inputs["x"])
    for lay in (lay_tokenizer, lay_linear_attention, lay_experts16, lay_rope_attention, lay_gat):
        laid.update(lay(inputs))
    nc = _bacc.Bacc("TRN2", target_bir_lowering=False, num_devices=1)
    arrays, args = {}, {}
    for name, value in laid.items():
        value = _np.ascontiguousarray(value)
        arrays[name + "_dram"] = value
        args[name] = nc.dram_tensor(name + "_dram", value.shape, _mybir.dt.from_np(value.dtype), kind="ExternalInput").ap()
    out = nc.dram_tensor("out_0_dram", (128, 128, D), _mybir.dt.float32, kind="ExternalOutput").ap()
    tower(nc, args, out)
    r = _run(nc, [arrays], core_ids=[0])
    return r.results[0]["out_0_dram"]
```
